# Optimizing a Trainium2 kernel written in Bass

```python
import numpy as np
import jax
import jax.numpy as jnp

def _softmax(x, axis=-1):
    return jax.nn.softmax(x, axis=axis)

def _gelu(x):
    return jax.nn.gelu(x, approximate=True)

def _silu(x):
    return jax.nn.silu(x)

def _sigmoid(x):
    return jax.nn.sigmoid(x)

def _layernorm(x, axis=-1, eps=1e-05):
    m = jnp.mean(x, axis=axis, keepdims=True)
    v = jnp.var(x, axis=axis, keepdims=True)
    return (x - m) / jnp.sqrt(v + eps)

def _scatter_add(tgt, idx, src, axis=0):
    return tgt.at[idx].add(src)

def _segment_sum(src, seg, n):
    return jax.ops.segment_sum(src, seg, n)
kernel_name = 'mk_gps_d1_gnn_r8_29e312'

def setup_inputs(seed: int=0):
    np.random.seed(seed)
    _w = jnp.asarray

    def _rec_inputs():
        import jax
        import jax.numpy as jnp
        _gk = jax.random.key(seed)
        x = -0.0002117 + 1 * jax.random.normal(jax.random.fold_in(_gk, 1), (6250, 256), jnp.float32)
        _s = jax.random.randint(jax.random.fold_in(_gk, 2), (50000,), 0, 6250, jnp.int32)
        _d = jax.random.randint(jax.random.fold_in(_gk, 3), (50000,), 0, 6250, jnp.int32)
        _loop = jnp.arange(6250, dtype=jnp.int32)
        src = jnp.concatenate([_s, _d, _loop])
        dst = jnp.concatenate([_d, _s, _loop])
        _o = jnp.argsort(dst, stable=True)
        src = src[_o]
        dst = dst[_o]
        return (x, src, dst)
    x, src, dst = _rec_inputs()

    def _L0_gnn_setup():
        import jax, jax.numpy as jnp
        import numpy as np
        N = 12500
        E = 100000
        D_IN = 256
        D_H = 512

        def _gcn_prep(edge_index, n_nodes):
            loop = jnp.arange(n_nodes, dtype=edge_index.dtype)
            row = jnp.concatenate([edge_index[0], loop])
            col = jnp.concatenate([edge_index[1], loop])
            deg = jax.ops.segment_sum(jnp.ones_like(row, dtype=jnp.float32), row, num_segments=n_nodes)
            dinv = jax.lax.rsqrt(deg)
            norm = dinv[row] * dinv[col]
            return (row, col, norm)

        def _gcn_conv(x, W, b, row, col, norm, n_nodes):
            h = x @ W
            msg = h[col] * norm[:, None]
            out = jax.ops.segment_sum(msg, row, num_segments=n_nodes)
            return out + b
        key = jax.random.key(seed)
        ks = jax.random.split(key, 8)
        s_in = 1.0 / np.sqrt(D_IN)
        s_h = 1.0 / np.sqrt(D_H)
        return {'x': jax.random.normal(ks[0], (N, D_IN), jnp.float32), 'edge_index': jax.random.randint(ks[1], (2, E), 0, N, dtype=jnp.int64), 'W1': jax.random.normal(ks[2], (D_IN, D_H), jnp.float32) * s_in, 'b1': jnp.zeros((D_H,), jnp.float32), 'W2': jax.random.normal(ks[3], (D_H, D_H), jnp.float32) * s_h, 'b2': jnp.zeros((D_H,), jnp.float32), 'W3': jax.random.normal(ks[4], (D_H, D_H), jnp.float32) * s_h, 'b3': jnp.zeros((D_H,), jnp.float32), 'Wfc': jax.random.normal(ks[5], (D_H, D_IN), jnp.float32) * s_h, 'bfc': jnp.zeros((D_IN,), jnp.float32)}
    _L0_gnn_all = _L0_gnn_setup()
    _L0_gnn_in = {k: v for k, v in _L0_gnn_all.items() if k in ('W1', 'b1', 'W2', 'b2', 'W3', 'b3', 'Wfc', 'bfc')}
    del _L0_gnn_all

    def _L0_mix_setup():
        import jax, jax.numpy as jnp
        import numpy as np
        HEADS = 4
        DIM_HEAD = 32
        key = jax.random.key(seed)
        k1, k2, k3 = jax.random.split(key, 3)
        B, L, D = (16, 1024, 256)
        hidden = HEADS * DIM_HEAD
        x = jax.random.normal(k1, (B, L, D), dtype=jnp.float32)
        W_qkv = jax.random.normal(k2, (D, 3 * hidden), dtype=jnp.float32) * D ** (-0.5)
        W_out = jax.random.normal(k3, (hidden, D), dtype=jnp.float32) * hidden ** (-0.5)
        b_out = jnp.zeros((D,), dtype=jnp.float32)
        return {'x': x, 'W_qkv': W_qkv, 'W_out': W_out, 'b_out': b_out}
    _L0_mix_all = _L0_mix_setup()
    _L0_mix_in = {k: v for k, v in _L0_mix_all.items() if k in ('W_qkv', 'W_out', 'b_out')}
    del _L0_mix_all

    def _L0_ffn_setup():
        import jax, jax.numpy as jnp
        import numpy as np
        E = 8
        K = 2
        D = 256
        H = 512
        DOUT = 256
        EPS = 1e-05
        key = jax.random.key(seed)
        ks = jax.random.split(key, 9)
        s = 0.02
        return {'x': jax.random.normal(ks[0], (4, 1024, D), jnp.float32), 'gamma': 1.0 + 0.05 * jax.random.normal(ks[1], (D,), jnp.float32), 'beta': 0.05 * jax.random.normal(ks[2], (D,), jnp.float32), 'Wr': 0.01 * jax.random.normal(ks[3], (D, E), jnp.float32), 'br': jnp.zeros((E,), jnp.float32), 'W1': s * jax.random.normal(ks[4], (E, D, H), jnp.float32), 'b1': s * jax.random.normal(ks[5], (E, H), jnp.float32), 'W2': s * jax.random.normal(ks[6], (E, H, DOUT), jnp.float32), 'b2': s * jax.random.normal(ks[7], (E, DOUT), jnp.float32)}
    _L0_ffn_all = _L0_ffn_setup()
    _L0_ffn_in = {k: v for k, v in _L0_ffn_all.items() if k in ('gamma', 'beta', 'Wr', 'br', 'W1', 'b1', 'W2', 'b2')}
    del _L0_ffn_all
    return {'x': x, 'src': src, 'dst': dst, 'L0_gnn_W1': _L0_gnn_in['W1'], 'L0_gnn_b1': _L0_gnn_in['b1'], 'L0_gnn_W2': _L0_gnn_in['W2'], 'L0_gnn_b2': _L0_gnn_in['b2'], 'L0_gnn_W3': _L0_gnn_in['W3'], 'L0_gnn_b3': _L0_gnn_in['b3'], 'L0_gnn_Wfc': _L0_gnn_in['Wfc'], 'L0_gnn_bfc': _L0_gnn_in['bfc'], 'L0_mix_W_qkv': _L0_mix_in['W_qkv'], 'L0_mix_W_out': _L0_mix_in['W_out'], 'L0_mix_b_out': _L0_mix_in['b_out'], 'L0_ffn_gamma': _L0_ffn_in['gamma'], 'L0_ffn_beta': _L0_ffn_in['beta'], 'L0_ffn_Wr': _L0_ffn_in['Wr'], 'L0_ffn_br': _L0_ffn_in['br'], 'L0_ffn_W1': _L0_ffn_in['W1'], 'L0_ffn_b1': _L0_ffn_in['b1'], 'L0_ffn_W2': _L0_ffn_in['W2'], 'L0_ffn_b2': _L0_ffn_in['b2']}

def reference(x, src, dst, L0_gnn_W1, L0_gnn_b1, L0_gnn_W2, L0_gnn_b2, L0_gnn_W3, L0_gnn_b3, L0_gnn_Wfc, L0_gnn_bfc, L0_mix_W_qkv, L0_mix_W_out, L0_mix_b_out, L0_ffn_gamma, L0_ffn_beta, L0_ffn_Wr, L0_ffn_br, L0_ffn_W1, L0_ffn_b1, L0_ffn_W2, L0_ffn_b2):
    import jax
    import jax.numpy as jnp

    def _L0_gnn_ref(x, edge_index, W1, b1, W2, b2, W3, b3, Wfc, bfc):
        import jax, jax.numpy as jnp
        import numpy as np
        N = 12500
        E = 100000
        D_IN = 256
        D_H = 512

        def _gcn_prep(edge_index, n_nodes):
            loop = jnp.arange(n_nodes, dtype=edge_index.dtype)
            row = jnp.concatenate([edge_index[0], loop])
            col = jnp.concatenate([edge_index[1], loop])
            deg = jax.ops.segment_sum(jnp.ones_like(row, dtype=jnp.float32), row, num_segments=n_nodes)
            dinv = jax.lax.rsqrt(deg)
            norm = dinv[row] * dinv[col]
            return (row, col, norm)

        def _gcn_conv(x, W, b, row, col, norm, n_nodes):
            h = x @ W
            msg = h[col] * norm[:, None]
            out = jax.ops.segment_sum(msg, row, num_segments=n_nodes)
            return out + b
        n = x.shape[0]
        row, col, norm = _gcn_prep(edge_index, n)
        h = jax.nn.relu(_gcn_conv(x, W1, b1, row, col, norm, n))
        h = jax.nn.relu(_gcn_conv(h, W2, b2, row, col, norm, n))
        h = jax.nn.relu(_gcn_conv(h, W3, b3, row, col, norm, n))
        return h @ Wfc + bfc

    def _L0_mix_ref(x, W_qkv, W_out, b_out):
        import jax, jax.numpy as jnp
        import numpy as np
        HEADS = 4
        DIM_HEAD = 32
        B, L, D = x.shape
        scale = DIM_HEAD ** (-0.5)
        qkv = jnp.einsum('bld,df->blf', x, W_qkv)
        qkv = qkv.reshape(B, L, 3, HEADS, DIM_HEAD)
        q = jnp.transpose(qkv[:, :, 0], (0, 2, 1, 3)) * scale
        k = jax.nn.softmax(jnp.transpose(qkv[:, :, 1], (0, 2, 1, 3)), axis=2)
        v = jnp.transpose(qkv[:, :, 2], (0, 2, 1, 3))
        context = jnp.einsum('bhld,bhle->bhde', k, v)
        out = jnp.einsum('bhde,bhld->bhle', context, q)
        out = jnp.transpose(out, (0, 2, 1, 3)).reshape(B, L, HEADS * DIM_HEAD)
        return jnp.einsum('blf,fd->bld', out, W_out) + b_out

    def _L0_ffn_ref(x, gamma, beta, Wr, br, W1, b1, W2, b2):
        import jax, jax.numpy as jnp
        import numpy as np
        E = 8
        K = 2
        D = 256
        H = 512
        DOUT = 256
        EPS = 1e-05
        mu = jnp.mean(x, axis=-1, keepdims=True)
        var = jnp.mean(jnp.square(x - mu), axis=-1, keepdims=True)
        xn = (x - mu) * jax.lax.rsqrt(var + EPS) * gamma + beta
        logits = jnp.einsum('bsd,de->bse', xn, Wr) + br
        top_vals, top_idx = jax.lax.top_k(logits, K)
        w = jax.nn.softmax(top_vals, axis=-1)
        w_full = jnp.einsum('bsk,bske->bse', w, jax.nn.one_hot(top_idx, E, dtype=w.dtype))
        y = jnp.zeros(x.shape[:-1] + (DOUT,), x.dtype)
        for e in range(E):
            h = jax.nn.gelu(jnp.einsum('bsd,dh->bsh', xn, W1[e]) + b1[e], approximate=False)
            y_e = jnp.einsum('bsh,hd->bsd', h, W2[e]) + b2[e]
            y = y + y_e * w_full[..., e, None]
        return y
    edge_index = jnp.stack([src, dst])
    xn = _layernorm(x, axis=-1)
    x = x + _L0_gnn_ref(xn, edge_index, L0_gnn_W1, L0_gnn_b1, L0_gnn_W2, L0_gnn_b2, L0_gnn_W3, L0_gnn_b3, L0_gnn_Wfc, L0_gnn_bfc) + _L0_mix_ref(xn[None], L0_mix_W_qkv, L0_mix_W_out, L0_mix_b_out)[0]
    x = x + _L0_ffn_ref(_layernorm(x, axis=-1)[None], L0_ffn_gamma, L0_ffn_beta, L0_ffn_Wr, L0_ffn_br, L0_ffn_W1, L0_ffn_b1, L0_ffn_W2, L0_ffn_b2)[0]
    return x

_drawn_inputs = setup_inputs


def setup_inputs(seed=0):
    import zlib

    import numpy as np

    out = dict(_drawn_inputs(seed))
    spreads = {'L0_gnn_b1': (0.0, 0.372),
     'L0_gnn_b2': (0.0, 0.1),
     'L0_gnn_b3': (0.0, 0.1),
     'L0_gnn_bfc': (0.0, 0.1),
     'L0_mix_b_out': (0.0, 0.1),
     'L0_ffn_br': (0.0, 0.1)}
    factors = {'L0_gnn_W1': 4.777,
     'L0_ffn_gamma': 6.756,
     'L0_ffn_beta': 5.127,
     'L0_ffn_b1': 8.0,
     'L0_ffn_b2': 4.354}
    for name, (base, spread) in spreads.items():
        noise = np.random.default_rng([zlib.crc32(name.encode()), seed]).standard_normal(out[name].shape)
        drawn = base * np.exp(spread * noise) if base else spread * noise
        out[name] = jnp.asarray(drawn.astype(out[name].dtype))
    for name, factor in factors.items():
        out[name] = (out[name] * factor).astype(out[name].dtype)
    return out
```

```python
from contextlib import ExitStack

import concourse.bass as bass
from concourse import mybir

ALU = mybir.AluOpType
ACT = mybir.ActivationFunctionType
AX = mybir.AxisListType
F32 = mybir.dt.float32
F16 = mybir.dt.float16
I32 = mybir.dt.int32
U32 = mybir.dt.uint32
U16 = mybir.dt.uint16

P = 128
NODES, D, H = 6250, 256, 512
TILES = -(-NODES // P)
LAST = NODES - (TILES - 1) * P
KD, KH = D // P, H // P
HID, DH = 128, 32
EXPERTS = 8
EDGES = 106250
EP = 125
EC = EDGES // EP
GRP = 2
UNROLL = 8
GROUPS = -(-((EDGES + TILES * (GRP * P - 1)) // (GRP * P)) // UNROLL) * UNROLL
SLOTS = GROUPS * GRP
HALF = SLOTS // 2
STEPS = GROUPS // UNROLL
RING = UNROLL * GRP
QUAD = 4
QUADS = TILES // QUAD
EPS = 1e-5
SHIFT = 7
assert EP * EC == EDGES and 1 << SHIFT == P and QUADS * QUAD + 1 == TILES and TILES % 2 == 1


class Core:
    pass


def over_tiles(eng, body):
    body(0, 0)
    body(1, 1)
    with eng.Fori(1, TILES // 2) as i:
        body(2 * i, 0)
        body(2 * i + 1, 1)
    body(TILES - 1, 0)


def reuse(eng, sem, t, lag=2):
    if not isinstance(t, int) or t >= lag:
        eng.wait_ge(sem, t - (lag - 1))


def allocate(nc, ctx, k):
    def sb(name, shape, dt=F32):
        return ctx.enter_context(nc.sbuf_tensor("sb_" + name, shape, dt))

    def sem(name):
        return ctx.enter_context(nc.semaphore(name))

    k.nc, k.sem = nc, sem
    k.bank = [ctx.enter_context(nc.psum_tensor(f"bank{i}", [P, 512], F32)) for i in range(8)]
    k.acc = sb("acc", [P, TILES, H])
    k.work = sb("work", [P, 11264])
    k.wts = sb("wts", [P, 6144])
    k.Wqkv = sb("Wqkv", [P, KD, 3, HID])
    k.Wout = sb("Wout", [P, D])
    k.bias = [sb(f"bias{i}", [P, H]) for i in range(3)]
    k.rb, k.bfc = sb("rb", [P, D]), sb("bfc", [P, D])
    k.gamma, k.beta = sb("gamma", [P, D]), sb("beta", [P, D])
    k.Wr, k.br = sb("Wr", [P, KD, EXPERTS]), sb("br", [P, EXPERTS])
    k.eb1, k.eb2 = sb("eb1", [P, EXPERTS, KH]), sb("eb2", [EXPERTS, D])
    k.iota16 = sb("iota16", [P, SLOTS], F16)
    k.iota = sb("iota", [P, P])
    k.ident, k.ones = sb("ident", [P, P]), sb("ones", [P, P])
    k.lower = sb("lower", [P, P])
    k.slot_dst = sb("slot_dst", [P, SLOTS], U32)
    k.slot_row = sb("slot_row", [P, SLOTS])
    k.table = sb("table", [1, GROUPS], I32)
    k.index = sb("index", [P, RING], U32)
    k.dinv, k.mean, k.rstd = sb("dinv", [P, TILES]), sb("mean", [P, TILES]), sb("rstd", [P, TILES])
    k.stats = sb("stats", [P, TILES, 6])
    k.small = sb("small", [P, 5, TILES])
    k.eps = sb("eps", [P, 1])
    k.W1 = k.wts[:, 0:KD * H].rearrange("p (k n) -> p k n", k=KD)
    k.Wfc = k.wts[:, 1024:1024 + KH * D].rearrange("p (k n) -> p k n", k=KH)
    k.W2 = k.wts[:, 2048:4096].rearrange("p (k n) -> p k n", k=KH)
    k.W3 = k.wts[:, 4096:6144].rearrange("p (k n) -> p k n", k=KH)
    k.keys = k.work[:, 0:TILES * P]
    k.edge = [k.wts[0:EP, i * EC:(i + 1) * EC] for i in range(7)]
    k.edge += [k.work[0:EP, TILES * P + i * EC:TILES * P + (i + 1) * EC] for i in range(5)]
    k.feats = [nc.dram_tensor(f"feats{i}", (TILES * P, w), F32, kind="Internal").ap()
               for i, w in enumerate((D, H, H))]
    k.resid = nc.dram_tensor("resid", (TILES * P, D), F32, kind="Internal").ap()
    k.s_const = sem("constants_ready")
    k.s_tick = sem("tick")


def load(k, a):
    nc, sem = k.nc, k.sem
    s_zeroed, s_x, s_w, s_e, s_pad = sem("zeroed"), sem("x_loaded"), sem("w_loaded"), sem("e_loaded"), sem("pad_zeroed")
    with nc.Block() as block:
        @block.sync
        def _(sp):
            sp.dma_start(k.edge[7].bitcast(I32), a["src"].rearrange("(p c) -> p c", c=EC)).then_inc(s_e, 16)
            sp.dma_start(k.edge[8].bitcast(I32), a["dst"].rearrange("(p c) -> p c", c=EC)).then_inc(s_e, 16)
            sp.dma_start(k.acc[:, 0:TILES - 1, 0:D],
                         a["x"][0:(TILES - 1) * P, :].rearrange("(t p) d -> p t d", p=P)).then_inc(s_x, 16)
            sp.wait_ge(s_pad, 1)
            sp.dma_start(k.acc[0:LAST, TILES - 1, 0:D], a["x"][(TILES - 1) * P:NODES, :]).then_inc(s_x, 16)
            sp.wait_ge(s_x, 32)
            sp.wait_ge(s_e, 32)

        @block.scalar
        def _(act):
            def get(to, of):
                act.dma_start(to, of).then_inc(s_w, 16)
            get(k.Wqkv[:, :, :, :], a["L0_mix_W_qkv"].rearrange("(k p) (c n) -> p k c n", p=P, c=3))
            get(k.Wout[:, :], a["L0_mix_W_out"])
            rows = [(k.bias[0], "L0_gnn_b1"), (k.bias[1], "L0_gnn_b2"), (k.bias[2], "L0_gnn_b3"),
                    (k.rb, "L0_mix_b_out"), (k.bfc, "L0_gnn_bfc"), (k.gamma, "L0_ffn_gamma"),
                    (k.beta, "L0_ffn_beta"), (k.br, "L0_ffn_br")]
            for to, name in rows:
                n = a[name].shape[0]
                get(to[:, :], a[name].rearrange("(a n) -> a n", a=1).to_broadcast([P, n]))
            get(k.Wr[:, :, :], a["L0_ffn_Wr"].rearrange("(k p) n -> p k n", p=P))
            get(k.eb2[:, :], a["L0_ffn_b2"])
            with nc.allow_non_contiguous_dma(reason="a small bias, its features on partitions"):
                for e in range(EXPERTS):
                    get(k.eb1[:, e, :], a["L0_ffn_b1"][e].rearrange("(k p) -> p k", p=P))
            act.wait_ge(s_w, 16 * (4 + len(rows) + EXPERTS))

        @block.gpsimd
        def _(pool):
            pool.memset(k.ident[:, :], 0.0).then_inc(s_zeroed, 1)
            pool.memset(k.lower[:, :], 1.0).then_inc(s_zeroed, 1)
            pool.memset(k.ones[:, :], 1.0)
            pool.memset(k.eps[:, :], EPS)
            for row in (k.iota16, k.iota):
                pool.iota(row[:, :], pattern=[[1, row.shape[1]]], base=0, channel_multiplier=0,
                          allow_small_or_imprecise_dtypes=True)
            pool.wait_ge(s_zeroed, 2)
            pool.affine_select(out=k.ident[:, :], in_=k.ident[:, :], compare_op=ALU.not_equal, fill=1.0, base=0,
                               pattern=[[-1, P]], channel_multiplier=1)
            pool.affine_select(out=k.lower[:, :], in_=k.lower[:, :], compare_op=ALU.is_gt, fill=0.0, base=0,
                               pattern=[[1, P]], channel_multiplier=-1).then_inc(k.s_const, 1)

        @block.vector
        def _(dve):
            dve.memset(k.acc[:, TILES - 1, 0:D], 0.0).then_inc(s_pad, 1)


def norm(k, name, lo, to):
    nc, sem = k.nc, k.sem
    s_stats, s_var, s_sqrt, s_done = (sem(f"{name}_{x}") for x in ("stats", "var", "sqrt", "done"))
    sm = k.small
    with nc.Block() as block:
        @block.vector
        def _(dve):
            with dve.Fori(0, TILES) as t:
                dve.bn_stats(k.stats[:, bass.ds(t, 1), :], k.acc[:, bass.ds(t, 1), lo:lo + D]).then_inc(s_stats, 1)
            dve.wait_ge(s_stats, TILES)
            m0, m1, q0, q1 = (k.stats[:, :, i] for i in (1, 4, 2, 5))
            dve.tensor_tensor(sm[:, 0, :], m0, m1, ALU.add).then_inc(s_var, 1)
            dve.tensor_tensor(sm[:, 1, :], m0, m1, ALU.subtract).then_inc(s_var, 1)
            dve.tensor_tensor(sm[:, 2, :], q0, q1, ALU.add).then_inc(s_var, 1)
            dve.wait_ge(s_var, 3)
            dve.tensor_scalar(k.mean[:, :], sm[:, 0, :], 0.5, None, ALU.mult).then_inc(s_var, 1)
            dve.scalar_tensor_tensor(out=sm[:, 3, :], in0=sm[:, 1, :], scalar=D / 4.0, in1=sm[:, 1, :],
                                     op0=ALU.mult, op1=ALU.mult).then_inc(s_var, 1)
            dve.wait_ge(s_var, 5)
            dve.tensor_tensor(sm[:, 4, :], sm[:, 3, :], sm[:, 2, :], ALU.add).then_inc(s_var, 1)
            dve.wait_ge(s_sqrt, 1)
            dve.reciprocal(k.rstd[:, :], k.rstd[:, :]).then_inc(s_var, 1)
            dve.wait_ge(s_var, 7)
            with dve.Fori(0, TILES) as t:
                dve.tensor_scalar(k.acc[:, bass.ds(t, 1), to:to + D], k.acc[:, bass.ds(t, 1), lo:lo + D],
                                  k.mean[:, bass.ds(t, 1)], k.rstd[:, bass.ds(t, 1)],
                                  ALU.subtract, ALU.mult).then_inc(s_done, 1)
            dve.wait_ge(s_done, TILES)

        @block.scalar
        def _(act):
            act.wait_ge(s_var, 6)
            act.activation(k.rstd[:, :], sm[:, 4, :], ACT.Sqrt, bias=k.eps[:, 0:1], scale=1.0 / D).then_inc(s_sqrt, 1)


def attention(k, a):
    nc, sem, work = k.nc, k.sem, k.work
    st = [k.wts[:, i * D:(i + 1) * D] for i in range(2)]
    xT = [k.wts[:, (2 + i) * D:(3 + i) * D].rearrange("p (k n) -> p k n", k=KD) for i in range(2)]
    expk = [k.wts[:, 1024 + i * P:1024 + (i + 1) * P] for i in range(2)]
    ctx_m, ctx_T = k.wts[:, 1280:1408], k.wts[:, 1408:1536]
    mix = k.wts[:, 1536:1792]
    xr = [k.wts[:, 1792 + i * D:1792 + (i + 1) * D] for i in range(2)]
    ro = [k.wts[:, 2304 + i * D:2304 + (i + 1) * D] for i in range(2)]
    kmax, ksum, krec = k.wts[:, 2816:2817], k.wts[:, 2817:2818], k.wts[:, 2818:2819]
    scratch = [sem(f"att_{x}") for x in (
        "staged", "turned", "turned_kept", "projected", "keys_kept", "qv_kept", "max", "exp", "pad")]
    s_st, s_tr, s_xT, s_qkv, s_k, s_qv, s_max, s_exp, s_pad = scratch
    e_st, e_tr, e_kept, s_ctx, s_fin = (sem(f"ctx_{x}") for x in ("staged", "turned", "kept", "summed", "finished"))
    o_st, o_mm, o_done = (sem(f"mix_{x}") for x in ("staged", "product", "added"))
    o_x = [sem(f"mix_x_loaded{i}") for i in range(2)]
    s_rb = sem("rb_ready")
    o_added2 = sem("mix_finished")
    o_outs = [sem(f"mix_stored{i}") for i in range(2)]

    with nc.Block() as block:
        @block.scalar
        def _(act):
            def stage_x(t, s):
                reuse(act, s_tr, t)
                act.sem_inc(k.s_tick, 1)
                act.activation(st[s], k.acc[:, bass.ds(t, 1), 0:D], ACT.Copy).then_inc(s_st, 1)

            def project(t, s):
                if not isinstance(t, int) or t < TILES - 1:
                    stage_x(t + 1, 1 - s)
                act.wait_ge(s_qkv, t + 1)
                act.sem_inc(k.s_tick, 1)
                act.activation(k.keys[:, bass.ds(t * P, P)], k.bank[6 + s][:, 0:P], ACT.Copy).then_inc(s_k, 1)
            stage_x(0, 0)
            over_tiles(act, project)
            act.wait_ge(s_k, TILES)
            act.wait_ge(s_max, 1)
            act.activation(k.keys[:, 0:NODES], k.keys[:, 0:NODES], ACT.Exp, bias=kmax, accum_out=ksum).then_inc(s_exp, 1)
            act.wait_ge(s_exp, 1)
            act.wait_ge(s_pad, 1)

            def stage_keys(t, s):
                reuse(act, e_tr, t)
                act.sem_inc(k.s_tick, 1)
                act.activation(st[s][:, 0:P], k.keys[:, bass.ds(t * P, P)], ACT.Copy).then_inc(e_st, 1)
            over_tiles(act, stage_keys)
            act.wait_ge(e_tr, TILES)

            def stage_queries(t, s):
                reuse(act, o_mm, t)
                act.sem_inc(k.s_tick, 1)
                act.activation(st[s][:, 0:P], k.acc[:, bass.ds(t, 1), D:D + P], ACT.Copy).then_inc(o_st, 1)
            over_tiles(act, stage_queries)

        @block.tensor
        def _(pe):
            def turn(t, s):
                pe.wait_ge(s_st, t + 1)
                reuse(pe, s_xT, t)
                for c in range(KD):
                    mm = pe.transpose(k.bank[s][:, c * P:(c + 1) * P], st[s][:, c * P:(c + 1) * P], k.ident[:, :])
                mm.then_inc(s_tr, 1)

            def project(t, s):
                if not isinstance(t, int) or t < TILES - 1:
                    turn(t + 1, 1 - s)
                pe.wait_ge(s_xT, t + 1)
                reuse(pe, s_k, t)
                reuse(pe, s_qv, t)
                for c in range(KD):
                    pe.matmul(k.bank[2 + s][:, 0:P], k.Wqkv[:, c, 0, :], xT[s][:, c, :], start=c == 0, stop=c == KD - 1)
                for c in range(KD):
                    pe.matmul(k.bank[2 + s][:, P:2 * P], xT[s][:, c, :], k.Wqkv[:, c, 2, :],
                              start=c == 0, stop=c == KD - 1)
                for c in range(KD):
                    mm = pe.matmul(k.bank[6 + s][:, 0:P], k.Wqkv[:, c, 1, :], xT[s][:, c, :],
                                   start=c == 0, stop=c == KD - 1)
                mm.then_inc(s_qkv, 1)
            turn(0, 0)
            over_tiles(pe, project)

            def turn_keys(t, s):
                pe.wait_ge(e_st, t + 1)
                reuse(pe, e_kept, t)
                pe.transpose(k.bank[s][:, 0:P], st[s][:, 0:P], k.ident[:, :]).then_inc(e_tr, 1)

            def context(t, s):
                if not isinstance(t, int) or t < TILES - 1:
                    turn_keys(t + 1, 1 - s)
                pe.wait_ge(e_kept, t + 1)
                pe.sem_inc(k.s_tick, 1)
                first, last = isinstance(t, int) and t == 0, isinstance(t, int) and t == TILES - 1
                pe.matmul(k.bank[4][:, 0:P], expk[s], k.acc[:, bass.ds(t, 1), D + P:D + 2 * P],
                          start=first, stop=last).then_inc(s_ctx, 1)
            turn_keys(0, 0)
            over_tiles(pe, context)
            pe.wait_ge(s_fin, 4)
            pe.transpose(k.bank[5][:, 0:P], ctx_m, k.ident[:, :]).then_inc(s_ctx, 1)
            pe.wait_ge(s_fin, 5)
            pe.matmul(k.bank[6][:, 0:D], ctx_T, k.Wout[:, :], start=True, stop=True).then_inc(s_ctx, 1)
            pe.wait_ge(s_fin, 6)

            def apply(t, s):
                pe.wait_ge(o_st, t + 1)
                reuse(pe, o_done, t)
                pe.matmul(k.bank[s][:, 0:D], st[s][:, 0:P], mix, start=True, stop=True).then_inc(o_mm, 1)
            over_tiles(pe, apply)

        @block.vector
        def _(dve):
            dve.tensor_tensor(k.rb[:, :], k.rb[:, :], k.bfc[:, :], ALU.add).then_inc(s_rb, 1)

            def keep(t, s):
                dve.wait_ge(s_tr, t + 1)
                reuse(dve, s_qkv, t)
                dve.sem_inc(k.s_tick, 1)
                dve.tensor_copy(xT[s], k.bank[s][:, 0:D].rearrange("p (k n) -> p k n", k=KD)).then_inc(s_xT, 1)
                dve.wait_ge(s_qkv, t + 1)
                dve.sem_inc(k.s_tick, 1)
                dve.tensor_copy(k.acc[:, bass.ds(t, 1), D:2 * D],
                                k.bank[2 + s][:, 0:D].rearrange("p (a n) -> p a n", a=1)).then_inc(s_qv, 1)
            over_tiles(dve, keep)
            dve.wait_ge(s_k, TILES)
            dve.memset(k.keys[:, NODES:TILES * P], 0.0).then_inc(s_pad, 1)
            dve.tensor_reduce(krec, k.keys[:, 0:NODES], AX.X, ALU.max).then_inc(s_rb, 1)
            dve.wait_ge(s_rb, 2)
            dve.tensor_scalar(kmax, krec, -1.0, None, ALU.mult).then_inc(s_max, 1)

            def keep_keys(t, s):
                dve.wait_ge(e_tr, t + 1)
                reuse(dve, s_ctx, t)
                dve.sem_inc(k.s_tick, 1)
                dve.tensor_copy(expk[s], k.bank[s][:, 0:P]).then_inc(e_kept, 1)
            over_tiles(dve, keep_keys)
            dve.wait_ge(s_exp, 1)
            dve.wait_ge(s_max, 1)
            dve.memset(ctx_m, 0.0).then_inc(s_rb, 1)
            dve.reciprocal(krec, ksum).then_inc(s_rb, 1)
            dve.wait_ge(s_rb, 4)
            dve.wait_ge(s_ctx, TILES)
            for h in range(HID // DH):
                b = slice(h * DH, (h + 1) * DH)
                dve.tensor_scalar(ctx_m[b, b], k.bank[4][b, b], krec[b, :], float(DH) ** -0.5,
                                  ALU.mult, ALU.mult).then_inc(s_fin, 1)
            dve.wait_ge(s_ctx, TILES + 1)
            dve.tensor_copy(ctx_T, k.bank[5][:, 0:P]).then_inc(s_fin, 1)
            dve.wait_ge(s_ctx, TILES + 2)
            dve.tensor_copy(mix, k.bank[6][:, 0:D]).then_inc(s_fin, 1)

            def add(t, s):
                dve.wait_ge(o_x[s], 16 * (t // 2 + 1) if isinstance(t, int) else 8 * (t - s) + 16)
                reuse(dve, o_added2, t)
                dve.wait_ge(o_mm, t + 1)
                dve.tensor_tensor(xr[s], xr[s], k.bank[s][:, 0:D], ALU.add).then_inc(o_done, 1)
                dve.wait_ge(o_done, t + 1)
                if not isinstance(t, int) or t >= 2:
                    dve.wait_ge(o_outs[s], 16 * (t // 2) if isinstance(t, int) else 8 * (t - s))
                dve.tensor_tensor(ro[s], xr[s], k.rb[:, :], ALU.add).then_inc(o_added2, 1)
            over_tiles(dve, add)

        @block.sync
        def _(sp):
            def fetch(t, s):
                reuse(sp, o_added2, t)
                n = LAST if isinstance(t, int) and t == TILES - 1 else P
                sp.dma_start(xr[s][0:n, :], a["x"][bass.ds(t * P, n), :]).then_inc(o_x[s], 16)

            over_tiles(sp, fetch)

        @block.gpsimd
        def _(pool):
            def store(t, s):
                pool.wait_ge(o_added2, t + 1)
                pool.sem_inc(k.s_tick, 1)
                pool.dma_start(k.resid[bass.ds(t * P, P), :], ro[s]).then_inc(o_outs[s], 16)
            over_tiles(pool, store)
            pool.wait_ge(o_outs[0], 16 * (TILES // 2 + 1))
            pool.wait_ge(o_outs[1], 16 * (TILES // 2))


def place_edges(k):
    nc, sem = k.nc, k.sem
    hi, lo, v1, v2, pos, part, chunk = k.edge[0:7]
    src, dst, tmp = (k.edge[i].bitcast(I32) for i in (7, 8, 9))
    mask = [k.edge[8][:, i * (EC // 2):(i + 1) * (EC // 2)].bitcast(U16) for i in range(2)]
    zeros = k.edge[7][:, 0:EC // 2].bitcast(U16)
    count = [k.edge[10], k.edge[11]]
    tab = k.keys
    per = tab[0:EP, 0:TILES]
    need, groups, ends, start = (tab[:, 64 * i:64 * i + TILES] for i in range(1, 5))
    needi = tab[:, 320:320 + TILES].bitcast(I32)
    col, coli, colg, cole = (tab[0:TILES, 384 + i:385 + i] for i in range(4))
    behind = tab[0:TILES, 512:512 + GROUPS]
    zrow = tab[:, 1024:1024 + TILES]
    tabf = tab[0:1, 1088:1088 + GROUPS]
    s_key, s_per, s_tot, s_tab, s_cmp, s_look = (sem(f"edges_{x}") for x in (
        "keyed", "counted", "totals", "tabled", "ends", "looked_up"))
    s_mask, s_count, s_pos, s_prep = (sem(f"rank_{x}") for x in ("masked", "counted", "placed", "prepared"))
    n = [0]

    with nc.Block() as block:
        @block.vector
        def _(dve):
            def link(ins):
                n[0] += 1
                ins.then_inc(s_key, 1)
                dve.wait_ge(s_key, n[0])
            link(dve.tensor_scalar(tmp, src, SHIFT, None, ALU.logical_shift_right))
            link(dve.tensor_copy(hi, tmp))
            link(dve.tensor_scalar(tmp, src, P - 1, None, ALU.bitwise_and))
            link(dve.tensor_copy(lo, tmp))
            link(dve.tensor_scalar(tmp, dst, 2, None, ALU.logical_shift_right))
            link(dve.tensor_copy(v1, tmp))
            link(dve.tensor_scalar(tmp, dst, 3, None, ALU.bitwise_and))
            link(dve.tensor_copy(pos, tmp))
            link(dve.tensor_scalar(v2, pos, 256.0, 1.0, ALU.mult, ALU.add))
            link(dve.tensor_tensor(v2, v2, lo, ALU.add))
            link(dve.memset(zeros, 0))
            link(dve.memset(zrow, 0.0))
            with dve.Fori(0, TILES) as b:
                dve.tensor_scalar(tmp.bitcast(F32), hi, k.iota[0:EP, bass.ds(b, 1)], None, ALU.is_equal, ALU.add,
                                  accum_out=per[:, bass.ds(b, 1)]).then_inc(s_per, 1)
                dve.wait_ge(s_per, b + 1)
            dve.wait_ge(s_tot, 1)
            link(dve.tensor_scalar(needi, k.bank[0][:, 64:64 + TILES], GRP * P - 1.0, None, ALU.add))
            link(dve.tensor_scalar(needi, needi, SHIFT + GRP.bit_length() - 1, None, ALU.logical_shift_right))
            link(dve.tensor_copy(groups, needi))
            link(dve.tensor_tensor_scan(ends, groups, zrow, 0.0, ALU.add, ALU.add))
            link(dve.tensor_tensor(start, ends, groups, ALU.subtract))
            link(dve.tensor_scalar(start, start, float(GRP * P), -1.0, ALU.mult, ALU.add))
            link(dve.tensor_tensor(start[0:EP, :], start[0:EP, :], k.bank[0][0:EP, 0:TILES], ALU.add))
            link(dve.tensor_scalar(coli.bitcast(I32), k.bank[0][0:TILES, 128:129], GRP * P - 1.0, None, ALU.add))
            link(dve.tensor_scalar(coli.bitcast(I32), coli.bitcast(I32), SHIFT + GRP.bit_length() - 1, None,
                                   ALU.logical_shift_right))
            link(dve.tensor_copy(colg, coli.bitcast(I32)))
            dve.drain().then_inc(s_tab, 1)
            dve.wait_ge(s_cmp, 1)
            link(dve.tensor_tensor(cole, colg, k.bank[1][0:TILES, 0:1], ALU.add))
            link(dve.tensor_scalar(behind, k.iota16[0:TILES, 0:GROUPS], cole, None, ALU.is_ge))
            dve.drain().then_inc(s_tab, 1)
            dve.wait_ge(s_look, 1)
            link(dve.tensor_scalar(tabf, k.bank[2][0:1, 0:GROUPS], TILES - 1.0, None, ALU.min))
            link(dve.tensor_copy(k.table[:, :], tabf))
            def rank(b, s):
                reuse(dve, s_pos, b)
                dve.tensor_scalar(mask[s], hi, k.iota[0:EP, bass.ds(b, 1)], None, ALU.is_equal).then_inc(s_mask, 1)
                dve.wait_ge(s_mask, b + 1)
                dve.tensor_tensor_scan(count[s], mask[s], zeros, start[0:EP, bass.ds(b, 1)],
                                       ALU.add, ALU.add).then_inc(s_count, 1)
                dve.wait_ge(s_count, b + 1)
                dve.sem_inc(k.s_tick, 1)
                dve.copy_predicated(pos, mask[s], count[s]).then_inc(s_pos, 1)
            over_tiles(dve, rank)
            dve.wait_ge(s_pos, TILES)
            link(dve.tensor_copy(tmp, pos))
            link(dve.tensor_scalar(count[0].bitcast(I32), tmp, P - 1, None, ALU.bitwise_and))
            link(dve.tensor_copy(part, count[0].bitcast(I32)))
            link(dve.tensor_scalar(count[0].bitcast(I32), tmp, SHIFT, None, ALU.logical_shift_right))
            link(dve.tensor_copy(chunk, count[0].bitcast(I32)))

        @block.tensor
        def _(pe):
            pe.wait_ge(s_per, TILES)
            pe.matmul(k.bank[0][:, 0:TILES], k.lower[0:EP, :], per, start=True, stop=True)
            pe.matmul(k.bank[0][:, 64:64 + TILES], k.ones[0:EP, :], per, start=True, stop=True)
            pe.matmul(k.bank[0][0:TILES, 128:129], per, k.ones[0:EP, 0:1], start=True, stop=True).then_inc(s_tot, 1)
            pe.wait_ge(s_tab, 1)
            pe.matmul(k.bank[1][0:TILES, 0:1], k.lower[0:TILES, 0:TILES], colg, start=True, stop=True).then_inc(s_cmp, 1)
            pe.wait_ge(s_tab, 2)
            pe.matmul(k.bank[2][0:1, 0:GROUPS], k.ones[0:TILES, 0:1], behind, start=True, stop=True).then_inc(s_look, 1)

    DEPTH = 2
    tabs = k.keys.bitcast(F16)
    stat = [tabs[0:EP, s * 384:(s + 1) * 384].rearrange("p (a n) -> p a n", a=3) for s in range(DEPTH)]
    move = [tabs[0:EP, 1024 * (s + 1):1024 * (s + 2)] for s in range(DEPTH)]
    s_hot, s_mm, s_fin, s_deg = (sem(f"place_{x}") for x in ("one_hot", "product", "finish", "degree"))
    with nc.Block() as block:
        def over_columns(eng, body):
            body(0, 0, True, False)
            body(1, 1, False, False)
            with eng.Fori(1, EC // 2 - 1) as i:
                body(2 * i, 0, False, False)
                body(2 * i + 1, 1, False, False)
            body(EC - 2, 0, False, False)
            body(EC - 1, 1, False, True)

        @block.vector
        def _(dve):
            def hot(c, s, first, last):
                reuse(dve, s_mm, c)
                row = k.iota16[0:EP, 0:P]
                dve.tensor_scalar(stat[s][:, 0, :], row, part[:, bass.ds(c, 1)], v1[:, bass.ds(c, 1)],
                                  ALU.is_equal, ALU.mult)
                dve.tensor_scalar(stat[s][:, 1, :], row, part[:, bass.ds(c, 1)], v2[:, bass.ds(c, 1)],
                                  ALU.is_equal, ALU.mult)
                dve.tensor_scalar(stat[s][:, 2, :], row, lo[:, bass.ds(c, 1)], None, ALU.is_equal)
                dve.tensor_scalar(move[s][:, SLOTS:SLOTS + TILES], row[:, 0:TILES], hi[:, bass.ds(c, 1)], None,
                                  ALU.is_equal)
                dve.tensor_scalar(move[s][:, 0:SLOTS], k.iota16[0:EP, :], chunk[:, bass.ds(c, 1)], None,
                                  ALU.is_equal).then_inc(s_hot, 1)
            over_columns(dve, hot)
            dve.wait_ge(s_mm, EC)
            m = [0]

            def link(ins):
                m[0] += 1
                ins.then_inc(s_fin, 1)
                dve.wait_ge(s_fin, m[0])
            w = k.wts
            f1, f2, i1, i2 = (w[:, i * SLOTS:(i + 1) * SLOTS] for i in range(4))
            for h in range(2):
                sl = slice(h * HALF, (h + 1) * HALF)
                link(dve.tensor_scalar(f1[:, sl], k.bank[h][:, 0:HALF], 4.0, None, ALU.mult))
                link(dve.tensor_copy(i2.bitcast(I32)[:, sl], k.bank[2 + h][:, 0:HALF]))
            link(dve.tensor_scalar(i1.bitcast(I32), i2.bitcast(I32), 8, None, ALU.logical_shift_right))
            link(dve.tensor_copy(f2, i1.bitcast(I32)))
            link(dve.tensor_tensor(f1, f1, f2, ALU.add))
            link(dve.tensor_copy(k.slot_dst[:, :], f1))
            link(dve.tensor_scalar(i1.bitcast(I32), i2.bitcast(I32), 255, None, ALU.bitwise_and))
            link(dve.tensor_copy(f2, i1.bitcast(I32)))
            link(dve.tensor_scalar(k.slot_row[:, :], f2, -1.0, None, ALU.add))
            dve.tensor_scalar(k.small[:, 0, :], k.bank[4][:, 0:TILES], 1.0, None, ALU.add).then_inc(s_deg, 1)
            dve.wait_ge(s_deg, 2)
            link(dve.reciprocal(k.dinv[:, :], k.small[:, 1, :]))

        @block.scalar
        def _(act):
            act.wait_ge(s_deg, 1)
            act.activation(k.small[:, 1, :], k.small[:, 0, :], ACT.Sqrt).then_inc(s_deg, 1)

        @block.tensor
        def _(pe):
            def products(c, s, first, last):
                pe.wait_ge(s_hot, c + 1)
                for v in range(2):
                    for h in range(2):
                        pe.matmul(k.bank[2 * v + h][:, 0:HALF], stat[s][:, v, :], move[s][:, h * HALF:(h + 1) * HALF],
                                  start=first, stop=last)
                pe.matmul(k.bank[4][:, 0:TILES], stat[s][:, 2, :], move[s][:, SLOTS:SLOTS + TILES],
                          start=first, stop=last).then_inc(s_mm, 1)
            over_columns(pe, products)


def scale_input(k, a):
    nc, sem = k.nc, k.sem
    s_scaled, s_written, s_loaded = sem("scaled"), sem("scaled_written"), sem("gnn_weights_loaded")
    with nc.Block() as block:
        @block.vector
        def _(dve):
            with dve.Fori(0, TILES) as t:
                dve.tensor_scalar(k.acc[:, bass.ds(t, 1), 0:D], k.acc[:, bass.ds(t, 1), 0:D],
                                  k.dinv[:, bass.ds(t, 1)], None, ALU.mult).then_inc(s_scaled, 1)

        @block.sync
        def _(sp):
            for to, name in ((k.W1, "L0_gnn_W1"), (k.Wfc, "L0_gnn_Wfc"), (k.W2, "L0_gnn_W2"), (k.W3, "L0_gnn_W3")):
                sp.dma_start(to, a[name].rearrange("(k p) n -> p k n", p=P)).then_inc(s_loaded, 16)
            sp.wait_ge(s_scaled, TILES)
            sp.dma_start(k.feats[0].rearrange("(t p) d -> p t d", p=P), k.acc[:, :, 0:D]).then_inc(s_written, 16)
            sp.wait_ge(s_written, 16)
            sp.wait_ge(s_loaded, 64)


def aggregate(k, layer, width):
    nc, sem = k.nc, k.sem
    feats = k.feats[layer]
    ring = k.work[:, 0:RING * H].rearrange("p (s n) -> p s n", s=RING)
    hot = k.work[:, RING * H:RING * (H + P)].rearrange("p (s n) -> p s n", s=RING)
    if layer == 0:
        k.agg = [sem(f"agg_{x}") for x in ("index", "one_hot", "summed", "added")]
        k.agg_got = [sem(f"agg_got{s}") for s in range(RING)]
    s_index, s_hot, s_sum, s_add = k.agg
    s_got = k.agg_got
    G0, I0 = layer * GROUPS, layer * STEPS
    BANKS = 4
    LEAD = 3
    half = RING // 2

    def over_steps(eng, body):
        body(0)
        with eng.Fori(1, STEPS) as i:
            body(i)

    with nc.Block() as block:
        @block.gpsimd
        def _(pool):
            def step(i):
                start = isinstance(i, int)
                for h in range(2):
                    for j in range(half // GRP):
                        if not start:
                            pool.wait_ge(s_sum, G0 + (i - 1) * UNROLL + h * (UNROLL // 2) + j + 1)
                    pool.sem_inc(k.s_tick, 1)
                    pool.tensor_copy(k.index[:, h * half:(h + 1) * half],
                                     k.slot_dst[:, bass.ds(i * RING + h * half, half)]).then_inc(s_index, 1)
                    pool.wait_ge(s_index, 2 * I0 + 2 * i + h + 1)
                    pool.sem_inc(k.s_tick, 1)
                    for s in range(h * half, (h + 1) * half):
                        pool.indirect_dma_start(
                            out=ring[:, s, 0:width], out_offset=None, in_=feats[:, :],
                            in_offset=bass.IndirectOffsetOnAxis(ap=k.index[:, s:s + 1], axis=0),
                            bounds_check=TILES * P - 1, oob_is_err=False).then_inc(s_got[s], 16)
            over_steps(pool, step)

        @block.vector
        def _(dve):
            def one_hot(g, j, free):
                if free:
                    dve.wait_ge(s_sum, G0 + g - UNROLL + 1)
                for c in range(GRP):
                    s = j * GRP + c
                    ins = dve.tensor_scalar(hot[:, s, :], k.iota[:, :], k.slot_row[:, bass.ds(g * GRP + c, 1)], None,
                                            ALU.is_equal)
                ins.then_inc(s_hot, 1)

            def add(g, j):
                t = dve.value_load(k.table[0:1, bass.ds(g, 1)], min_val=0, max_val=TILES - 1)
                if not isinstance(g, int) or g > 0:
                    dve.wait_ge(s_add, G0 + g)
                dve.wait_ge(s_sum, G0 + g + 1)
                dve.tensor_tensor(k.acc[:, bass.ds(t, 1), 0:width], k.acc[:, bass.ds(t, 1), 0:width],
                                  k.bank[j % BANKS][:, 0:width].rearrange("p (a n) -> p a n", a=1),
                                  ALU.add).then_inc(s_add, 1)

            for g in range(LEAD):
                one_hot(g, g, False)

            def step(i, last=False):
                for j in range(UNROLL):
                    g = i * UNROLL + j
                    if not (last and j + LEAD >= UNROLL):
                        free = not isinstance(i, int) or g + LEAD >= UNROLL
                        one_hot(g + LEAD, (j + LEAD) % UNROLL, free)
                    add(g, j)
            step(0)
            with dve.Fori(1, STEPS - 1) as i:
                step(i)
            step(STEPS - 1, last=True)

        @block.tensor
        def _(pe):
            def step(i):
                for j in range(UNROLL):
                    g = i * UNROLL + j
                    pe.wait_ge(s_hot, G0 + g + 1)
                    if not isinstance(i, int) or g >= BANKS:
                        pe.wait_ge(s_add, G0 + g - BANKS + 1)
                    for c in range(GRP):
                        s = j * GRP + c
                        pe.wait_ge(s_got[s], 16 * (I0 + i + 1))
                        mm = pe.matmul(k.bank[j % BANKS][:, 0:width], hot[:, s, :], ring[:, s, 0:width],
                                       start=c == 0, stop=c == GRP - 1)
                    mm.then_inc(s_sum, 1)
            over_steps(pe, step)


def update(k, layer):
    nc, sem, work = k.nc, k.sem, k.work
    names = ("scaled", "turned1", "kept1", "lifted", "biased", "active", "turned", "kept", "product", "done", "extra")
    s_v, s_t1, s_k1, s_m1, s_z, s_r, s_t, s_k, s_m, s_done, s_extra = (sem(f"upd{layer}_{x}") for x in names)
    s_res = [sem(f"upd{layer}_resid{i}") for i in range(2)]
    v = [work[:, i * D:(i + 1) * D] for i in range(2)]
    vT = [work[:, 512 + i * D:512 + (i + 1) * D] for i in range(2)]
    z = [work[:, 1024 + i * H:1024 + (i + 1) * H] for i in range(2)]
    zT = [work[:, 2048 + i * H:2048 + (i + 1) * H] for i in range(2)]
    res = [work[:, 3072 + i * D:3072 + (i + 1) * D] for i in range(2)]
    W = (k.W2, k.W3, k.Wfc)[layer]
    width = (H, H, D)[layer]
    A, B, C, E = k.bank[0:2], k.bank[2:4], k.bank[4:6], k.bank[6:8]

    def more(t):
        return not isinstance(t, int) or t < TILES - 1

    with nc.Block() as block:
        @block.vector
        def _(dve):
            def head(t, s):
                if layer == 0:
                    reuse(dve, s_t1, t)
                    dve.tensor_scalar(v[s], k.acc[:, bass.ds(t, 1), 0:D].rearrange("p a n -> p (a n)"),
                                      k.dinv[:, bass.ds(t, 1)], None, ALU.mult).then_inc(s_v, 1)

            def bias(t, s):
                reuse(dve, s_t, t)
                if layer == 0:
                    dve.wait_ge(s_m1, t + 1)
                    dve.tensor_tensor(z[s], B[s][:, :], k.bias[0][:, :], ALU.add).then_inc(s_z, 1)
                else:
                    dve.scalar_tensor_tensor(out=z[s], in0=k.acc[:, bass.ds(t, 1), :].rearrange("p a n -> p (a n)"),
                                             scalar=k.dinv[:, bass.ds(t, 1)], in1=k.bias[layer][:, :],
                                             op0=ALU.mult, op1=ALU.add).then_inc(s_z, 1)

            def tail(t, s):
                dve.wait_ge(s_m, t + 1)
                one = k.acc[:, bass.ds(t, 1), 0:width].rearrange("p a n -> p (a n)")
                if layer < 2:
                    dve.tensor_scalar(one, E[s][:, :], k.dinv[:, bass.ds(t, 1)], None, ALU.mult).then_inc(s_done, 1)
                else:
                    dve.wait_ge(s_res[s], 16 * (t // 2 + 1) if isinstance(t, int) else 8 * (t - s) + 16)
                    dve.wait_ge(s_m, t + 1)
                    dve.tensor_tensor(one, E[s][:, 0:D], res[s], ALU.add).then_inc(s_done, 1)

            head(0, 0)
            if layer:
                bias(0, 0)

            def step(t, s):
                if more(t):
                    head(t + 1, 1 - s)
                if layer == 0:
                    bias(t, s)
                elif more(t):
                    bias(t + 1, 1 - s)
                tail(t, s)
            over_tiles(dve, step)
            dve.wait_ge(s_done, TILES)

        @block.scalar
        def _(act):
            def step(t, s):
                if layer == 0:
                    reuse(act, s_m1, t)
                    act.wait_ge(s_t1, t + 1)
                    act.activation(vT[s], A[s][:, 0:D], ACT.Copy).then_inc(s_k1, 1)
                act.wait_ge(s_z, t + 1)
                act.activation(z[s], z[s], ACT.Relu).then_inc(s_r, 1)
                reuse(act, s_m, t)
                act.wait_ge(s_t, t + 1)
                act.activation(zT[s], C[s][:, :], ACT.Copy).then_inc(s_k, 1)
            over_tiles(act, step)

        @block.tensor
        def _(pe):
            def turn1(t, s):
                pe.wait_ge(s_v, t + 1)
                reuse(pe, s_k1, t)
                for c in range(KD):
                    mm = pe.transpose(A[s][:, c * P:(c + 1) * P], v[s][:, c * P:(c + 1) * P], k.ident[:, :])
                mm.then_inc(s_t1, 1)

            def lift(t, s):
                pe.wait_ge(s_k1, t + 1)
                reuse(pe, s_z, t)
                for c in range(KD):
                    mm = pe.matmul(B[s][:, :], vT[s][:, c * P:(c + 1) * P], k.W1[:, c, :], start=c == 0, stop=c == KD - 1)
                mm.then_inc(s_m1, 1)

            def turn(t, s):
                pe.wait_ge(s_r, t + 1)
                reuse(pe, s_k, t)
                for c in range(KH):
                    mm = pe.transpose(C[s][:, c * P:(c + 1) * P], z[s][:, c * P:(c + 1) * P], k.ident[:, :])
                mm.then_inc(s_t, 1)

            def product(t, s):
                pe.wait_ge(s_k, t + 1)
                reuse(pe, s_done, t)
                for c in range(KH):
                    mm = pe.matmul(E[s][:, 0:width], zT[s][:, c * P:(c + 1) * P], W[:, c, :],
                                   start=c == 0, stop=c == KH - 1)
                mm.then_inc(s_m, 1)

            if layer == 0:
                turn1(0, 0)
                lift(0, 0)
            else:
                turn(0, 0)

            def step(t, s):
                if layer == 0:
                    if more(t):
                        turn1(t + 1, 1 - s)
                    turn(t, s)
                    if more(t):
                        lift(t + 1, 1 - s)
                elif more(t):
                    turn(t + 1, 1 - s)
                product(t, s)
            over_tiles(pe, step)

        @block.sync
        def _(sp):
            if layer < 2:
                def store(t, s):
                    sp.wait_ge(s_done, t + 1)
                    sp.dma_start(k.feats[layer + 1][bass.ds(t * P, P), :],
                                 k.acc[:, bass.ds(t, 1), :].rearrange("p a n -> p (a n)")).then_inc(s_extra, 16)
                over_tiles(sp, store)
                sp.wait_ge(s_extra, 16 * TILES)
            else:
                def fetch(t, s):
                    reuse(sp, s_done, t)
                    sp.dma_start(res[s], k.resid[bass.ds(t * P, P), :]).then_inc(s_res[s], 16)
                over_tiles(sp, fetch)
                sp.wait_ge(s_res[0], 16 * (TILES // 2 + 1))
                sp.wait_ge(s_res[1], 16 * (TILES // 2))


def route(k):
    nc, sem, work = k.nc, k.sem, k.work
    y = [work[:, i * D:(i + 1) * D] for i in range(2)]
    yT = [work[:, 512 + i * D:512 + (i + 1) * D] for i in range(2)]
    wT = [work[0:EXPERTS, 1024 + i * P:1024 + (i + 1) * P] for i in range(2)]
    logits = k.gates = k.wts[:, 0:TILES * EXPERTS].rearrange("p (t e) -> p t e", e=EXPERTS)
    best = k.wts[:, 512:512 + TILES * 8].rearrange("p (t e) -> p t e", e=8)
    which = k.wts[:, 1024:1024 + TILES * 8].bitcast(U32).rearrange("p (t e) -> p t e", e=8)
    whichf = k.wts[:, 1536:1536 + TILES * 8].rearrange("p (t e) -> p t e", e=8)
    one, two = (k.wts[:, 2048 + i * 512:2048 + i * 512 + TILES * EXPERTS].rearrange("p (t e) -> p t e", e=EXPERTS)
                for i in range(2))
    w1, w2, dif = (k.small[:, i, :] for i in range(3))
    names = ("g", "b", "turned", "kept", "copied", "logits", "biased", "best", "chain", "exp", "wturned", "wkept", "b2", "added")
    s_g, s_b, s_t, s_k, s_c, s_l, s_lb, s_best, s_ch, s_exp, s_wt, s_wk, s_b2, s_add = (sem(f"gate_{x}") for x in names)
    with nc.Block() as block:
        @block.vector
        def _(dve):
            def affine(t, s):
                reuse(dve, s_t, t)
                dve.tensor_tensor(y[s], k.acc[:, bass.ds(t, 1), D:2 * D].rearrange("p a n -> p (a n)"), k.gamma[:, :],
                                  ALU.mult).then_inc(s_g, 1)
                dve.wait_ge(s_g, t + 1)
                dve.tensor_tensor(y[s], y[s], k.beta[:, :], ALU.add).then_inc(s_b, 1)
                dve.wait_ge(s_l, t + 1)
                dve.tensor_tensor(logits[:, bass.ds(t, 1), :].rearrange("p a e -> p (a e)"), k.bank[2 + s][:, 0:EXPERTS],
                                  k.br[:, :], ALU.add).then_inc(s_lb, 1)
            over_tiles(dve, affine)
            dve.wait_ge(s_lb, TILES)
            for t in range(TILES):
                dve.max(best[:, t, :], logits[:, t, :]).then_inc(s_best, 1)
            dve.wait_ge(s_best, TILES)
            for t in range(TILES):
                dve.max_index(which[:, t, :], best[:, t, :], logits[:, t, :]).then_inc(s_best, 1)
            n = [0]

            def link(ins):
                n[0] += 1
                ins.then_inc(s_ch, 1)
                dve.wait_ge(s_ch, n[0])
            link(dve.tensor_tensor(dif, best[:, :, 1], best[:, :, 0], ALU.subtract))
            dve.wait_ge(s_exp, 1)
            link(dve.tensor_scalar(w2, dif, 1.0, None, ALU.add))
            link(dve.reciprocal(w1, w2))
            link(dve.tensor_tensor(w2, dif, w1, ALU.mult))
            dve.wait_ge(s_best, 2 * TILES)
            link(dve.tensor_copy(whichf, which))

            def wide(x):
                return x.rearrange("p (t a) -> p t a", a=1).to_broadcast([P, TILES, EXPERTS])
            numbers = k.iota[:, 0:EXPERTS].rearrange("p (a e) -> p a e", a=1).to_broadcast([P, TILES, EXPERTS])
            for i, (to, w) in enumerate(((one, w1), (two, w2))):
                link(dve.tensor_tensor(to, numbers, whichf[:, :, i:i + 1].to_broadcast([P, TILES, EXPERTS]), ALU.is_equal))
                link(dve.tensor_tensor(to, to, wide(w), ALU.mult))
            link(dve.tensor_tensor(k.gates, one, two, ALU.add))
            dve.drain().then_inc(s_exp, 1)

            def keep(t, s):
                reuse(dve, s_b2, t)
                dve.wait_ge(s_wt, t + 1)
                dve.sem_inc(k.s_tick, 1)
                dve.tensor_copy(wT[s], k.bank[s][0:EXPERTS, 0:P]).then_inc(s_wk, 1)
                dve.wait_ge(s_b2, t + 1)
                x2 = k.acc[:, bass.ds(t, 1), 0:D].rearrange("p a n -> p (a n)")
                dve.tensor_tensor(x2, x2, k.bank[2 + s][:, 0:D], ALU.add).then_inc(s_add, 1)
            over_tiles(dve, keep)
            dve.wait_ge(s_add, TILES)

        @block.scalar
        def _(act):
            def step(t, s):
                reuse(act, s_l, t)
                reuse(act, s_c, t)
                act.wait_ge(s_t, t + 1)
                act.activation(yT[s], k.bank[s][:, 0:D], ACT.Copy).then_inc(s_k, 1)
            over_tiles(act, step)
            act.wait_ge(s_ch, 1)
            act.activation(dif, dif, ACT.Exp).then_inc(s_exp, 1)
            act.wait_ge(s_exp, 2)

            def stage(t, s):
                reuse(act, s_wt, t)
                act.sem_inc(k.s_tick, 1)
                act.activation(y[s][:, 0:EXPERTS], k.gates[:, bass.ds(t, 1), :].rearrange("p a e -> p (a e)"),
                               ACT.Copy).then_inc(s_k, 1)
            over_tiles(act, stage)

        @block.gpsimd
        def _(pool):
            def step(t, s):
                pool.wait_ge(s_k, t + 1)
                pool.sem_inc(k.s_tick, 1)
                pool.tensor_copy(k.acc[:, bass.ds(t, 1), D:2 * D].rearrange("p a n -> p (a n)"), yT[s]).then_inc(s_c, 1)
            over_tiles(pool, step)
            pool.wait_ge(s_c, TILES)

        @block.tensor
        def _(pe):
            def turn(t, s):
                pe.wait_ge(s_b, t + 1)
                reuse(pe, s_k, t)
                for c in range(KD):
                    mm = pe.transpose(k.bank[s][:, c * P:(c + 1) * P], y[s][:, c * P:(c + 1) * P], k.ident[:, :])
                mm.then_inc(s_t, 1)
                pe.wait_ge(s_k, t + 1)
                reuse(pe, s_lb, t)
                for c in range(KD):
                    mm = pe.matmul(k.bank[2 + s][:, 0:EXPERTS], yT[s][:, c * P:(c + 1) * P], k.Wr[:, c, :],
                                   start=c == 0, stop=c == KD - 1)
                mm.then_inc(s_l, 1)
            over_tiles(pe, turn)

            def biases(t, s):
                pe.wait_ge(s_k, TILES + t + 1)
                reuse(pe, s_wk, t)
                pe.transpose(k.bank[s][0:EXPERTS, 0:P], y[s][:, 0:EXPERTS], k.ident[:, :]).then_inc(s_wt, 1)
                pe.wait_ge(s_wk, t + 1)
                reuse(pe, s_add, t)
                pe.matmul(k.bank[2 + s][:, 0:D], wT[s], k.eb2[:, :], start=True, stop=True).then_inc(s_b2, 1)
            over_tiles(pe, biases)


def experts(k, a):
    nc, sem, work = k.nc, k.sem, k.work
    w1 = [work[:, i * 1024:(i + 1) * 1024].rearrange("p (k n) -> p k n", k=KD) for i in range(2)]
    w2 = [work[:, 2048 + i * 1024:2048 + (i + 1) * 1024].rearrange("p (k n) -> p k n", k=KH) for i in range(2)]
    hT = work[:, 4096:4096 + KH * QUAD * P].rearrange("p (m n) -> p m n", m=KH)
    s_h, s_o, s_y = sem("ffn_hidden"), sem("ffn_out"), sem("ffn_stored")
    s_g, s_add, s_through = sem("ffn_active"), sem("ffn_added"), sem("ffn_expert_through")
    s_w = [sem(f"ffn_weights{i}") for i in range(2)]

    def over_quads(eng, body):
        with eng.Fori(0, QUADS) as q:
            body(q, QUAD)
        body(QUADS, 1)

    def over_experts(eng, body):
        with eng.Fori(0, EXPERTS // 2) as i:
            body(i, 0)
            body(i, 1)

    with nc.Block() as block:
        @block.sync
        def _(sp):
            def fetch(i, par):
                e = 2 * i + par
                sp.wait_ge(s_through, e + 1)
                sp.dma_start(w1[par], a["L0_ffn_W1"][bass.ds(e, 1), :, :].rearrange("a (k p) n -> p (a k) n", p=P)
                             ).then_inc(s_w[par], 16)
                sp.dma_start(w2[par], a["L0_ffn_W2"][bass.ds(e, 1), :, :].rearrange("a (k p) n -> p (a k) n", p=P)
                             ).then_inc(s_w[par], 16)
            sp.sem_inc(s_through, 2)
            over_experts(sp, fetch)
            sp.wait_ge(s_add, 1 + EXPERTS * TILES)
            sp.dma_start(a["out"][0:(TILES - 1) * P, :].rearrange("(t p) d -> p t d", p=P),
                         k.acc[:, 0:TILES - 1, 0:D]).then_inc(s_y, 16)
            sp.dma_start(a["out"][(TILES - 1) * P:NODES, :], k.acc[0:LAST, TILES - 1, 0:D]).then_inc(s_y, 16)
            sp.wait_ge(s_y, 32)

        @block.tensor
        def _(pe):
            def expert(i, par):
                e = 2 * i + par
                pe.wait_ge(s_w[par], 32 * i + 32)
                pe.sem_inc(k.s_tick, 1)

                def quad(q, tiles):
                    n = e * (QUADS + 1) + q
                    for m in range(KH):
                        pe.wait_ge(s_g, KH * n + m + 1)
                        pe.sem_inc(k.s_tick, 1)
                        for c in range(KD):
                            mm = pe.matmul(k.bank[m][:, 0:tiles * P].rearrange("p (t n) -> p t n", n=P),
                                           w1[par][:, c, m * P:(m + 1) * P],
                                           k.acc[:, bass.ds(q * QUAD, tiles), D + c * P:D + (c + 1) * P],
                                           start=c == 0, stop=c == KD - 1)
                        mm.then_inc(s_h, 1)
                    pe.wait_ge(s_g, KH * (n + 2))
                    pe.wait_ge(s_add, e * TILES + q * QUAD + 1)
                    for t in range(tiles):
                        for m in range(KH):
                            mm = pe.matmul(k.bank[4 + t][:, 0:D], hT[:, m, t * P:(t + 1) * P], w2[par][:, m, :],
                                           start=m == 0, stop=m == KH - 1)
                        mm.then_inc(s_o, 1)
                over_quads(pe, quad)
            over_experts(pe, expert)

        @block.scalar
        def _(act):
            act.sem_inc(s_g, KH)

            def expert(i, par):
                e = 2 * i + par

                def quad(q, tiles):
                    n = e * (QUADS + 1) + q
                    for m in range(KH):
                        act.wait_ge(s_h, KH * n + m + 1)
                        act.sem_inc(k.s_tick, 1)
                        act.activation(hT[:, m, 0:tiles * P], k.bank[m][:, 0:tiles * P], ACT.Gelu,
                                       bias=k.eb1[:, bass.ds(e, 1), m:m + 1].rearrange("p a b -> p (a b)")
                                       ).then_inc(s_g, 1)
                over_quads(act, quad)
            over_experts(act, expert)

        @block.vector
        def _(dve):
            dve.sem_inc(s_add, 1)

            def expert(i, par):
                e = 2 * i + par

                def quad(q, tiles):
                    for t in range(tiles):
                        dve.wait_ge(s_o, e * TILES + q * QUAD + t + 1)
                        y = k.acc[:, bass.ds(q * QUAD + t, 1), 0:D].rearrange("p a n -> p (a n)")
                        dve.scalar_tensor_tensor(
                            out=y, in0=k.bank[4 + t][:, 0:D],
                            scalar=k.gates[:, bass.ds(q * QUAD + t, 1), bass.ds(e, 1)].rearrange("p a b -> p (a b)"),
                            in1=y, op0=ALU.mult, op1=ALU.add).then_inc(s_add, 1)
                over_quads(dve, quad)
                dve.wait_ge(s_add, 1 + (e + 1) * TILES)
                dve.sem_inc(s_through, 1)
            over_experts(dve, expert)


def build(nc, a):
    with ExitStack() as ctx:
        k = Core()
        allocate(nc, ctx, k)
        load(k, a)
        norm(k, "norm1", 0, 0)
        attention(k, a)
        place_edges(k)
        scale_input(k, a)
        for layer, width in enumerate((D, H, H)):
            aggregate(k, layer, width)
            update(k, layer)
        norm(k, "norm2", 0, D)
        norm(k, "norm3", D, D)
        route(k)
        experts(k, a)


INPUTS = ["x", "src", "dst", "L0_gnn_W1", "L0_gnn_b1", "L0_gnn_W2", "L0_gnn_b2", "L0_gnn_W3", "L0_gnn_b3",
          "L0_gnn_Wfc", "L0_gnn_bfc", "L0_mix_W_qkv", "L0_mix_W_out", "L0_mix_b_out", "L0_ffn_gamma",
          "L0_ffn_beta", "L0_ffn_Wr", "L0_ffn_br", "L0_ffn_W1", "L0_ffn_b1", "L0_ffn_W2", "L0_ffn_b2"]


def kernel(**inputs):
    import numpy as np
    import concourse.bacc as bacc
    from concourse.bass_utils import run_bass_kernel_spmd

    nc = bacc.Bacc("TRN2", target_bir_lowering=False, num_devices=1)
    arrays, a = {}, {}
    for name in INPUTS:
        array = np.ascontiguousarray(inputs[name])
        arrays[f"in_{name}"] = array
        a[name] = nc.dram_tensor(f"in_{name}", array.shape, mybir.dt.from_np(array.dtype), kind="ExternalInput").ap()
    a["out"] = nc.dram_tensor("out_0", (NODES, D), F32, kind="ExternalOutput").ap()
    build(nc, a)
    r = run_bass_kernel_spmd(nc, [arrays], core_ids=[0])
    return r.results[0]["out_0"]
```

```python
from contextlib import ExitStack

import concourse.bass as bass
from concourse import mybir

ALU = mybir.AluOpType
ACT = mybir.ActivationFunctionType
AX = mybir.AxisListType
F32 = mybir.dt.float32
F16 = mybir.dt.float16
I32 = mybir.dt.int32
U32 = mybir.dt.uint32
U16 = mybir.dt.uint16

P = 128
NODES, D, H = 6250, 256, 512
TILES = -(-NODES // P)
LAST = NODES - (TILES - 1) * P
KD, KH = D // P, H // P
HID, DH = 128, 32
EXPERTS = 8
EDGES = 106250
EP = 125
EC = EDGES // EP
GRP = 2
UNROLL = 8
GROUPS = -(-((EDGES + TILES * (GRP * P - 1)) // (GRP * P)) // UNROLL) * UNROLL
SLOTS = GROUPS * GRP
HALF = SLOTS // 2
STEPS = GROUPS // UNROLL
RING = UNROLL * GRP
LAG = STEPS - TILES + 1
QUAD = 4
QUADS = TILES // QUAD
EPS = 1e-5
SHIFT = 7
assert EP * EC == EDGES and 1 << SHIFT == P and QUADS * QUAD + 1 == TILES and TILES % 2 == 1


class Core:
    pass


def over_tiles(eng, body):
    body(0, 0)
    body(1, 1)
    with eng.Fori(1, TILES // 2) as i:
        body(2 * i, 0)
        body(2 * i + 1, 1)
    body(TILES - 1, 0)


def reuse(eng, sem, t, lag=2):
    if not isinstance(t, int) or t >= lag:
        eng.wait_ge(sem, t - (lag - 1))


def allocate(nc, ctx, k):
    def sb(name, shape, dt=F32):
        return ctx.enter_context(nc.sbuf_tensor("sb_" + name, shape, dt))

    def sem(name):
        return ctx.enter_context(nc.semaphore(name))

    k.nc, k.sem = nc, sem
    k.bank = [ctx.enter_context(nc.psum_tensor(f"bank{i}", [P, 512], F32)) for i in range(8)]
    k.acc = sb("acc", [P, TILES, H])
    k.work = sb("work", [P, 11264])
    k.wts = sb("wts", [P, 6144])
    k.Wqkv = sb("Wqkv", [P, KD, 3, HID])
    k.Wout = sb("Wout", [P, D])
    k.bias = [sb(f"bias{i}", [P, H]) for i in range(3)]
    k.rb, k.bfc = sb("rb", [P, D]), sb("bfc", [P, D])
    k.gamma, k.beta = sb("gamma", [P, D]), sb("beta", [P, D])
    k.Wr, k.br = sb("Wr", [P, KD, EXPERTS]), sb("br", [P, EXPERTS])
    k.eb1, k.eb2 = sb("eb1", [P, EXPERTS, KH]), sb("eb2", [EXPERTS, D])
    k.iota16 = sb("iota16", [P, SLOTS], F16)
    k.iota = sb("iota", [P, P])
    k.ident, k.ones = sb("ident", [P, P]), sb("ones", [P, P])
    k.lower = sb("lower", [P, P])
    k.slot_dst = sb("slot_dst", [P, SLOTS], U32)
    k.slot_row = sb("slot_row", [P, SLOTS])
    k.even = sb("even", [1, 1], I32)
    k.table = sb("table", [1, GROUPS], I32)
    k.index = sb("index", [P, RING], U32)
    k.dinv, k.mean, k.rstd = sb("dinv", [P, TILES]), sb("mean", [P, TILES]), sb("rstd", [P, TILES])
    k.stats = sb("stats", [P, TILES, 6])
    k.small = sb("small", [P, 5, TILES])
    k.eps = sb("eps", [P, 1])
    k.stage = sb("stage", [P, 2 * (D + H)])
    k.agg = [sem(f"agg_{x}") for x in ("index", "one_hot", "summed", "added")]
    k.agg_got = [sem(f"agg_got{s}") for s in range(RING)]
    k.upd = [[sem(f"upd{layer}_{x}") for x in (
        "scaled", "turned1", "kept1", "lifted", "biased", "active", "turned", "kept", "product", "done", "stored",
        "resid0", "resid1")] for layer in range(3)]
    k.small_hot = sb("small_hot", [P, 10, TILES + 1], F16)
    k.W1 = k.wts[:, 0:KD * H].rearrange("p (k n) -> p k n", k=KD)
    k.Wfc = k.wts[:, 1024:1024 + KH * D].rearrange("p (k n) -> p k n", k=KH)
    k.W2 = k.wts[:, 2048:4096].rearrange("p (k n) -> p k n", k=KH)
    k.W3 = k.wts[:, 4096:6144].rearrange("p (k n) -> p k n", k=KH)
    k.keys = k.work[:, 0:TILES * P]
    k.edge = [k.wts[0:EP, i * EC:(i + 1) * EC] for i in range(7)]
    k.edge += [k.work[0:EP, TILES * P + i * EC:TILES * P + (i + 1) * EC] for i in range(5)]
    k.feats = [nc.dram_tensor(f"feats{i}", (TILES * P, w), F32, kind="Internal").ap()
               for i, w in enumerate((D, H, H))]
    k.resid = nc.dram_tensor("resid", (TILES * P, D), F32, kind="Internal").ap()
    k.s_const = sem("constants_ready")
    k.s_tick = sem("tick")


def load(k, a):
    nc, sem = k.nc, k.sem
    s_zeroed, s_x, s_w, s_e, s_pad = sem("zeroed"), sem("x_loaded"), sem("w_loaded"), sem("e_loaded"), sem("pad_zeroed")
    with nc.Block() as block:
        @block.sync
        def _(sp):
            sp.dma_start(k.edge[7].bitcast(I32), a["src"].rearrange("(p c) -> p c", c=EC)).then_inc(s_e, 16)
            sp.dma_start(k.edge[8].bitcast(I32), a["dst"].rearrange("(p c) -> p c", c=EC)).then_inc(s_e, 16)
            sp.dma_start(k.acc[:, 0:TILES - 1, 0:D],
                         a["x"][0:(TILES - 1) * P, :].rearrange("(t p) d -> p t d", p=P)).then_inc(s_x, 16)
            sp.wait_ge(s_pad, 1)
            sp.dma_start(k.acc[0:LAST, TILES - 1, 0:D], a["x"][(TILES - 1) * P:NODES, :]).then_inc(s_x, 16)
            sp.wait_ge(s_x, 32)
            sp.wait_ge(s_e, 32)

        @block.scalar
        def _(act):
            def get(to, of):
                act.dma_start(to, of).then_inc(s_w, 16)
            get(k.Wqkv[:, :, :, :], a["L0_mix_W_qkv"].rearrange("(k p) (c n) -> p k c n", p=P, c=3))
            get(k.Wout[:, :], a["L0_mix_W_out"])
            rows = [(k.bias[0], "L0_gnn_b1"), (k.bias[1], "L0_gnn_b2"), (k.bias[2], "L0_gnn_b3"),
                    (k.rb, "L0_mix_b_out"), (k.bfc, "L0_gnn_bfc"), (k.gamma, "L0_ffn_gamma"),
                    (k.beta, "L0_ffn_beta"), (k.br, "L0_ffn_br")]
            for to, name in rows:
                n = a[name].shape[0]
                get(to[:, :], a[name].rearrange("(a n) -> a n", a=1).to_broadcast([P, n]))
            get(k.Wr[:, :, :], a["L0_ffn_Wr"].rearrange("(k p) n -> p k n", p=P))
            get(k.eb2[:, :], a["L0_ffn_b2"])
            with nc.allow_non_contiguous_dma(reason="a small bias, its features on partitions"):
                for e in range(EXPERTS):
                    get(k.eb1[:, e, :], a["L0_ffn_b1"][e].rearrange("(k p) -> p k", p=P))
            act.wait_ge(s_w, 16 * (4 + len(rows) + EXPERTS))

        @block.gpsimd
        def _(pool):
            pool.memset(k.ident[:, :], 0.0).then_inc(s_zeroed, 1)
            pool.memset(k.lower[:, :], 1.0).then_inc(s_zeroed, 1)
            pool.memset(k.ones[:, :], 1.0)
            pool.memset(k.eps[:, :], EPS)
            for row in (k.iota16, k.iota):
                pool.iota(row[:, :], pattern=[[1, row.shape[1]]], base=0, channel_multiplier=0,
                          allow_small_or_imprecise_dtypes=True)
            pool.wait_ge(s_zeroed, 2)
            pool.affine_select(out=k.ident[:, :], in_=k.ident[:, :], compare_op=ALU.not_equal, fill=1.0, base=0,
                               pattern=[[-1, P]], channel_multiplier=1)
            pool.affine_select(out=k.lower[:, :], in_=k.lower[:, :], compare_op=ALU.is_gt, fill=0.0, base=0,
                               pattern=[[1, P]], channel_multiplier=-1).then_inc(k.s_const, 1)

        @block.vector
        def _(dve):
            dve.memset(k.acc[:, TILES - 1, 0:D], 0.0).then_inc(s_pad, 1)


def norm(k, name, lo, to):
    nc, sem = k.nc, k.sem
    s_stats, s_var, s_sqrt, s_done = (sem(f"{name}_{x}") for x in ("stats", "var", "sqrt", "done"))
    sm = k.small
    with nc.Block() as block:
        @block.vector
        def _(dve):
            with dve.Fori(0, TILES) as t:
                dve.bn_stats(k.stats[:, bass.ds(t, 1), :], k.acc[:, bass.ds(t, 1), lo:lo + D]).then_inc(s_stats, 1)
            dve.wait_ge(s_stats, TILES)
            m0, m1, q0, q1 = (k.stats[:, :, i] for i in (1, 4, 2, 5))
            dve.tensor_tensor(sm[:, 0, :], m0, m1, ALU.add).then_inc(s_var, 1)
            dve.tensor_tensor(sm[:, 1, :], m0, m1, ALU.subtract).then_inc(s_var, 1)
            dve.tensor_tensor(sm[:, 2, :], q0, q1, ALU.add).then_inc(s_var, 1)
            dve.wait_ge(s_var, 3)
            dve.tensor_scalar(k.mean[:, :], sm[:, 0, :], 0.5, None, ALU.mult).then_inc(s_var, 1)
            dve.scalar_tensor_tensor(out=sm[:, 3, :], in0=sm[:, 1, :], scalar=D / 4.0, in1=sm[:, 1, :],
                                     op0=ALU.mult, op1=ALU.mult).then_inc(s_var, 1)
            dve.wait_ge(s_var, 5)
            dve.tensor_tensor(sm[:, 4, :], sm[:, 3, :], sm[:, 2, :], ALU.add).then_inc(s_var, 1)
            dve.wait_ge(s_sqrt, 1)
            dve.reciprocal(k.rstd[:, :], k.rstd[:, :]).then_inc(s_var, 1)
            dve.wait_ge(s_var, 7)
            with dve.Fori(0, TILES) as t:
                dve.tensor_scalar(k.acc[:, bass.ds(t, 1), to:to + D], k.acc[:, bass.ds(t, 1), lo:lo + D],
                                  k.mean[:, bass.ds(t, 1)], k.rstd[:, bass.ds(t, 1)],
                                  ALU.subtract, ALU.mult).then_inc(s_done, 1)
            dve.wait_ge(s_done, TILES)

        @block.scalar
        def _(act):
            act.wait_ge(s_var, 6)
            act.activation(k.rstd[:, :], sm[:, 4, :], ACT.Sqrt, bias=k.eps[:, 0:1], scale=1.0 / D).then_inc(s_sqrt, 1)


def attention(k, a):
    nc, sem, work = k.nc, k.sem, k.work
    st = [k.wts[:, i * D:(i + 1) * D] for i in range(2)]
    xT = [k.wts[:, (2 + i) * D:(3 + i) * D].rearrange("p (k n) -> p k n", k=KD) for i in range(2)]
    expk = [k.wts[:, 1024 + i * P:1024 + (i + 1) * P] for i in range(2)]
    ctx_m, ctx_T = k.wts[:, 1280:1408], k.wts[:, 1408:1536]
    mix = k.wts[:, 1536:1792]
    xr = [k.wts[:, 1792 + i * D:1792 + (i + 1) * D] for i in range(2)]
    ro = [k.wts[:, 2304 + i * D:2304 + (i + 1) * D] for i in range(2)]
    kmax, ksum, krec = k.wts[:, 2816:2817], k.wts[:, 2817:2818], k.wts[:, 2818:2819]
    scratch = [sem(f"att_{x}") for x in (
        "staged", "turned", "turned_kept", "projected", "keys_kept", "qv_kept", "max", "exp", "pad")]
    s_st, s_tr, s_xT, s_qkv, s_k, s_qv, s_max, s_exp, s_pad = scratch
    e_st, e_tr, e_kept, s_ctx, s_fin = (sem(f"ctx_{x}") for x in ("staged", "turned", "kept", "summed", "finished"))
    o_st, o_mm, o_done = (sem(f"mix_{x}") for x in ("staged", "product", "added"))
    o_x = [sem(f"mix_x_loaded{i}") for i in range(2)]
    s_rb = sem("rb_ready")
    o_added2 = sem("mix_finished")
    o_outs = [sem(f"mix_stored{i}") for i in range(2)]

    with nc.Block() as block:
        @block.scalar
        def _(act):
            def stage_x(t, s):
                reuse(act, s_tr, t)
                act.sem_inc(k.s_tick, 1)
                act.activation(st[s], k.acc[:, bass.ds(t, 1), 0:D], ACT.Copy).then_inc(s_st, 1)

            def project(t, s):
                if not isinstance(t, int) or t < TILES - 1:
                    stage_x(t + 1, 1 - s)
                act.wait_ge(s_qkv, t + 1)
                act.sem_inc(k.s_tick, 1)
                act.activation(k.keys[:, bass.ds(t * P, P)], k.bank[6 + s][:, 0:P], ACT.Copy).then_inc(s_k, 1)
            stage_x(0, 0)
            over_tiles(act, project)
            act.wait_ge(s_k, TILES)
            act.wait_ge(s_max, 1)
            act.activation(k.keys[:, 0:NODES], k.keys[:, 0:NODES], ACT.Exp, bias=kmax, accum_out=ksum).then_inc(s_exp, 1)
            act.wait_ge(s_exp, 1)
            act.wait_ge(s_pad, 1)

            def stage_keys(t, s):
                reuse(act, e_tr, t)
                act.sem_inc(k.s_tick, 1)
                act.activation(st[s][:, 0:P], k.keys[:, bass.ds(t * P, P)], ACT.Copy).then_inc(e_st, 1)
            over_tiles(act, stage_keys)
            act.wait_ge(e_tr, TILES)

            def stage_queries(t, s):
                reuse(act, o_mm, t)
                act.sem_inc(k.s_tick, 1)
                act.activation(st[s][:, 0:P], k.acc[:, bass.ds(t, 1), D:D + P], ACT.Copy).then_inc(o_st, 1)
            over_tiles(act, stage_queries)

        @block.tensor
        def _(pe):
            def turn(t, s):
                pe.wait_ge(s_st, t + 1)
                reuse(pe, s_xT, t)
                for c in range(KD):
                    mm = pe.transpose(k.bank[s][:, c * P:(c + 1) * P], st[s][:, c * P:(c + 1) * P], k.ident[:, :])
                mm.then_inc(s_tr, 1)

            def project(t, s):
                if not isinstance(t, int) or t < TILES - 1:
                    turn(t + 1, 1 - s)
                pe.wait_ge(s_xT, t + 1)
                reuse(pe, s_k, t)
                reuse(pe, s_qv, t)
                for c in range(KD):
                    pe.matmul(k.bank[2 + s][:, 0:P], k.Wqkv[:, c, 0, :], xT[s][:, c, :], start=c == 0, stop=c == KD - 1)
                for c in range(KD):
                    pe.matmul(k.bank[2 + s][:, P:2 * P], xT[s][:, c, :], k.Wqkv[:, c, 2, :],
                              start=c == 0, stop=c == KD - 1)
                for c in range(KD):
                    mm = pe.matmul(k.bank[6 + s][:, 0:P], k.Wqkv[:, c, 1, :], xT[s][:, c, :],
                                   start=c == 0, stop=c == KD - 1)
                mm.then_inc(s_qkv, 1)
            turn(0, 0)
            over_tiles(pe, project)

            def turn_keys(t, s):
                pe.wait_ge(e_st, t + 1)
                reuse(pe, e_kept, t)
                pe.transpose(k.bank[s][:, 0:P], st[s][:, 0:P], k.ident[:, :]).then_inc(e_tr, 1)

            def context(t, s):
                if not isinstance(t, int) or t < TILES - 1:
                    turn_keys(t + 1, 1 - s)
                pe.wait_ge(e_kept, t + 1)
                pe.sem_inc(k.s_tick, 1)
                first, last = isinstance(t, int) and t == 0, isinstance(t, int) and t == TILES - 1
                pe.matmul(k.bank[4][:, 0:P], expk[s], k.acc[:, bass.ds(t, 1), D + P:D + 2 * P],
                          start=first, stop=last).then_inc(s_ctx, 1)
            turn_keys(0, 0)
            over_tiles(pe, context)
            pe.wait_ge(s_fin, 4)
            pe.transpose(k.bank[5][:, 0:P], ctx_m, k.ident[:, :]).then_inc(s_ctx, 1)
            pe.wait_ge(s_fin, 5)
            pe.matmul(k.bank[6][:, 0:D], ctx_T, k.Wout[:, :], start=True, stop=True).then_inc(s_ctx, 1)
            pe.wait_ge(s_fin, 6)

            def apply(t, s):
                pe.wait_ge(o_st, t + 1)
                reuse(pe, o_done, t)
                pe.matmul(k.bank[s][:, 0:D], st[s][:, 0:P], mix, start=True, stop=True).then_inc(o_mm, 1)
            over_tiles(pe, apply)

        @block.vector
        def _(dve):
            dve.tensor_tensor(k.rb[:, :], k.rb[:, :], k.bfc[:, :], ALU.add).then_inc(s_rb, 1)

            def keep(t, s):
                dve.wait_ge(s_tr, t + 1)
                reuse(dve, s_qkv, t)
                dve.sem_inc(k.s_tick, 1)
                dve.tensor_copy(xT[s], k.bank[s][:, 0:D].rearrange("p (k n) -> p k n", k=KD)).then_inc(s_xT, 1)
                dve.wait_ge(s_qkv, t + 1)
                dve.sem_inc(k.s_tick, 1)
                dve.tensor_copy(k.acc[:, bass.ds(t, 1), D:2 * D],
                                k.bank[2 + s][:, 0:D].rearrange("p (a n) -> p a n", a=1)).then_inc(s_qv, 1)
            over_tiles(dve, keep)
            dve.wait_ge(s_k, TILES)
            dve.memset(k.keys[:, NODES:TILES * P], 0.0).then_inc(s_pad, 1)
            dve.tensor_reduce(krec, k.keys[:, 0:NODES], AX.X, ALU.max).then_inc(s_rb, 1)
            dve.wait_ge(s_rb, 2)
            dve.tensor_scalar(kmax, krec, -1.0, None, ALU.mult).then_inc(s_max, 1)

            def keep_keys(t, s):
                dve.wait_ge(e_tr, t + 1)
                reuse(dve, s_ctx, t)
                dve.sem_inc(k.s_tick, 1)
                dve.tensor_copy(expk[s], k.bank[s][:, 0:P]).then_inc(e_kept, 1)
            over_tiles(dve, keep_keys)
            dve.wait_ge(s_exp, 1)
            dve.wait_ge(s_max, 1)
            dve.memset(ctx_m, 0.0).then_inc(s_rb, 1)
            dve.reciprocal(krec, ksum).then_inc(s_rb, 1)
            dve.wait_ge(s_rb, 4)
            dve.wait_ge(s_ctx, TILES)
            for h in range(HID // DH):
                b = slice(h * DH, (h + 1) * DH)
                dve.tensor_scalar(ctx_m[b, b], k.bank[4][b, b], krec[b, :], float(DH) ** -0.5,
                                  ALU.mult, ALU.mult).then_inc(s_fin, 1)
            dve.wait_ge(s_ctx, TILES + 1)
            dve.tensor_copy(ctx_T, k.bank[5][:, 0:P]).then_inc(s_fin, 1)
            dve.wait_ge(s_ctx, TILES + 2)
            dve.tensor_copy(mix, k.bank[6][:, 0:D]).then_inc(s_fin, 1)

            def add(t, s):
                dve.wait_ge(o_x[s], 16 * (t // 2 + 1) if isinstance(t, int) else 8 * (t - s) + 16)
                reuse(dve, o_added2, t)
                dve.wait_ge(o_mm, t + 1)
                dve.tensor_tensor(xr[s], xr[s], k.bank[s][:, 0:D], ALU.add).then_inc(o_done, 1)
                dve.wait_ge(o_done, t + 1)
                if not isinstance(t, int) or t >= 2:
                    dve.wait_ge(o_outs[s], 16 * (t // 2) if isinstance(t, int) else 8 * (t - s))
                dve.tensor_tensor(ro[s], xr[s], k.rb[:, :], ALU.add).then_inc(o_added2, 1)
            over_tiles(dve, add)

        @block.sync
        def _(sp):
            def fetch(t, s):
                reuse(sp, o_added2, t)
                n = LAST if isinstance(t, int) and t == TILES - 1 else P
                sp.dma_start(xr[s][0:n, :], a["x"][bass.ds(t * P, n), :]).then_inc(o_x[s], 16)

            over_tiles(sp, fetch)

        @block.gpsimd
        def _(pool):
            def store(t, s):
                pool.wait_ge(o_added2, t + 1)
                pool.sem_inc(k.s_tick, 1)
                pool.dma_start(k.resid[bass.ds(t * P, P), :], ro[s]).then_inc(o_outs[s], 16)
            over_tiles(pool, store)
            pool.wait_ge(o_outs[0], 16 * (TILES // 2 + 1))
            pool.wait_ge(o_outs[1], 16 * (TILES // 2))


def place_edges(k):
    nc, sem = k.nc, k.sem
    npart, nv1, v1, part, v2, chunk, hi = k.edge[0:7]
    lo, pos = k.edge[11], npart
    src, dst, tmp = (k.edge[i].bitcast(I32) for i in (7, 8, 9))
    mask = [k.edge[8][:, i * (EC // 2):(i + 1) * (EC // 2)].bitcast(U16) for i in range(2)]
    zeros = k.edge[7][:, 0:EC // 2].bitcast(U16)
    count = [k.edge[10], nv1]
    tab = k.keys
    per = tab[0:EP, 0:TILES]
    need, groups, ends, start = (tab[:, 64 * i:64 * i + TILES] for i in range(1, 5))
    needi = tab[:, 320:320 + TILES].bitcast(I32)
    col, coli, colg, cole = (tab[0:TILES, 384 + i:385 + i] for i in range(4))
    behind = tab[0:TILES, 512:512 + GROUPS]
    evenf = tab[0:1, 2600:2600 + 128]
    zrow = tab[:, 1536:1536 + TILES]
    tabf = tab[0:1, 1600:1600 + GROUPS]
    s_link, s_per, s_tot, s_tab, s_cmp, s_look = (sem(f"edges_{x}") for x in (
        "keyed", "counted", "totals", "tabled", "ends", "looked_up"))
    s_mask, s_count, s_pos, s_prep = (sem(f"rank_{x}") for x in ("masked", "counted", "placed", "prepared"))
    n = [0]
    GH = GROUPS // 2

    with nc.Block() as block:
        @block.vector
        def _(dve):
            def link(ins):
                n[0] += 1
                ins.then_inc(s_link, 1)
                dve.wait_ge(s_link, n[0])
            link(dve.tensor_scalar(tmp, src, SHIFT, None, ALU.logical_shift_right))
            link(dve.tensor_copy(hi, tmp))
            link(dve.tensor_scalar(tmp, src, P - 1, None, ALU.bitwise_and))
            link(dve.tensor_copy(lo, tmp))
            link(dve.tensor_scalar(tmp, dst, 2, None, ALU.logical_shift_right))
            link(dve.tensor_copy(v1, tmp))
            link(dve.tensor_scalar(tmp, dst, 3, None, ALU.bitwise_and))
            link(dve.tensor_copy(pos, tmp))
            link(dve.tensor_scalar(v2, pos, 256.0, 1.0, ALU.mult, ALU.add))
            link(dve.tensor_tensor(v2, v2, lo, ALU.add))
            link(dve.memset(zeros, 0))
            link(dve.memset(zrow, 0.0))
            with dve.Fori(0, TILES) as b:
                dve.tensor_scalar(tmp.bitcast(F32), hi, k.iota[0:EP, bass.ds(b, 1)], None, ALU.is_equal, ALU.add,
                                  accum_out=per[:, bass.ds(b, 1)]).then_inc(s_per, 1)
                dve.wait_ge(s_per, b + 1)
            dve.wait_ge(s_tot, 1)
            link(dve.tensor_scalar(needi, k.bank[0][:, 64:64 + TILES], GRP * P - 1.0, None, ALU.add))
            link(dve.tensor_scalar(needi, needi, SHIFT + GRP.bit_length() - 1, None, ALU.logical_shift_right))
            link(dve.tensor_copy(groups, needi))
            link(dve.tensor_tensor_scan(ends, groups, zrow, 0.0, ALU.add, ALU.add))
            link(dve.tensor_scalar(evenf[:, 0:TILES], k.iota[0:1, 0:TILES], float(UNROLL), float(UNROLL * LAG),
                                   ALU.mult, ALU.add))
            link(dve.tensor_tensor(evenf[:, 0:TILES], evenf[:, 0:TILES], ends[0:1, :], ALU.is_ge))
            link(dve.tensor_reduce(evenf[:, 64:65], evenf[:, 0:TILES - 1], AX.X, ALU.min))
            link(dve.tensor_copy(k.even[:, :], evenf[:, 64:65]))
            link(dve.tensor_tensor(start, ends, groups, ALU.subtract))
            link(dve.tensor_scalar(start, start, float(GRP * P), -1.0, ALU.mult, ALU.add))
            link(dve.tensor_tensor(start[0:EP, :], start[0:EP, :], k.bank[0][0:EP, 0:TILES], ALU.add))
            link(dve.tensor_scalar(coli.bitcast(I32), k.bank[0][0:TILES, 128:129], GRP * P - 1.0, None, ALU.add))
            link(dve.tensor_scalar(coli.bitcast(I32), coli.bitcast(I32), SHIFT + GRP.bit_length() - 1, None,
                                   ALU.logical_shift_right))
            link(dve.tensor_copy(colg, coli.bitcast(I32)))
            dve.drain().then_inc(s_tab, 1)
            dve.wait_ge(s_cmp, 1)
            link(dve.tensor_tensor(cole, colg, k.bank[1][0:TILES, 0:1], ALU.add))
            link(dve.tensor_scalar(behind, k.iota16[0:TILES, 0:GROUPS], cole, None, ALU.is_ge))
            dve.drain().then_inc(s_tab, 1)
            dve.wait_ge(s_look, 2)
            for h in range(2):
                link(dve.tensor_scalar(tabf[:, h * GH:(h + 1) * GH], k.bank[2 + h][0:1, 0:GH], TILES - 1.0, None, ALU.min))
            link(dve.tensor_copy(k.table[:, :], tabf))
            def rank(b, s):
                reuse(dve, s_pos, b)
                dve.tensor_scalar(mask[s], hi, k.iota[0:EP, bass.ds(b, 1)], None, ALU.is_equal).then_inc(s_mask, 1)
                dve.wait_ge(s_mask, b + 1)
                dve.tensor_tensor_scan(count[s], mask[s], zeros, start[0:EP, bass.ds(b, 1)],
                                       ALU.add, ALU.add).then_inc(s_count, 1)
                dve.wait_ge(s_count, b + 1)
                dve.sem_inc(k.s_tick, 1)
                dve.copy_predicated(pos, mask[s], count[s]).then_inc(s_pos, 1)
            over_tiles(dve, rank)
            dve.wait_ge(s_pos, TILES)
            link(dve.tensor_copy(tmp, pos))
            link(dve.tensor_scalar(count[0].bitcast(I32), tmp, P - 1, None, ALU.bitwise_and))
            link(dve.tensor_copy(part, count[0].bitcast(I32)))
            link(dve.tensor_scalar(count[0].bitcast(I32), tmp, SHIFT, None, ALU.logical_shift_right))
            link(dve.tensor_copy(chunk, count[0].bitcast(I32)))

        @block.tensor
        def _(pe):
            pe.wait_ge(s_per, TILES)
            pe.matmul(k.bank[0][:, 0:TILES], k.lower[0:EP, :], per, start=True, stop=True)
            pe.matmul(k.bank[0][:, 64:64 + TILES], k.ones[0:EP, :], per, start=True, stop=True)
            pe.matmul(k.bank[0][0:TILES, 128:129], per, k.ones[0:EP, 0:1], start=True, stop=True).then_inc(s_tot, 1)
            pe.wait_ge(s_tab, 1)
            pe.matmul(k.bank[1][0:TILES, 0:1], k.lower[0:TILES, 0:TILES], colg, start=True, stop=True).then_inc(s_cmp, 1)
            pe.wait_ge(s_tab, 2)
            for h in range(2):
                pe.matmul(k.bank[2 + h][0:1, 0:GH], k.ones[0:TILES, 0:1], behind[:, h * GH:(h + 1) * GH],
                          start=True, stop=True).then_inc(s_look, 1)

    BATCH = 5
    tabs = k.work[0:EP, 0:TILES * P].bitcast(F16)
    wide = 930
    move = [tabs[:, b * BATCH * wide:(b + 1) * BATCH * wide].rearrange("p (c n) -> p c n", c=BATCH) for b in range(2)]
    stat = [k.edge[8 + b].bitcast(F16)[:, 0:BATCH * 256].rearrange("p (c a n) -> p c a n", c=BATCH, a=2)
            for b in range(2)]
    stat_lo = [k.edge[10].bitcast(F16)[:, b * BATCH * P:(b + 1) * BATCH * P].rearrange("p (c n) -> p c n", c=BATCH)
               for b in range(2)]
    hi_hot = [k.small_hot[0:EP, b * BATCH:(b + 1) * BATCH, 0:TILES] for b in range(2)]
    far = [k.work[0:EP, 4700 + b * BATCH * P:4700 + (b + 1) * BATCH * P].rearrange("p (c n) -> p c n", c=BATCH)
           for b in range(2)]
    few_act = [k.edge[7][:, 512 + 32 * b:512 + 32 * b + 3 * BATCH].rearrange("p (a c) -> p a c", a=3) for b in range(2)]
    few_dve = [k.edge[7][:, 576 + 32 * b:576 + 32 * b + 4 * BATCH].rearrange("p (a c) -> p a c", a=4) for b in range(2)]
    few_pool = [k.edge[7][:, 640 + 32 * b:640 + 32 * b + BATCH] for b in range(2)]
    for_act = k.wts[0:EP, 0:3 * EC].rearrange("p (a c) -> p a c", a=3)
    for_dve = k.wts[0:EP, 3 * EC:7 * EC].rearrange("p (a c) -> p a c", a=4)
    s_neg, s_far, s_act, s_pool = (sem(f"place_{x}") for x in ("negated", "far", "scalar", "gpsimd"))
    s_fa, s_fd, s_fp = (sem(f"place_few_{x}") for x in ("scalar", "vector", "gpsimd"))
    s_hot, s_mm, s_fin, s_deg = (sem(f"place_{x}") for x in ("one_hot", "product", "finish", "degree"))
    row = k.iota16[0:EP, 0:P]
    with nc.Block() as block:
        def over_batches(eng, body):
            n = EC // BATCH
            body(0, 0, False)
            body(1, 1, False)
            with eng.Fori(1, n // 2 - 1) as i:
                body(2 * i, 0, False)
                body(2 * i + 1, 1, False)
            body(n - 2, 0, False)
            body(n - 1, 1, True)

        @block.scalar
        def _(act):
            def hot(n, s, last):
                if isinstance(n, int) and n == 0:
                    act.wait_ge(s_neg, 2)
                reuse(act, s_mm, n)
                act.sem_inc(k.s_tick, 1)
                act.activation(few_act[s], for_act[:, :, bass.ds(n * BATCH, BATCH)], ACT.Copy).then_inc(s_fa, 1)
                act.wait_ge(s_fa, n + 1)
                for c in range(BATCH):
                    ins = act.activation(far[s][:, c, :], row, ACT.Abs, bias=few_act[s][:, 0, c:c + 1])
                ins.then_inc(s_far, 1)
                act.wait_ge(s_far, n + 1)
                for c in range(BATCH):
                    ins = act.activation(stat[s][:, c, 0, :], far[s][:, c, :], ACT.Relu,
                                         scale=few_act[s][:, 1, c:c + 1], bias=few_act[s][:, 2, c:c + 1])
                ins.then_inc(s_act, 1)
            over_batches(act, hot)
            act.wait_ge(s_deg, 1)
            act.activation(k.small[:, 1, :], k.small[:, 0, :], ACT.Sqrt).then_inc(s_deg, 1)

        @block.gpsimd
        def _(pool):
            def hot(n, s, last):
                reuse(pool, s_mm, n)
                pool.sem_inc(k.s_tick, 1)
                pool.tensor_copy(few_pool[s], lo[:, bass.ds(n * BATCH, BATCH)]).then_inc(s_fp, 1)
                pool.wait_ge(s_fp, n + 1)
                pool.sem_inc(k.s_tick, 1)
                for c in range(BATCH):
                    ins = pool.tensor_scalar(stat_lo[s][:, c, :], row, few_pool[s][:, c:c + 1], None, ALU.is_equal)
                ins.then_inc(s_pool, 1)
            over_batches(pool, hot)

        @block.vector
        def _(dve):
            dve.tensor_scalar(nv1, v1, -1.0, None, ALU.mult).then_inc(s_neg, 1)
            dve.tensor_scalar(npart, part, -1.0, None, ALU.mult).then_inc(s_neg, 1)

            def hot(n, s, last):
                reuse(dve, s_mm, n)
                dve.sem_inc(k.s_tick, 1)
                dve.tensor_copy(few_dve[s], for_dve[:, :, bass.ds(n * BATCH, BATCH)]).then_inc(s_fd, 1)
                dve.wait_ge(s_fd, n + 1)
                for c in range(BATCH):
                    part_c, v2_c, chunk_c = (few_dve[s][:, a, c:c + 1] for a in range(3))
                    dve.tensor_scalar(stat[s][:, c, 1, :], row, part_c, v2_c, ALU.is_equal, ALU.mult)
                    dve.tensor_scalar(move[s][:, c, 0:SLOTS], k.iota16[0:EP, :], chunk_c, None, ALU.is_equal)
                tiles = few_dve[s][:, 3, :].rearrange("p (c a) -> p c a", a=1).to_broadcast([EP, BATCH, TILES])
                columns = row[:, 0:TILES].rearrange("p (a n) -> p a n", a=1).to_broadcast([EP, BATCH, TILES])
                ins = dve.tensor_tensor(hi_hot[s], columns, tiles, ALU.is_equal)
                ins.then_inc(s_hot, 1)
            over_batches(dve, hot)
            dve.wait_ge(s_mm, EC // BATCH)
            m = [0]

            def link(ins):
                m[0] += 1
                ins.then_inc(s_fin, 1)
                dve.wait_ge(s_fin, m[0])
            w = k.wts
            f1, f2, i1, i2 = (w[:, i * SLOTS:(i + 1) * SLOTS] for i in range(4))
            for h in range(2):
                sl = slice(h * HALF, (h + 1) * HALF)
                link(dve.tensor_scalar(f1[:, sl], k.bank[h][:, 0:HALF], 4.0, None, ALU.mult))
                link(dve.tensor_copy(i2.bitcast(I32)[:, sl], k.bank[2 + h][:, 0:HALF]))
            link(dve.tensor_scalar(i1.bitcast(I32), i2.bitcast(I32), 8, None, ALU.logical_shift_right))
            link(dve.tensor_copy(f2, i1.bitcast(I32)))
            link(dve.tensor_tensor(f1, f1, f2, ALU.add))
            link(dve.tensor_copy(k.slot_dst[:, :], f1))
            link(dve.tensor_scalar(i1.bitcast(I32), i2.bitcast(I32), 255, None, ALU.bitwise_and))
            link(dve.tensor_copy(f2, i1.bitcast(I32)))
            link(dve.tensor_scalar(k.slot_row[:, :], f2, -1.0, None, ALU.add))
            dve.tensor_scalar(k.small[:, 0, :], k.bank[4][:, 0:TILES], 1.0, None, ALU.add).then_inc(s_deg, 1)
            dve.wait_ge(s_deg, 2)
            link(dve.reciprocal(k.dinv[:, :], k.small[:, 1, :]))

        @block.tensor
        def _(pe):
            def products(n, s, last):
                pe.wait_ge(s_hot, n + 1)
                pe.wait_ge(s_act, n + 1)
                pe.wait_ge(s_pool, n + 1)
                for c in range(BATCH):
                    start, stop = isinstance(n, int) and n == 0 and c == 0, last and c == BATCH - 1
                    for v in range(2):
                        for h in range(2):
                            pe.matmul(k.bank[2 * v + h][:, 0:HALF], stat[s][:, c, v, :],
                                      move[s][:, c, h * HALF:(h + 1) * HALF], start=start, stop=stop)
                    mm = pe.matmul(k.bank[4][:, 0:TILES], stat_lo[s][:, c, :], hi_hot[s][:, c, :],
                                   start=start, stop=stop)
                mm.then_inc(s_mm, 1)
            over_batches(pe, products)


def scale_input(k, a):
    nc, sem = k.nc, k.sem
    s_scaled, s_written, s_loaded = sem("scaled"), sem("scaled_written"), sem("gnn_weights_loaded")
    with nc.Block() as block:
        @block.vector
        def _(dve):
            with dve.Fori(0, TILES) as t:
                dve.tensor_scalar(k.acc[:, bass.ds(t, 1), 0:D], k.acc[:, bass.ds(t, 1), 0:D],
                                  k.dinv[:, bass.ds(t, 1)], None, ALU.mult).then_inc(s_scaled, 1)

        @block.sync
        def _(sp):
            for to, name in ((k.W1, "L0_gnn_W1"), (k.Wfc, "L0_gnn_Wfc"), (k.W2, "L0_gnn_W2"), (k.W3, "L0_gnn_W3")):
                sp.dma_start(to, a[name].rearrange("(k p) n -> p k n", p=P)).then_inc(s_loaded, 16)
            sp.wait_ge(s_scaled, TILES)
            sp.dma_start(k.feats[0].rearrange("(t p) d -> p t d", p=P), k.acc[:, :, 0:D]).then_inc(s_written, 16)
            sp.wait_ge(s_written, 16)
            sp.wait_ge(s_loaded, 64)


class Update:

    def __init__(self, k, layer, depth, place, banks):
        self.k, self.layer, self.depth = k, layer, depth

        def parts(at, width):
            return [place[:, at + i * width:at + (i + 1) * width] for i in range(depth)]
        self.v, self.vT = parts(0, D), parts(depth * D, D)
        self.z, self.zT = parts(2 * depth * D, H), parts(depth * (2 * D + H), H)
        self.res = self.v
        self.A, self.B, self.C, self.E = (banks[i * depth:(i + 1) * depth] for i in range(4))
        self.W, self.width = (k.W2, k.W3, k.Wfc)[layer], (H, H, D)[layer]
        sems = k.upd[layer]
        (self.s_v, self.s_t1, self.s_k1, self.s_m1, self.s_z, self.s_r, self.s_t, self.s_k, self.s_m, self.s_done,
         self.s_stored) = sems[0:11]
        self.s_res = sems[11:13]

    def reuse(self, eng, sem, t):
        reuse(eng, sem, t, self.depth)

    def scale(self, dve, t, s):
        self.reuse(dve, self.s_t1, t)
        dve.tensor_scalar(self.v[s], self.k.acc[:, bass.ds(t, 1), 0:D].rearrange("p a n -> p (a n)"),
                          self.k.dinv[:, bass.ds(t, 1)], None, ALU.mult).then_inc(self.s_v, 1)

    def bias(self, dve, t, s):
        self.reuse(dve, self.s_t, t)
        if self.layer == 0:
            dve.wait_ge(self.s_m1, t + 1)
            dve.tensor_tensor(self.z[s], self.B[s][:, :], self.k.bias[0][:, :], ALU.add).then_inc(self.s_z, 1)
        else:
            dve.scalar_tensor_tensor(out=self.z[s], in0=self.k.acc[:, bass.ds(t, 1), :].rearrange("p a n -> p (a n)"),
                                     scalar=self.k.dinv[:, bass.ds(t, 1)], in1=self.k.bias[self.layer][:, :],
                                     op0=ALU.mult, op1=ALU.add).then_inc(self.s_z, 1)

    def finish(self, dve, t, s):
        one = self.k.acc[:, bass.ds(t, 1), 0:self.width].rearrange("p a n -> p (a n)")
        if self.layer < 2:
            dve.wait_ge(self.s_m, t + 1)
            dve.tensor_scalar(one, self.E[s][:, :], self.k.dinv[:, bass.ds(t, 1)], None, ALU.mult
                              ).then_inc(self.s_done, 1)
        else:
            dve.wait_ge(self.s_res[s], self.loads(t, s))
            dve.wait_ge(self.s_m, t + 1)
            dve.tensor_tensor(one, self.E[s][:, 0:D], self.res[s], ALU.add).then_inc(self.s_done, 1)

    def keep1(self, act, t, s):
        self.reuse(act, self.s_m1, t)
        act.wait_ge(self.s_t1, t + 1)
        act.activation(self.vT[s], self.A[s][:, 0:D], ACT.Copy).then_inc(self.s_k1, 1)

    def relu(self, act, t, s):
        act.wait_ge(self.s_z, t + 1)
        act.activation(self.z[s], self.z[s], ACT.Relu).then_inc(self.s_r, 1)

    def keep(self, act, t, s):
        self.reuse(act, self.s_m, t)
        act.wait_ge(self.s_t, t + 1)
        act.activation(self.zT[s], self.C[s][:, :], ACT.Copy).then_inc(self.s_k, 1)

    def turn1(self, pe, t, s):
        pe.wait_ge(self.s_v, t + 1)
        self.reuse(pe, self.s_k1, t)
        for c in range(KD):
            mm = pe.transpose(self.A[s][:, c * P:(c + 1) * P], self.v[s][:, c * P:(c + 1) * P], self.k.ident[:, :])
        mm.then_inc(self.s_t1, 1)

    def lift(self, pe, t, s):
        pe.wait_ge(self.s_k1, t + 1)
        self.reuse(pe, self.s_z, t)
        for c in range(KD):
            mm = pe.matmul(self.B[s][:, :], self.vT[s][:, c * P:(c + 1) * P], self.k.W1[:, c, :],
                           start=c == 0, stop=c == KD - 1)
        mm.then_inc(self.s_m1, 1)

    def turn(self, pe, t, s):
        pe.wait_ge(self.s_r, t + 1)
        self.reuse(pe, self.s_k, t)
        for c in range(KH):
            mm = pe.transpose(self.C[s][:, c * P:(c + 1) * P], self.z[s][:, c * P:(c + 1) * P], self.k.ident[:, :])
        mm.then_inc(self.s_t, 1)

    def product(self, pe, t, s):
        pe.wait_ge(self.s_k, t + 1)
        self.reuse(pe, self.s_done, t)
        for c in range(KH):
            mm = pe.matmul(self.E[s][:, 0:self.width], self.zT[s][:, c * P:(c + 1) * P], self.W[:, c, :],
                           start=c == 0, stop=c == KH - 1)
        mm.then_inc(self.s_m, 1)

    def store(self, sp, t):
        sp.wait_ge(self.s_done, t + 1)
        sp.dma_start(self.k.feats[self.layer + 1][bass.ds(t * P, P), :],
                     self.k.acc[:, bass.ds(t, 1), :].rearrange("p a n -> p (a n)")).then_inc(self.s_stored, 16)

    def fetch(self, sp, t, s):
        self.reuse(sp, self.s_done, t)
        sp.dma_start(self.res[s], self.k.resid[bass.ds(t * P, P), :]).then_inc(self.s_res[s], 16)

    def loads(self, t, s):
        if self.depth == 1:
            return 16 * (t + 1)
        return 16 * (t // 2 + 1) if isinstance(t, int) else 8 * (t - s) + 16


def more(t):
    return not isinstance(t, int) or t < TILES - 1


def evenly(k, eng):
    return eng.value_load(k.even[0:1, 0:1], min_val=0, max_val=1)


def update(k, layer):
    u = Update(k, layer, 2, k.work, k.bank)
    with k.nc.Block() as block:
        @block.vector
        def _(dve):
            with dve.If(evenly(k, dve) == 0):
                if layer == 0:
                    u.scale(dve, 0, 0)
                else:
                    u.bias(dve, 0, 0)

                def step(t, s):
                    if layer == 0:
                        if more(t):
                            u.scale(dve, t + 1, 1 - s)
                        u.bias(dve, t, s)
                    elif more(t):
                        u.bias(dve, t + 1, 1 - s)
                    u.finish(dve, t, s)
                over_tiles(dve, step)
                dve.wait_ge(u.s_done, TILES)
                dve.sem_inc(k.s_tick, 1)

        @block.scalar
        def _(act):
            with act.If(evenly(k, act) == 0):
                def step(t, s):
                    if layer == 0:
                        u.keep1(act, t, s)
                    u.relu(act, t, s)
                    u.keep(act, t, s)
                over_tiles(act, step)
                act.sem_inc(k.s_tick, 1)

        @block.tensor
        def _(pe):
            with pe.If(evenly(k, pe) == 0):
                if layer == 0:
                    u.turn1(pe, 0, 0)
                    u.lift(pe, 0, 0)
                else:
                    u.turn(pe, 0, 0)

                def step(t, s):
                    if layer == 0:
                        if more(t):
                            u.turn1(pe, t + 1, 1 - s)
                        u.turn(pe, t, s)
                        if more(t):
                            u.lift(pe, t + 1, 1 - s)
                    elif more(t):
                        u.turn(pe, t + 1, 1 - s)
                    u.product(pe, t, s)
                over_tiles(pe, step)
                pe.sem_inc(k.s_tick, 1)

        @block.sync
        def _(sp):
            with sp.If(evenly(k, sp) == 0):
                if layer < 2:
                    over_tiles(sp, lambda t, s: u.store(sp, t))
                    sp.wait_ge(u.s_stored, 16 * TILES)
                else:
                    over_tiles(sp, lambda t, s: u.fetch(sp, t, s))
                    for s in range(2):
                        sp.wait_ge(u.s_res[s], u.loads(TILES - 1 - s, s))
                sp.sem_inc(k.s_tick, 1)


def aggregate(k, layer, width):
    nc = k.nc
    feats = k.feats[layer]
    ring = k.work[:, 0:RING * H].rearrange("p (s n) -> p s n", s=RING)
    hot = k.work[:, RING * H:RING * (H + P)].rearrange("p (s n) -> p s n", s=RING)
    s_index, s_hot, s_sum, s_add = k.agg
    s_got = k.agg_got
    G0, I0 = layer * GROUPS, layer * STEPS
    BANKS = 4
    LEAD = 3
    half = RING // 2
    u = Update(k, layer, 1, k.stage, k.bank[BANKS:])
    pe_does = {0: u.turn1, 2: u.lift, 4: u.turn, 6: u.product} if layer == 0 else {1: u.turn, 4: u.product}
    dve_does = {3: u.bias, 7: u.finish} if layer == 0 else {5: u.finish}

    def over_steps(eng, step):
        step(0, None)
        with eng.Fori(1, STEPS - 1) as i:
            step(i, None)
        step(STEPS - 1, None)

    def over_steps_even(eng, step):
        step(0, None)
        with eng.Fori(1, LAG) as i:
            step(i, None)
        step(LAG, 0)
        with eng.Fori(LAG + 1, STEPS - 1) as i:
            step(i, i - LAG)
        step(STEPS - 1, STEPS - 1 - LAG)

    with nc.Block() as block:
        @block.gpsimd
        def _(pool):
            def step(i, tile):
                for h in range(2):
                    if not isinstance(i, int) or i > 0:
                        pool.wait_ge(s_sum, G0 + (i - 1) * UNROLL + (h + 1) * (UNROLL // 2))
                    pool.sem_inc(k.s_tick, 1)
                    pool.tensor_copy(k.index[:, h * half:(h + 1) * half],
                                     k.slot_dst[:, bass.ds(i * RING + h * half, half)]).then_inc(s_index, 1)
                    pool.wait_ge(s_index, 2 * I0 + 2 * i + h + 1)
                    pool.sem_inc(k.s_tick, 1)
                    for s in range(h * half, (h + 1) * half):
                        pool.indirect_dma_start(
                            out=ring[:, s, 0:width], out_offset=None, in_=feats[:, :],
                            in_offset=bass.IndirectOffsetOnAxis(ap=k.index[:, s:s + 1], axis=0),
                            bounds_check=TILES * P - 1, oob_is_err=False).then_inc(s_got[s], 16)
            over_steps(pool, step)

        @block.vector
        def _(dve):
            def one_hot(g, j):
                if not isinstance(g, int) or g >= UNROLL:
                    dve.wait_ge(s_sum, G0 + g - UNROLL + 1)
                for c in range(GRP):
                    s = j * GRP + c
                    ins = dve.tensor_scalar(hot[:, s, :], k.iota[:, :], k.slot_row[:, bass.ds(g * GRP + c, 1)], None,
                                            ALU.is_equal)
                ins.then_inc(s_hot, 1)

            def add(g, j):
                t = dve.value_load(k.table[0:1, bass.ds(g, 1)], min_val=0, max_val=TILES - 1)
                if not isinstance(g, int) or g > 0:
                    dve.wait_ge(s_add, G0 + g)
                dve.wait_ge(s_sum, G0 + g + 1)
                dve.tensor_tensor(k.acc[:, bass.ds(t, 1), 0:width], k.acc[:, bass.ds(t, 1), 0:width],
                                  k.bank[j % BANKS][:, 0:width].rearrange("p (a n) -> p a n", a=1),
                                  ALU.add).then_inc(s_add, 1)

            def step(i, tile):
                if tile is not None:
                    dve.wait_ge(s_add, G0 + i * UNROLL)
                    (u.scale if layer == 0 else u.bias)(dve, tile, 0)
                for j in range(UNROLL):
                    g = i * UNROLL + j
                    if not (isinstance(i, int) and g + LEAD >= GROUPS):
                        one_hot(g + LEAD, (j + LEAD) % UNROLL)
                    if tile is not None and j in dve_does:
                        dve_does[j](dve, tile, 0)
                    add(g, j)

            for g in range(LEAD):
                one_hot(g, g)
            with dve.If(evenly(k, dve) == 1):
                over_steps_even(dve, step)
                dve.wait_ge(s_add, G0 + GROUPS)
                if layer == 0:
                    u.scale(dve, TILES - 1, 0)
                u.bias(dve, TILES - 1, 0)
                u.finish(dve, TILES - 1, 0)
                dve.wait_ge(u.s_done, TILES)
                dve.sem_inc(k.s_tick, 1)
            with dve.Else():
                over_steps(dve, step)
                dve.sem_inc(k.s_tick, 1)

        @block.tensor
        def _(pe):
            def step(i, tile):
                for j in range(UNROLL):
                    g = i * UNROLL + j
                    pe.wait_ge(s_hot, G0 + g + 1)
                    if not isinstance(i, int) or g >= BANKS:
                        pe.wait_ge(s_add, G0 + g - BANKS + 1)
                    for c in range(GRP):
                        s = j * GRP + c
                        pe.wait_ge(s_got[s], 16 * (I0 + i + 1))
                        mm = pe.matmul(k.bank[j % BANKS][:, 0:width], hot[:, s, :], ring[:, s, 0:width],
                                       start=c == 0, stop=c == GRP - 1)
                    mm.then_inc(s_sum, 1)
                    if tile is not None and j in pe_does:
                        pe_does[j](pe, tile, 0)
            with pe.If(evenly(k, pe) == 1):
                over_steps_even(pe, step)
                for j in sorted(pe_does):
                    pe_does[j](pe, TILES - 1, 0)
                pe.sem_inc(k.s_tick, 1)
            with pe.Else():
                over_steps(pe, step)
                pe.sem_inc(k.s_tick, 1)

        @block.scalar
        def _(act):
            with act.If(evenly(k, act) == 1):
                def step(t):
                    if layer == 0:
                        u.keep1(act, t, 0)
                    u.relu(act, t, 0)
                    u.keep(act, t, 0)
                step(0)
                with act.Fori(1, TILES) as t:
                    step(t)
                act.sem_inc(k.s_tick, 1)

        @block.sync
        def _(sp):
            with sp.If(evenly(k, sp) == 1):
                if layer < 2:
                    with sp.Fori(0, TILES) as t:
                        u.store(sp, t)
                    sp.wait_ge(u.s_stored, 16 * TILES)
                else:
                    u.fetch(sp, 0, 0)
                    with sp.Fori(1, TILES) as t:
                        u.fetch(sp, t, 0)
                    sp.wait_ge(u.s_res[0], 16 * TILES)
                sp.sem_inc(k.s_tick, 1)


def route(k):
    nc, sem, work = k.nc, k.sem, k.work
    y = [work[:, i * D:(i + 1) * D] for i in range(2)]
    yT = [work[:, 512 + i * D:512 + (i + 1) * D] for i in range(2)]
    wT = [work[0:EXPERTS, 1024 + i * P:1024 + (i + 1) * P] for i in range(2)]
    logits = k.gates = k.wts[:, 0:TILES * EXPERTS].rearrange("p (t e) -> p t e", e=EXPERTS)
    best = k.wts[:, 512:512 + TILES * 8].rearrange("p (t e) -> p t e", e=8)
    which = k.wts[:, 1024:1024 + TILES * 8].bitcast(U32).rearrange("p (t e) -> p t e", e=8)
    whichf = k.wts[:, 1536:1536 + TILES * 8].rearrange("p (t e) -> p t e", e=8)
    one, two = (k.wts[:, 2048 + i * 512:2048 + i * 512 + TILES * EXPERTS].rearrange("p (t e) -> p t e", e=EXPERTS)
                for i in range(2))
    w1, w2, dif = (k.small[:, i, :] for i in range(3))
    names = ("g", "b", "turned", "kept", "copied", "logits", "biased", "best", "chain", "exp", "wturned", "wkept", "b2", "added")
    s_g, s_b, s_t, s_k, s_c, s_l, s_lb, s_best, s_ch, s_exp, s_wt, s_wk, s_b2, s_add = (sem(f"gate_{x}") for x in names)
    with nc.Block() as block:
        @block.vector
        def _(dve):
            def affine(t, s):
                reuse(dve, s_t, t)
                dve.tensor_tensor(y[s], k.acc[:, bass.ds(t, 1), D:2 * D].rearrange("p a n -> p (a n)"), k.gamma[:, :],
                                  ALU.mult).then_inc(s_g, 1)
                dve.wait_ge(s_g, t + 1)
                dve.tensor_tensor(y[s], y[s], k.beta[:, :], ALU.add).then_inc(s_b, 1)
                dve.wait_ge(s_l, t + 1)
                dve.tensor_tensor(logits[:, bass.ds(t, 1), :].rearrange("p a e -> p (a e)"), k.bank[2 + s][:, 0:EXPERTS],
                                  k.br[:, :], ALU.add).then_inc(s_lb, 1)
            over_tiles(dve, affine)
            dve.wait_ge(s_lb, TILES)
            for t in range(TILES):
                dve.max(best[:, t, :], logits[:, t, :]).then_inc(s_best, 1)
            dve.wait_ge(s_best, TILES)
            for t in range(TILES):
                dve.max_index(which[:, t, :], best[:, t, :], logits[:, t, :]).then_inc(s_best, 1)
            n = [0]

            def link(ins):
                n[0] += 1
                ins.then_inc(s_ch, 1)
                dve.wait_ge(s_ch, n[0])
            link(dve.tensor_tensor(dif, best[:, :, 1], best[:, :, 0], ALU.subtract))
            dve.wait_ge(s_exp, 1)
            link(dve.tensor_scalar(w2, dif, 1.0, None, ALU.add))
            link(dve.reciprocal(w1, w2))
            link(dve.tensor_tensor(w2, dif, w1, ALU.mult))
            dve.wait_ge(s_best, 2 * TILES)
            link(dve.tensor_copy(whichf, which))

            def wide(x):
                return x.rearrange("p (t a) -> p t a", a=1).to_broadcast([P, TILES, EXPERTS])
            numbers = k.iota[:, 0:EXPERTS].rearrange("p (a e) -> p a e", a=1).to_broadcast([P, TILES, EXPERTS])
            for i, (to, w) in enumerate(((one, w1), (two, w2))):
                link(dve.tensor_tensor(to, numbers, whichf[:, :, i:i + 1].to_broadcast([P, TILES, EXPERTS]), ALU.is_equal))
                link(dve.tensor_tensor(to, to, wide(w), ALU.mult))
            link(dve.tensor_tensor(k.gates, one, two, ALU.add))
            dve.drain().then_inc(s_exp, 1)

            def keep(t, s):
                reuse(dve, s_b2, t)
                dve.wait_ge(s_wt, t + 1)
                dve.sem_inc(k.s_tick, 1)
                dve.tensor_copy(wT[s], k.bank[s][0:EXPERTS, 0:P]).then_inc(s_wk, 1)
                dve.wait_ge(s_b2, t + 1)
                x2 = k.acc[:, bass.ds(t, 1), 0:D].rearrange("p a n -> p (a n)")
                dve.tensor_tensor(x2, x2, k.bank[2 + s][:, 0:D], ALU.add).then_inc(s_add, 1)
            over_tiles(dve, keep)
            dve.wait_ge(s_add, TILES)

        @block.scalar
        def _(act):
            def step(t, s):
                reuse(act, s_l, t)
                reuse(act, s_c, t)
                act.wait_ge(s_t, t + 1)
                act.activation(yT[s], k.bank[s][:, 0:D], ACT.Copy).then_inc(s_k, 1)
            over_tiles(act, step)
            act.wait_ge(s_ch, 1)
            act.activation(dif, dif, ACT.Exp).then_inc(s_exp, 1)
            act.wait_ge(s_exp, 2)

            def stage(t, s):
                reuse(act, s_wt, t)
                act.sem_inc(k.s_tick, 1)
                act.activation(y[s][:, 0:EXPERTS], k.gates[:, bass.ds(t, 1), :].rearrange("p a e -> p (a e)"),
                               ACT.Copy).then_inc(s_k, 1)
            over_tiles(act, stage)

        @block.gpsimd
        def _(pool):
            def step(t, s):
                pool.wait_ge(s_k, t + 1)
                pool.sem_inc(k.s_tick, 1)
                pool.tensor_copy(k.acc[:, bass.ds(t, 1), D:2 * D].rearrange("p a n -> p (a n)"), yT[s]).then_inc(s_c, 1)
            over_tiles(pool, step)
            pool.wait_ge(s_c, TILES)

        @block.tensor
        def _(pe):
            def turn(t, s):
                pe.wait_ge(s_b, t + 1)
                reuse(pe, s_k, t)
                for c in range(KD):
                    mm = pe.transpose(k.bank[s][:, c * P:(c + 1) * P], y[s][:, c * P:(c + 1) * P], k.ident[:, :])
                mm.then_inc(s_t, 1)
                pe.wait_ge(s_k, t + 1)
                reuse(pe, s_lb, t)
                for c in range(KD):
                    mm = pe.matmul(k.bank[2 + s][:, 0:EXPERTS], yT[s][:, c * P:(c + 1) * P], k.Wr[:, c, :],
                                   start=c == 0, stop=c == KD - 1)
                mm.then_inc(s_l, 1)
            over_tiles(pe, turn)

            def biases(t, s):
                pe.wait_ge(s_k, TILES + t + 1)
                reuse(pe, s_wk, t)
                pe.transpose(k.bank[s][0:EXPERTS, 0:P], y[s][:, 0:EXPERTS], k.ident[:, :]).then_inc(s_wt, 1)
                pe.wait_ge(s_wk, t + 1)
                reuse(pe, s_add, t)
                pe.matmul(k.bank[2 + s][:, 0:D], wT[s], k.eb2[:, :], start=True, stop=True).then_inc(s_b2, 1)
            over_tiles(pe, biases)


def experts(k, a):
    nc, sem, work = k.nc, k.sem, k.work
    w1 = [work[:, i * 1024:(i + 1) * 1024].rearrange("p (k n) -> p k n", k=KD) for i in range(2)]
    w2 = [work[:, 2048 + i * 1024:2048 + (i + 1) * 1024].rearrange("p (k n) -> p k n", k=KH) for i in range(2)]
    hT = work[:, 4096:4096 + KH * QUAD * P].rearrange("p (m n) -> p m n", m=KH)
    s_h, s_o, s_y = sem("ffn_hidden"), sem("ffn_out"), sem("ffn_stored")
    s_g, s_add, s_through = sem("ffn_active"), sem("ffn_added"), sem("ffn_expert_through")
    s_w = [sem(f"ffn_weights{i}") for i in range(2)]

    def over_quads(eng, body):
        with eng.Fori(0, QUADS) as q:
            body(q, QUAD)
        body(QUADS, 1)

    def over_experts(eng, body):
        with eng.Fori(0, EXPERTS // 2) as i:
            body(i, 0)
            body(i, 1)

    with nc.Block() as block:
        @block.sync
        def _(sp):
            def fetch(i, par):
                e = 2 * i + par
                sp.wait_ge(s_through, e + 1)
                sp.dma_start(w1[par], a["L0_ffn_W1"][bass.ds(e, 1), :, :].rearrange("a (k p) n -> p (a k) n", p=P)
                             ).then_inc(s_w[par], 16)
                sp.dma_start(w2[par], a["L0_ffn_W2"][bass.ds(e, 1), :, :].rearrange("a (k p) n -> p (a k) n", p=P)
                             ).then_inc(s_w[par], 16)
            sp.sem_inc(s_through, 2)
            over_experts(sp, fetch)
            sp.wait_ge(s_add, 1 + EXPERTS * TILES)
            sp.dma_start(a["out"][0:(TILES - 1) * P, :].rearrange("(t p) d -> p t d", p=P),
                         k.acc[:, 0:TILES - 1, 0:D]).then_inc(s_y, 16)
            sp.dma_start(a["out"][(TILES - 1) * P:NODES, :], k.acc[0:LAST, TILES - 1, 0:D]).then_inc(s_y, 16)
            sp.wait_ge(s_y, 32)

        @block.tensor
        def _(pe):
            def expert(i, par):
                e = 2 * i + par
                pe.wait_ge(s_w[par], 32 * i + 32)
                pe.sem_inc(k.s_tick, 1)

                def quad(q, tiles):
                    n = e * (QUADS + 1) + q
                    for m in range(KH):
                        pe.wait_ge(s_g, KH * n + m + 1)
                        pe.sem_inc(k.s_tick, 1)
                        for c in range(KD):
                            mm = pe.matmul(k.bank[m][:, 0:tiles * P].rearrange("p (t n) -> p t n", n=P),
                                           w1[par][:, c, m * P:(m + 1) * P],
                                           k.acc[:, bass.ds(q * QUAD, tiles), D + c * P:D + (c + 1) * P],
                                           start=c == 0, stop=c == KD - 1)
                        mm.then_inc(s_h, 1)
                    pe.wait_ge(s_g, KH * (n + 2))
                    pe.wait_ge(s_add, e * TILES + q * QUAD + 1)
                    for t in range(tiles):
                        for m in range(KH):
                            mm = pe.matmul(k.bank[4 + t][:, 0:D], hT[:, m, t * P:(t + 1) * P], w2[par][:, m, :],
                                           start=m == 0, stop=m == KH - 1)
                        mm.then_inc(s_o, 1)
                over_quads(pe, quad)
            over_experts(pe, expert)

        @block.scalar
        def _(act):
            act.sem_inc(s_g, KH)

            def expert(i, par):
                e = 2 * i + par

                def quad(q, tiles):
                    n = e * (QUADS + 1) + q
                    for m in range(KH):
                        act.wait_ge(s_h, KH * n + m + 1)
                        act.sem_inc(k.s_tick, 1)
                        act.activation(hT[:, m, 0:tiles * P], k.bank[m][:, 0:tiles * P], ACT.Gelu,
                                       bias=k.eb1[:, bass.ds(e, 1), m:m + 1].rearrange("p a b -> p (a b)")
                                       ).then_inc(s_g, 1)
                over_quads(act, quad)
            over_experts(act, expert)

        @block.vector
        def _(dve):
            dve.sem_inc(s_add, 1)

            def expert(i, par):
                e = 2 * i + par

                def quad(q, tiles):
                    for t in range(tiles):
                        dve.wait_ge(s_o, e * TILES + q * QUAD + t + 1)
                        y = k.acc[:, bass.ds(q * QUAD + t, 1), 0:D].rearrange("p a n -> p (a n)")
                        dve.scalar_tensor_tensor(
                            out=y, in0=k.bank[4 + t][:, 0:D],
                            scalar=k.gates[:, bass.ds(q * QUAD + t, 1), bass.ds(e, 1)].rearrange("p a b -> p (a b)"),
                            in1=y, op0=ALU.mult, op1=ALU.add).then_inc(s_add, 1)
                over_quads(dve, quad)
                dve.wait_ge(s_add, 1 + (e + 1) * TILES)
                dve.sem_inc(s_through, 1)
            over_experts(dve, expert)


def build(nc, a):
    with ExitStack() as ctx:
        k = Core()
        allocate(nc, ctx, k)
        load(k, a)
        norm(k, "norm1", 0, 0)
        attention(k, a)
        place_edges(k)
        scale_input(k, a)
        for layer, width in enumerate((D, H, H)):
            aggregate(k, layer, width)
            update(k, layer)
        norm(k, "norm2", 0, D)
        norm(k, "norm3", D, D)
        route(k)
        experts(k, a)


INPUTS = ["x", "src", "dst", "L0_gnn_W1", "L0_gnn_b1", "L0_gnn_W2", "L0_gnn_b2", "L0_gnn_W3", "L0_gnn_b3",
          "L0_gnn_Wfc", "L0_gnn_bfc", "L0_mix_W_qkv", "L0_mix_W_out", "L0_mix_b_out", "L0_ffn_gamma",
          "L0_ffn_beta", "L0_ffn_Wr", "L0_ffn_br", "L0_ffn_W1", "L0_ffn_b1", "L0_ffn_W2", "L0_ffn_b2"]


def kernel(**inputs):
    import numpy as np
    import concourse.bacc as bacc
    from concourse.bass_utils import run_bass_kernel_spmd

    nc = bacc.Bacc("TRN2", target_bir_lowering=False, num_devices=1)
    arrays, a = {}, {}
    for name in INPUTS:
        array = np.ascontiguousarray(inputs[name])
        arrays[f"in_{name}"] = array
        a[name] = nc.dram_tensor(f"in_{name}", array.shape, mybir.dt.from_np(array.dtype), kind="ExternalInput").ap()
    a["out"] = nc.dram_tensor("out_0", (NODES, D), F32, kind="ExternalOutput").ap()
    build(nc, a)
    r = run_bass_kernel_spmd(nc, [arrays], core_ids=[0])
    return r.results[0]["out_0"]
```

```python
from contextlib import ExitStack

import concourse.bass as bass
from concourse import mybir

ALU = mybir.AluOpType
ACT = mybir.ActivationFunctionType
AX = mybir.AxisListType
F32 = mybir.dt.float32
F16 = mybir.dt.float16
I32 = mybir.dt.int32
U32 = mybir.dt.uint32
U16 = mybir.dt.uint16

P = 128
NODES, D, H = 6250, 256, 512
TILES = -(-NODES // P)
LAST = NODES - (TILES - 1) * P
KD, KH = D // P, H // P
HID, DH = 128, 32
EXPERTS = 8
EDGES = 106250
EP = 125
EC = EDGES // EP
GRP = 2
UNROLL = 8
GROUPS = -(-((EDGES + TILES * (GRP * P - 1)) // (GRP * P)) // UNROLL) * UNROLL
SLOTS = GROUPS * GRP
HALF = SLOTS // 2
STEPS = GROUPS // UNROLL
RING = UNROLL * GRP
STEPS_EVEN = 56
LAG = STEPS_EVEN - TILES + 1
ETILES = (2 * TILES * P + EXPERTS * (P - 1)) // P
EW = EXPERTS * KH * D
NOWHERE = 2 * TILES * P
BY_PRODUCT = 250
EPS = 1e-5
SHIFT = 7
assert EP * EC == EDGES and 1 << SHIFT == P and TILES % 8 == 1


class Core:
    pass


def over_tiles(eng, body, unroll=6, tail=1):
    for j in range(unroll):
        body(j, j % 2)
    end = (TILES - tail) // unroll
    with eng.Fori(1, end) as i:
        for j in range(unroll):
            body(unroll * i + j, j % 2)
    for t in range(unroll * end, TILES):
        body(t, t % 2)


def reuse(eng, sem, t, lag=2):
    if not isinstance(t, int) or t >= lag:
        eng.wait_ge(sem, t - (lag - 1))


def allocate(nc, ctx, k):
    def sb(name, shape, dt=F32):
        return ctx.enter_context(nc.sbuf_tensor("sb_" + name, shape, dt))

    def sem(name):
        return ctx.enter_context(nc.semaphore(name))

    k.nc, k.sem = nc, sem
    k.bank = [ctx.enter_context(nc.psum_tensor(f"bank{i}", [P, 512], F32)) for i in range(8)]
    k.acc = sb("acc", [P, TILES, H])
    k.work = sb("work", [P, 11264])
    k.wts = sb("wts", [P, 6144])
    k.Wqkv = sb("Wqkv", [P, KD, 3, HID])
    k.Wout = sb("Wout", [P, D])
    k.bias = [sb(f"bias{i}", [P, H]) for i in range(3)]
    k.rb, k.bfc = sb("rb", [P, D]), sb("bfc", [P, D])
    k.gamma, k.beta = sb("gamma", [P, D]), sb("beta", [P, D])
    k.Wr, k.br = sb("Wr", [P, KD, EXPERTS]), sb("br", [P, EXPERTS])
    k.iota16 = sb("iota16", [P, SLOTS], F16)
    k.iota = sb("iota", [P, P])
    k.ident, k.ones = sb("ident", [P, P]), sb("ones", [P, P])
    k.lower = sb("lower", [P, P])
    k.slot_dst = sb("slot_dst", [P, SLOTS], U32)
    k.slot_row = sb("slot_row", [P, SLOTS])
    k.even = sb("even", [1, 1], I32)
    k.table = sb("table", [1, GROUPS], I32)
    k.index = sb("index", [P, 2 * RING], U32)
    k.dinv, k.mean, k.rstd = sb("dinv", [P, TILES]), sb("mean", [P, TILES]), sb("rstd", [P, TILES])
    k.stats = sb("stats", [P, TILES, 6])
    k.small = sb("small", [P, 5, TILES])
    k.eps = sb("eps", [P, 1])
    k.stage = sb("stage", [P, 2 * (D + H)])
    k.agg = [sem(f"agg_{x}") for x in ("index", "one_hot", "summed", "added")]
    k.agg_got = [sem(f"agg_got{s}") for s in range(RING)]
    needless = {0: ("resid0", "resid1"), 1: ("scaled", "turned1", "kept1", "lifted", "resid0", "resid1"),
                2: ("scaled", "turned1", "kept1", "lifted", "stored")}
    k.upd = [[None if x in needless[layer] else sem(f"upd{layer}_{x}") for x in (
        "scaled", "turned1", "kept1", "lifted", "biased", "active", "turned", "kept", "product", "done", "stored",
        "resid0", "resid1")] for layer in range(3)]
    k.small_hot = sb("small_hot", [P, 10, TILES + 1], F16)
    k.W1 = k.wts[:, 0:KD * H].rearrange("p (k n) -> p k n", k=KD)
    k.Wfc = k.wts[:, 1024:1024 + KH * D].rearrange("p (k n) -> p k n", k=KH)
    k.W2 = k.wts[:, 2048:4096].rearrange("p (k n) -> p k n", k=KH)
    k.W3 = k.wts[:, 4096:6144].rearrange("p (k n) -> p k n", k=KH)
    k.keys = k.work[:, 0:TILES * P]
    k.eW2 = k.work[:, 0:EW].rearrange("p (e n) -> p e n", n=D)
    k.logits = k.work[:, EW:EW + TILES * EXPERTS].rearrange("p (t e) -> p t e", e=EXPERTS)
    k.eb1 = k.wts[:, 0:EXPERTS * H].rearrange("p (e n) -> p e n", n=H)
    k.eb2 = k.wts[:, EXPERTS * H:EXPERTS * (H + D)].rearrange("p (e n) -> p e n", n=D)
    k.slot_node, k.slot_result = k.slot_dst[:, 0:ETILES], k.slot_dst[:, ETILES:2 * ETILES]
    k.tile_expert = sb("tile_expert", [1, ETILES], I32)
    k.edge = [k.wts[0:EP, i * EC:(i + 1) * EC] for i in range(7)]
    k.for_dve = k.wts[0:EP, 6 * EC:6 * EC + 3 * BY_PRODUCT].rearrange("p (a c) -> p a c", a=3)
    k.for_act = k.slot_dst[0:EP, 0:3 * BY_PRODUCT].bitcast(F32).rearrange("p (a c) -> p a c", a=3)
    k.edge += [k.work[0:EP, TILES * P + i * EC:TILES * P + (i + 1) * EC] for i in range(5)]
    k.feats = [nc.dram_tensor(f"feats{i}", (TILES * P, w), F32, kind="Internal").ap()
               for i, w in enumerate((D, H, H))]
    k.y_rows = nc.dram_tensor("y_rows", (TILES * P, D), F32, kind="Internal").ap()
    k.results = nc.dram_tensor("results", (2 * TILES * P, D), F32, kind="Internal").ap()
    k.slots = nc.dram_tensor("slots", (SLOTS * P, 1), I32, kind="Internal").ap()
    k.resid = nc.dram_tensor("resid", (TILES * P, D), F32, kind="Internal").ap()
    k.rows_moved = [sem(f"rows_moved{i}") for i in range(4)]
    k.s_const = sem("constants_ready")
    k.s_tick = sem("tick")


def load(k, a):
    nc, sem = k.nc, k.sem
    s_zeroed, s_x, s_w, s_e, s_pad = sem("zeroed"), sem("x_loaded"), sem("w_loaded"), sem("e_loaded"), sem("pad_zeroed")
    with nc.Block() as block:
        @block.sync
        def _(sp):
            sp.dma_start(k.edge[7].bitcast(I32), a["src"].rearrange("(p c) -> p c", c=EC)).then_inc(s_e, 16)
            sp.dma_start(k.edge[8].bitcast(I32), a["dst"].rearrange("(p c) -> p c", c=EC)).then_inc(s_e, 16)
            sp.dma_start(k.acc[:, 0:TILES - 1, 0:D],
                         a["x"][0:(TILES - 1) * P, :].rearrange("(t p) d -> p t d", p=P)).then_inc(s_x, 16)
            sp.wait_ge(s_pad, 1)
            sp.dma_start(k.acc[0:LAST, TILES - 1, 0:D], a["x"][(TILES - 1) * P:NODES, :]).then_inc(s_x, 16)
            sp.wait_ge(s_x, 32)
            sp.wait_ge(s_e, 32)

        @block.scalar
        def _(act):
            def get(to, of):
                act.dma_start(to, of).then_inc(s_w, 16)
            get(k.Wqkv[:, :, :, :], a["L0_mix_W_qkv"].rearrange("(k p) (c n) -> p k c n", p=P, c=3))
            get(k.Wout[:, :], a["L0_mix_W_out"])
            rows = [(k.bias[0], "L0_gnn_b1"), (k.bias[1], "L0_gnn_b2"), (k.bias[2], "L0_gnn_b3"),
                    (k.rb, "L0_mix_b_out"), (k.bfc, "L0_gnn_bfc"), (k.gamma, "L0_ffn_gamma"),
                    (k.beta, "L0_ffn_beta"), (k.br, "L0_ffn_br")]
            for to, name in rows:
                n = a[name].shape[0]
                get(to[:, :], a[name].rearrange("(a n) -> a n", a=1).to_broadcast([P, n]))
            get(k.Wr[:, :, :], a["L0_ffn_Wr"].rearrange("(k p) n -> p k n", p=P))
            act.wait_ge(s_w, 16 * (3 + len(rows)))

        @block.gpsimd
        def _(pool):
            pool.memset(k.ident[:, :], 0.0).then_inc(s_zeroed, 1)
            pool.memset(k.lower[:, :], 1.0).then_inc(s_zeroed, 1)
            pool.memset(k.ones[:, :], 1.0)
            pool.memset(k.eps[:, :], EPS)
            for row in (k.iota16, k.iota):
                pool.iota(row[:, :], pattern=[[1, row.shape[1]]], base=0, channel_multiplier=0,
                          allow_small_or_imprecise_dtypes=True)
            pool.wait_ge(s_zeroed, 2)
            pool.affine_select(out=k.ident[:, :], in_=k.ident[:, :], compare_op=ALU.not_equal, fill=1.0, base=0,
                               pattern=[[-1, P]], channel_multiplier=1)
            pool.affine_select(out=k.lower[:, :], in_=k.lower[:, :], compare_op=ALU.is_gt, fill=0.0, base=0,
                               pattern=[[1, P]], channel_multiplier=-1).then_inc(k.s_const, 1)

        @block.vector
        def _(dve):
            dve.memset(k.acc[:, TILES - 1, 0:D], 0.0).then_inc(s_pad, 1)


def norm(k, name, lo, to):
    nc, sem = k.nc, k.sem
    s_stats, s_var, s_sqrt, s_done = (sem(f"{name}_{x}") for x in ("stats", "var", "sqrt", "done"))
    sm = k.small
    with nc.Block() as block:
        @block.vector
        def _(dve):
            with dve.Fori(0, TILES // 7) as q:
                for i in range(7):
                    t = bass.ds(q * 7 + i, 1)
                    dve.bn_stats(k.stats[:, t, :], k.acc[:, t, lo:lo + D]).then_inc(s_stats, 1)
            dve.wait_ge(s_stats, TILES)
            m0, m1, q0, q1 = (k.stats[:, :, i] for i in (1, 4, 2, 5))
            dve.tensor_tensor(sm[:, 0, :], m0, m1, ALU.add).then_inc(s_var, 1)
            dve.tensor_tensor(sm[:, 1, :], m0, m1, ALU.subtract).then_inc(s_var, 1)
            dve.tensor_tensor(sm[:, 2, :], q0, q1, ALU.add).then_inc(s_var, 1)
            dve.wait_ge(s_var, 3)
            dve.tensor_scalar(k.mean[:, :], sm[:, 0, :], 0.5, None, ALU.mult).then_inc(s_var, 1)
            dve.scalar_tensor_tensor(out=sm[:, 3, :], in0=sm[:, 1, :], scalar=D / 4.0, in1=sm[:, 1, :],
                                     op0=ALU.mult, op1=ALU.mult).then_inc(s_var, 1)
            dve.wait_ge(s_var, 5)
            dve.tensor_tensor(sm[:, 4, :], sm[:, 3, :], sm[:, 2, :], ALU.add).then_inc(s_var, 1)
            dve.wait_ge(s_sqrt, 1)
            dve.reciprocal(k.rstd[:, :], k.rstd[:, :]).then_inc(s_var, 1)
            dve.wait_ge(s_var, 7)
            with dve.Fori(0, TILES // 7) as q:
                for i in range(7):
                    t = bass.ds(q * 7 + i, 1)
                    dve.tensor_scalar(k.acc[:, t, to:to + D], k.acc[:, t, lo:lo + D], k.mean[:, t], k.rstd[:, t],
                                      ALU.subtract, ALU.mult).then_inc(s_done, 1)
            dve.wait_ge(s_done, TILES)

        @block.scalar
        def _(act):
            act.wait_ge(s_var, 6)
            act.activation(k.rstd[:, :], sm[:, 4, :], ACT.Sqrt, bias=k.eps[:, 0:1], scale=1.0 / D).then_inc(s_sqrt, 1)


def attention(k, a):
    placing = Placing(k)
    nc, sem, work = k.nc, k.sem, k.work
    st = [k.wts[:, i * D:(i + 1) * D] for i in range(2)]
    xT = [k.wts[:, (2 + i) * D:(3 + i) * D].rearrange("p (k n) -> p k n", k=KD) for i in range(2)]
    expk = [k.wts[:, 1024 + i * P:1024 + (i + 1) * P] for i in range(2)]
    ctx_m, ctx_T = k.wts[:, 1280:1408], k.wts[:, 1408:1536]
    mix = k.wts[:, 1536:1792]
    stq = [k.wts[:, 1792 + i * H:1792 + (i + 1) * H] for i in range(2)]
    xr = [k.keys[:, i * 4 * D:(i + 1) * 4 * D] for i in range(2)]
    ro = [k.keys[:, (2 + i) * 4 * D:(3 + i) * 4 * D] for i in range(2)]
    FOURS = TILES // 4

    def over_fours(eng, body):
        body(0, 0, 4)
        body(1, 1, 4)
        with eng.Fori(1, FOURS // 2) as i:
            body(2 * i, 0, 4)
            body(2 * i + 1, 1, 4)
        body(FOURS, 0, 1)

    def by_tile(x, n):
        return x[:, 0:n * D].rearrange("p (t d) -> p t d", d=D)
    kmax, ksum, krec = (k.wts[:, 2816 + i:2817 + i] for i in range(3))
    scratch = [sem(f"att_{x}") for x in (
        "staged", "turned", "turned_kept", "projected", "keys_kept", "qv_kept", "max", "exp", "pad")]
    s_st, s_tr, s_xT, s_qkv, s_k, s_qv, s_max, s_exp, s_pad = scratch
    e_st, e_tr, e_kept, s_ctx, s_fin = (sem(f"ctx_{x}") for x in ("staged", "turned", "kept", "summed", "finished"))
    o_st, o_mm, o_done = (sem(f"mix_{x}") for x in ("staged", "product", "added"))
    o_x = [sem(f"mix_x_loaded{i}") for i in range(2)]
    s_rb = sem("rb_ready")
    o_added2 = sem("mix_finished")
    o_outs = [sem(f"mix_stored{i}") for i in range(2)]

    with nc.Block() as block:
        @block.scalar
        def _(act):
            def stage_x(t, s):
                reuse(act, s_tr, t)
                act.sem_inc(k.s_tick, 1)
                act.activation(st[s], k.acc[:, bass.ds(t, 1), 0:D], ACT.Copy).then_inc(s_st, 1)

            def project(t, s):
                if not isinstance(t, int) or t < TILES - 2:
                    stage_x(t + 2, s)
                act.wait_ge(s_qkv, t + 1)
                act.sem_inc(k.s_tick, 1)
                act.activation(k.keys[:, bass.ds(t * P, P)], k.bank[6 + s][:, 0:P], ACT.Copy).then_inc(s_k, 1)
            stage_x(0, 0)
            stage_x(1, 1)
            over_tiles(act, project, tail=2)
            act.wait_ge(s_k, TILES)
            act.wait_ge(s_max, 1)
            act.activation(k.keys[:, 0:NODES], k.keys[:, 0:NODES], ACT.Exp, bias=kmax, accum_out=ksum).then_inc(s_exp, 1)
            act.wait_ge(s_exp, 1)
            act.wait_ge(s_pad, 1)

            def stage_keys(t, s):
                reuse(act, e_tr, t)
                act.sem_inc(k.s_tick, 1)
                act.activation(st[s][:, 0:P], k.keys[:, bass.ds(t * P, P)], ACT.Copy).then_inc(e_st, 1)
            over_tiles(act, stage_keys)
            act.wait_ge(e_tr, TILES)

            def stage_queries(q, s, n):
                reuse(act, o_mm, q)
                act.sem_inc(k.s_tick, 1)
                act.activation(stq[s][:, 0:n * P].rearrange("p (t n) -> p t n", n=P),
                               k.acc[:, bass.ds(4 * q, n), D:D + P], ACT.Copy).then_inc(o_st, 1)
            over_fours(act, stage_queries)
            placing.high(act)
            placing.root(act)

        @block.tensor
        def _(pe):
            def turn(t, s):
                pe.wait_ge(s_st, t + 1)
                reuse(pe, s_xT, t)
                for c in range(KD):
                    mm = pe.transpose(k.bank[s][:, c * P:(c + 1) * P], st[s][:, c * P:(c + 1) * P], k.ident[:, :])
                mm.then_inc(s_tr, 1)

            def project(t, s):
                if not isinstance(t, int) or t < TILES - 1:
                    turn(t + 1, 1 - s)
                pe.wait_ge(s_xT, t + 1)
                reuse(pe, s_k, t)
                reuse(pe, s_qv, t)
                for c in range(KD):
                    pe.matmul(k.bank[2 + s][:, 0:P], k.Wqkv[:, c, 0, :], xT[s][:, c, :], start=c == 0, stop=c == KD - 1)
                for c in range(KD):
                    pe.matmul(k.bank[2 + s][:, P:2 * P], xT[s][:, c, :], k.Wqkv[:, c, 2, :],
                              start=c == 0, stop=c == KD - 1)
                for c in range(KD):
                    mm = pe.matmul(k.bank[6 + s][:, 0:P], k.Wqkv[:, c, 1, :], xT[s][:, c, :],
                                   start=c == 0, stop=c == KD - 1)
                mm.then_inc(s_qkv, 1)
            turn(0, 0)
            over_tiles(pe, project)

            def turn_keys(t, s):
                pe.wait_ge(e_st, t + 1)
                reuse(pe, e_kept, t)
                pe.transpose(k.bank[s][:, 0:P], st[s][:, 0:P], k.ident[:, :]).then_inc(e_tr, 1)

            def context(t, s):
                if not isinstance(t, int) or t < TILES - 1:
                    turn_keys(t + 1, 1 - s)
                pe.wait_ge(e_kept, t + 1)
                pe.sem_inc(k.s_tick, 1)
                first, last = isinstance(t, int) and t == 0, isinstance(t, int) and t == TILES - 1
                pe.matmul(k.bank[4][:, 0:P], expk[s], k.acc[:, bass.ds(t, 1), D + P:D + 2 * P],
                          start=first, stop=last).then_inc(s_ctx, 1)
            turn_keys(0, 0)
            over_tiles(pe, context)
            pe.wait_ge(s_fin, 4)
            pe.transpose(k.bank[5][:, 0:P], ctx_m, k.ident[:, :]).then_inc(s_ctx, 1)
            pe.wait_ge(s_fin, 5)
            pe.matmul(k.bank[6][:, 0:D], ctx_T, k.Wout[:, :], start=True, stop=True).then_inc(s_ctx, 1)
            pe.wait_ge(s_fin, 6)

            def apply(q, s, n):
                pe.wait_ge(o_st, q + 1)
                reuse(pe, o_done, q)
                for t in range(n):
                    mm = pe.matmul(k.bank[2 * s + t // 2][:, t % 2 * D:(t % 2 + 1) * D], stq[s][:, t * P:(t + 1) * P],
                                   mix, start=True, stop=True)
                mm.then_inc(o_mm, 1)
            over_fours(pe, apply)
            placing.degree_products(pe)
            placing.slot_products(pe)

        @block.vector
        def _(dve):
            dve.tensor_tensor(k.rb[:, :], k.rb[:, :], k.bfc[:, :], ALU.add).then_inc(s_rb, 1)

            def keep_x(t, s):
                dve.wait_ge(s_tr, t + 1)
                reuse(dve, s_qkv, t)
                dve.sem_inc(k.s_tick, 1)
                dve.tensor_copy(xT[s], k.bank[s][:, 0:D].rearrange("p (k n) -> p k n", k=KD)).then_inc(s_xT, 1)

            def keep(t, s):
                if more(t):
                    keep_x(t + 1, 1 - s)
                dve.wait_ge(s_qkv, t + 1)
                dve.sem_inc(k.s_tick, 1)
                dve.tensor_copy(k.acc[:, bass.ds(t, 1), D:2 * D],
                                k.bank[2 + s][:, 0:D].rearrange("p (a n) -> p a n", a=1)).then_inc(s_qv, 1)
            keep_x(0, 0)
            over_tiles(dve, keep)
            dve.wait_ge(s_k, TILES)
            dve.memset(k.keys[:, NODES:TILES * P], 0.0).then_inc(s_pad, 1)
            dve.tensor_reduce(krec, k.keys[:, 0:NODES], AX.X, ALU.max).then_inc(s_rb, 1)
            dve.wait_ge(s_rb, 2)
            dve.tensor_scalar(kmax, krec, -1.0, None, ALU.mult).then_inc(s_max, 1)

            def keep_keys(t, s):
                dve.wait_ge(e_tr, t + 1)
                reuse(dve, s_ctx, t)
                dve.sem_inc(k.s_tick, 1)
                dve.tensor_copy(expk[s], k.bank[s][:, 0:P]).then_inc(e_kept, 1)
            over_tiles(dve, keep_keys)
            dve.wait_ge(s_exp, 1)
            dve.wait_ge(s_max, 1)
            dve.memset(ctx_m, 0.0).then_inc(s_rb, 1)
            dve.reciprocal(krec, ksum).then_inc(s_rb, 1)
            dve.wait_ge(s_rb, 4)
            dve.wait_ge(s_ctx, TILES)
            for h in range(HID // DH):
                b = slice(h * DH, (h + 1) * DH)
                dve.tensor_scalar(ctx_m[b, b], k.bank[4][b, b], krec[b, :], float(DH) ** -0.5,
                                  ALU.mult, ALU.mult).then_inc(s_fin, 1)
            dve.wait_ge(s_ctx, TILES + 1)
            dve.tensor_copy(ctx_T, k.bank[5][:, 0:P]).then_inc(s_fin, 1)
            dve.wait_ge(s_ctx, TILES + 2)
            dve.tensor_copy(mix, k.bank[6][:, 0:D]).then_inc(s_fin, 1)

            def add_mix(q, s, n):
                dve.wait_ge(o_x[s], 16 * (q // 2 + 1) if isinstance(q, int) else 8 * (q - s) + 16)
                dve.wait_ge(o_mm, q + 1)
                for t in range(0, n, 2):
                    w = min(n - t, 2) * D
                    ins = dve.tensor_tensor(xr[s][:, t * D:t * D + w], xr[s][:, t * D:t * D + w],
                                            k.bank[2 * s + t // 2][:, 0:w], ALU.add)
                ins.then_inc(o_done, 1)

            def add(q, s, n):
                dve.wait_ge(o_done, q + 1)
                if not isinstance(q, int) or q >= 2:
                    dve.wait_ge(o_outs[s], 16 * (q // 2) if isinstance(q, int) else 8 * (q - s))
                dve.tensor_tensor(by_tile(ro[s], n), by_tile(xr[s], n),
                                  k.rb[:, :].rearrange("p (a n) -> p a n", a=1).to_broadcast([P, n, D]), ALU.add
                                  ).then_inc(o_added2, 1)

            def add_both(q, s, n):
                add_mix(q, s, n)
                add(q, s, n)
            over_fours(dve, add_both)
            placing.degree_hots(dve)
            dve.wait_ge(o_outs[0], 16 * (FOURS // 2 + 1))
            dve.wait_ge(o_outs[1], 16 * (FOURS // 2))
            placing.low_and_chunk(dve)
            placing.finish(dve)

        @block.sync
        def _(sp):
            def rows(x, q, n, last=P):
                part = x[bass.ds(4 * q * P, n * last), :]
                return part.rearrange("(t p) d -> p t d", p=last)

            def fetch(q, s, n):
                last = LAST if n == 1 else P
                sp.dma_start(by_tile(xr[s], n)[0:last, :, :], rows(a["x"], q, n, last)).then_inc(o_x[s], 16)

            def step(q, s, n):
                sp.wait_ge(o_added2, q + 1)
                sp.dma_start(rows(k.resid, q, n), by_tile(ro[s], n)).then_inc(o_outs[s], 16)
                if not isinstance(q, int) or q + 2 < FOURS:
                    fetch(q + 2, s, 4)
                elif q + 2 == FOURS:
                    fetch(q + 2, s, 1)
            sp.wait_ge(e_st, TILES)
            fetch(0, 0, 4)
            fetch(1, 1, 4)
            step(0, 0, 4)
            step(1, 1, 4)
            with sp.Fori(1, FOURS // 2 - 1) as i:
                step(2 * i, 0, 4)
                step(2 * i + 1, 1, 4)
            step(FOURS - 2, 0, 4)
            step(FOURS - 1, 1, 4)
            step(FOURS, 0, 1)
            sp.wait_ge(o_outs[0], 16 * (FOURS // 2 + 1))
            sp.wait_ge(o_outs[1], 16 * (FOURS // 2))
            placing.load(sp)

        @block.gpsimd
        def _(pool):
            placing.scatter(pool)


def rank_edges(k):
    nc, sem = k.nc, k.sem
    pos, part, chunk, val = k.edge[0], k.edge[3], k.edge[2], k.edge[2]
    hi, lo = k.edge[10], k.edge[11]
    spot, packed = k.edge[4].bitcast(I32), k.edge[5].bitcast(I32)
    src, dst, tmp = (k.edge[i].bitcast(I32) for i in (7, 8, 9))
    mask = [k.edge[8][:, i * (EC // 2):(i + 1) * (EC // 2)].bitcast(U16) for i in range(2)]
    zeros = k.edge[7][:, 0:EC // 2].bitcast(U16)
    count = [k.edge[6], k.edge[1]]
    tab = k.keys
    per = tab[0:EP, 0:TILES]
    groups, ends, start = (tab[:, 64 * i:64 * i + TILES] for i in range(2, 5))
    needi = tab[:, 320:320 + TILES].bitcast(I32)
    coli, colg, cole = (tab[0:TILES, 384 + i:385 + i] for i in range(1, 4))
    behind = tab[0:TILES, 512:512 + GROUPS]
    evenf = tab[0:1, 2600:2600 + 128]
    zrow = tab[:, 1536:1536 + TILES]
    tabf = tab[0:1, 1600:1600 + GROUPS]
    s_link, s_per, s_tot, s_tab, s_cmp, s_look = (sem(f"edges_{x}") for x in (
        "keyed", "counted", "totals", "tabled", "ends", "looked_up"))
    s_mask, s_count, s_pos, s_zero, s_empty, s_away = (sem(f"rank_{x}") for x in (
        "masked", "counted", "placed", "zeroed", "emptied", "distances"))
    away = [k.edge[2], k.edge[3]]
    n = [0]
    GH = GROUPS // 2

    with nc.Block() as block:
        @block.sync
        def _(sp):
            sp.wait_ge(s_zero, 1)
            sp.dma_start(k.slots.rearrange("(p c) a -> p (c a)", p=P), k.slot_row[:, :].bitcast(I32)).then_inc(s_empty, 16)
            sp.wait_ge(s_empty, 16)

        @block.vector
        def _(dve):
            def link(ins):
                n[0] += 1
                ins.then_inc(s_link, 1)
                dve.wait_ge(s_link, n[0])
            dve.memset(k.slot_row[:, :], 0.0).then_inc(s_zero, 1)
            link(dve.tensor_scalar(tmp, src, SHIFT, None, ALU.logical_shift_right))
            link(dve.tensor_copy(hi, tmp))
            link(dve.tensor_scalar(tmp, src, P - 1, None, ALU.bitwise_and))
            link(dve.tensor_copy(lo, tmp))
            link(dve.tensor_scalar(tmp, dst, 8, None, ALU.logical_shift_left))
            link(dve.tensor_copy(val, tmp))
            link(dve.scalar_tensor_tensor(out=val, in0=val, scalar=1.0, in1=lo, op0=ALU.add, op1=ALU.add))
            link(dve.tensor_copy(packed, val))
            link(dve.memset(zeros, 0))
            link(dve.memset(zrow, 0.0))
            junk = (tmp.bitcast(F32), count[1])
            def count_edges(b, s):
                reuse(dve, s_per, b)
                dve.tensor_scalar(junk[s], hi, k.iota[0:EP, bass.ds(b, 1)], None, ALU.is_equal, ALU.add,
                                  accum_out=per[:, bass.ds(b, 1)]).then_inc(s_per, 1)
            over_tiles(dve, count_edges)
            dve.wait_ge(s_tot, 1)
            link(dve.tensor_scalar(needi, k.bank[0][:, 64:64 + TILES], GRP * P - 1.0, None, ALU.add))
            link(dve.tensor_scalar(needi, needi, SHIFT + GRP.bit_length() - 1, None, ALU.logical_shift_right))
            link(dve.tensor_copy(groups, needi))
            link(dve.tensor_tensor_scan(ends, groups, zrow, 0.0, ALU.add, ALU.add))
            link(dve.tensor_scalar(evenf[:, 0:TILES], k.iota[0:1, 0:TILES], float(UNROLL), float(UNROLL * LAG),
                                   ALU.mult, ALU.add))
            link(dve.tensor_tensor(evenf[:, 0:TILES], evenf[:, 0:TILES], ends[0:1, :], ALU.is_ge))
            link(dve.tensor_reduce(evenf[:, 64:65], evenf[:, 0:TILES], AX.X, ALU.min))
            link(dve.tensor_copy(k.even[:, :], evenf[:, 64:65]))
            link(dve.tensor_tensor(start, ends, groups, ALU.subtract))
            link(dve.tensor_scalar(start, start, float(GRP * P), -1.0, ALU.mult, ALU.add))
            link(dve.tensor_tensor(start[0:EP, :], start[0:EP, :], k.bank[0][0:EP, 0:TILES], ALU.add))
            link(dve.tensor_scalar(coli.bitcast(I32), k.bank[0][0:TILES, 128:129], GRP * P - 1.0, None, ALU.add))
            link(dve.tensor_scalar(coli.bitcast(I32), coli.bitcast(I32), SHIFT + GRP.bit_length() - 1, None,
                                   ALU.logical_shift_right))
            link(dve.tensor_copy(colg, coli.bitcast(I32)))
            dve.drain().then_inc(s_tab, 1)
            dve.wait_ge(s_cmp, 1)
            link(dve.tensor_tensor(cole, colg, k.bank[1][0:TILES, 0:1], ALU.add))
            link(dve.tensor_scalar(behind, k.iota16[0:TILES, 0:GROUPS], cole, None, ALU.is_ge))
            dve.drain().then_inc(s_tab, 1)
            dve.wait_ge(s_look, 2)
            for h in range(2):
                link(dve.tensor_scalar(tabf[:, h * GH:(h + 1) * GH], k.bank[2 + h][0:1, 0:GH], TILES - 1.0, None, ALU.min))
            link(dve.tensor_copy(k.table[:, :], tabf))
            def rank(b, s):
                dve.wait_ge(s_mask, b + 1)
                dve.tensor_tensor_scan(count[s], mask[s], zeros, start[0:EP, bass.ds(b, 1)],
                                       ALU.add, ALU.add).then_inc(s_count, 1)
                dve.wait_ge(s_count, b + 1)
                dve.sem_inc(k.s_tick, 1)
                dve.copy_predicated(pos, mask[s], count[s]).then_inc(s_pos, 1)
            dve.drain().then_inc(s_tab, 1)
            over_tiles(dve, rank)
            dve.wait_ge(s_pos, TILES)
            link(dve.tensor_copy(tmp, pos))
            link(dve.tensor_scalar(count[0].bitcast(I32), tmp, P - 1, None, ALU.bitwise_and))
            link(dve.tensor_copy(part, count[0].bitcast(I32)))
            link(dve.tensor_scalar(count[0].bitcast(I32), tmp, SHIFT, None, ALU.logical_shift_right))
            link(dve.tensor_copy(chunk, count[0].bitcast(I32)))
            last = slice(EC - BY_PRODUCT, EC)
            for_act, for_dve = k.for_act, k.for_dve
            ti = tmp[:, 0:BY_PRODUCT]
            link(dve.tensor_scalar(ti, packed[:, last], 10, None, ALU.logical_shift_right))
            link(dve.tensor_copy(for_act[:, 2, :], ti))
            link(dve.tensor_scalar(for_act[:, 1, :], for_act[:, 2, :], -1.0, None, ALU.mult))
            link(dve.tensor_scalar(for_act[:, 0, :], part[:, last], -1.0, None, ALU.mult))
            link(dve.tensor_scalar(ti, packed[:, last], 1023, None, ALU.bitwise_and))
            link(dve.tensor_copy(for_dve[:, 1, :], ti))
            link(dve.tensor_copy(for_dve[:, 0, :], part[:, last]))
            link(dve.tensor_copy(for_dve[:, 2, :], chunk[:, last]))
            link(dve.scalar_tensor_tensor(out=pos, in0=part, scalar=float(SLOTS), in1=chunk, op0=ALU.mult, op1=ALU.add))
            link(dve.tensor_copy(spot, pos))

        @block.scalar
        def _(act):
            def distance(b, s):
                reuse(act, s_mask, b)
                act.sem_inc(k.s_tick, 1)
                act.activation(away[s], hi, ACT.Abs, scale=-1.0, bias=k.iota[0:EP, bass.ds(b, 1)]).then_inc(s_away, 1)

            def find(b, s):
                if more(b):
                    distance(b + 1, 1 - s)
                reuse(act, s_pos, b)
                act.wait_ge(s_away, b + 1)
                act.activation(mask[s], away[s], ACT.Relu, scale=-1.0, bias=k.ones[0:EP, 0:1]).then_inc(s_mask, 1)
            act.wait_ge(s_tab, 3)
            distance(0, 0)
            over_tiles(act, find)

        @block.tensor
        def _(pe):
            pe.wait_ge(s_per, TILES)
            pe.matmul(k.bank[0][:, 0:TILES], k.lower[0:EP, :], per, start=True, stop=True)
            pe.matmul(k.bank[0][:, 64:64 + TILES], k.ones[0:EP, :], per, start=True, stop=True)
            pe.matmul(k.bank[0][0:TILES, 128:129], per, k.ones[0:EP, 0:1], start=True, stop=True).then_inc(s_tot, 1)
            pe.wait_ge(s_tab, 1)
            pe.matmul(k.bank[1][0:TILES, 0:1], k.lower[0:TILES, 0:TILES], colg, start=True, stop=True).then_inc(s_cmp, 1)
            pe.wait_ge(s_tab, 2)
            for h in range(2):
                pe.matmul(k.bank[2 + h][0:1, 0:GH], k.ones[0:TILES, 0:1], behind[:, h * GH:(h + 1) * GH],
                          start=True, stop=True).then_inc(s_look, 1)


class Placing:

    BATCH = 5
    COLS = 25

    def __init__(self, k):
        self.k = k
        B = self.BATCH
        self.hi_lo = k.work[0:EP, TILES * P + 3 * EC:TILES * P + 5 * EC].rearrange("p (a c) -> p a c", a=2)
        self.spot_packed = k.wts[0:EP, 4 * EC:6 * EC].bitcast(I32).rearrange("p (a c) -> p a c", a=2)
        self.few = [k.edge[7][:, 32 * b:32 * b + 2 * B].rearrange("p (a c) -> p a c", a=2) for b in range(2)]
        self.lo_hot = [k.edge[8].bitcast(F16)[:, b * B * P:(b + 1) * B * P].rearrange("p (c n) -> p c n", c=B)
                       for b in range(2)]
        self.hi_hot = [k.small_hot[0:EP, b * B:(b + 1) * B, 0:TILES] for b in range(2)]
        self.fixed = [k.edge[9].bitcast(I32)[:, 64 * b:64 * b + 2 * self.COLS].rearrange("p (a c) -> p a c", a=2)
                      for b in range(2)]
        self.s_few, self.s_hot, self.s_mm, self.s_deg, self.s_fixed, self.s_loaded, self.s_fin = (
            k.sem(f"place_{x}") for x in ("few", "one_hot", "product", "degree", "fixed", "loaded", "finish"))
        self.s_put = [k.sem(f"place_put{b}") for b in range(2)]
        spent = k.keys[0:EP, :].bitcast(F16)
        wide = 930
        self.move = [spent[:, b * B * wide:(b + 1) * B * wide].rearrange("p (c n) -> p c n", c=B) for b in range(2)]
        at = 2 * B * wide
        self.stat = [spent[:, at + b * B * 2 * P:at + (b + 1) * B * 2 * P].rearrange("p (c a n) -> p c a n", c=B, a=2)
                     for b in range(2)]
        self.far = [k.stage[0:EP, b * B * P:(b + 1) * B * P].rearrange("p (c n) -> p c n", c=B) for b in range(2)]
        small = k.wts[0:EP, 7 * EC:7 * EC + 4 * 3 * B]
        few = [small[:, i * 3 * B:(i + 1) * 3 * B].rearrange("p (a c) -> p a c", a=3) for i in range(4)]
        self.few_act, self.few_dve = few[0:2], few[2:4]
        self.s_fa, self.s_fd, self.s_far, self.s_v1, self.s_v2, self.s_slots = (
            k.sem(f"product_{x}") for x in ("few_scalar", "few_vector", "far", "high", "low_and_chunk", "slots"))

    def high(self, act):
        k, B = self.k, self.BATCH

        def batch(n, s, last):
            reuse(act, self.s_slots, n)
            act.sem_inc(k.s_tick, 1)
            act.activation(self.few_act[s], k.for_act[:, :, bass.ds(n * B, B)], ACT.Copy).then_inc(self.s_fa, 1)
            act.wait_ge(self.s_fa, n + 1)
            for c in range(B):
                ins = act.activation(self.far[s][:, c, :], k.iota16[0:EP, 0:P], ACT.Abs, bias=self.few_act[s][:, 0, c:c + 1])
            ins.then_inc(self.s_far, 1)
            act.wait_ge(self.s_far, n + 1)
            for c in range(B):
                ins = act.activation(self.stat[s][:, c, 0, :], self.far[s][:, c, :], ACT.Relu,
                                     scale=self.few_act[s][:, 1, c:c + 1], bias=self.few_act[s][:, 2, c:c + 1])
            ins.then_inc(self.s_v1, 1)
        self.over(act, BY_PRODUCT // B, batch)

    def low_and_chunk(self, dve):
        k, B = self.k, self.BATCH

        def batch(n, s, last):
            reuse(dve, self.s_slots, n)
            dve.sem_inc(k.s_tick, 1)
            dve.tensor_copy(self.few_dve[s], k.for_dve[:, :, bass.ds(n * B, B)]).then_inc(self.s_fd, 1)
            dve.wait_ge(self.s_fd, n + 1)
            for c in range(B):
                part_c, v2_c, chunk_c = (self.few_dve[s][:, a, c:c + 1] for a in range(3))
                dve.tensor_scalar(self.stat[s][:, c, 1, :], k.iota16[0:EP, 0:P], part_c, v2_c, ALU.is_equal, ALU.mult)
                ins = dve.tensor_scalar(self.move[s][:, c, 0:SLOTS], k.iota16[0:EP, :], chunk_c, None, ALU.is_equal)
            ins.then_inc(self.s_v2, 1)
        self.over(dve, BY_PRODUCT // B, batch)

    def slot_products(self, pe):
        def batch(n, s, last):
            pe.wait_ge(self.s_v1, n + 1)
            pe.wait_ge(self.s_v2, n + 1)
            for c in range(self.BATCH):
                start, stop = isinstance(n, int) and n == 0 and c == 0, last and c == self.BATCH - 1
                for v in range(2):
                    for h in range(2):
                        mm = pe.matmul(self.k.bank[2 * v + h][:, 0:HALF], self.stat[s][:, c, v, :],
                                       self.move[s][:, c, h * HALF:(h + 1) * HALF], start=start, stop=stop)
            mm.then_inc(self.s_slots, 1)
        self.over(pe, BY_PRODUCT // self.BATCH, batch)

    def over(self, eng, n, body):
        body(0, 0, False)
        body(1, 1, False)
        odd = n % 2
        with eng.Fori(1, n // 2 - (0 if odd else 1)) as i:
            body(2 * i, 0, False)
            body(2 * i + 1, 1, False)
        if odd:
            body(n - 1, 0, True)
        else:
            body(n - 2, 0, False)
            body(n - 1, 1, True)

    def scatter(self, pool):
        k, C = self.k, self.COLS

        def batch(n, s, last):
            if not isinstance(n, int) or n >= 2:
                pool.wait_ge(self.s_put[s], 16 * C * (n // 2) if isinstance(n, int) else 8 * C * (n - s))
            pool.sem_inc(k.s_tick, 1)
            pool.tensor_copy(self.fixed[s], self.spot_packed[:, :, bass.ds(n * C, C)]).then_inc(self.s_fixed, 1)
            pool.wait_ge(self.s_fixed, n + 1)
            pool.sem_inc(k.s_tick, 1)
            for c in range(C):
                pool.indirect_dma_start(
                    out=k.slots[:, :], in_=self.fixed[s][:, 1, c:c + 1], in_offset=None,
                    out_offset=bass.IndirectOffsetOnAxis(ap=self.fixed[s][:, 0, c:c + 1].bitcast(U32), axis=0),
                    bounds_check=SLOTS * P - 1, oob_is_err=False).then_inc(self.s_put[s], 16)
        self.over(pool, (EC - BY_PRODUCT) // C, batch)

    def load(self, sp):
        n = (EC - BY_PRODUCT) // self.COLS
        for s in range(2):
            sp.wait_ge(self.s_put[s], 16 * self.COLS * ((n + 1 - s) // 2))
        sp.wait_ge(self.s_v1, BY_PRODUCT // self.BATCH)
        sp.dma_start(self.k.slot_dst[:, :].bitcast(I32), self.k.slots.rearrange("(p c) a -> p (c a)", p=P)
                     ).then_inc(self.s_loaded, 16)

    def degree_hots(self, dve):
        row = self.k.iota16[0:EP, 0:P]

        def batch(n, s, last):
            B = self.BATCH
            reuse(dve, self.s_mm, n)
            dve.sem_inc(self.k.s_tick, 1)
            dve.tensor_copy(self.few[s], self.hi_lo[:, :, bass.ds(n * B, B)]).then_inc(self.s_few, 1)
            dve.wait_ge(self.s_few, n + 1)
            for c in range(B):
                dve.tensor_scalar(self.lo_hot[s][:, c, :], row, self.few[s][:, 1, c:c + 1], None, ALU.is_equal)
            tiles = self.few[s][:, 0, :].rearrange("p (c a) -> p c a", a=1).to_broadcast([EP, B, TILES])
            columns = row[:, 0:TILES].rearrange("p (a n) -> p a n", a=1).to_broadcast([EP, B, TILES])
            dve.tensor_tensor(self.hi_hot[s], columns, tiles, ALU.is_equal).then_inc(self.s_hot, 1)
        self.over(dve, EC // self.BATCH, batch)

    def degree_products(self, pe):
        def batch(n, s, last):
            pe.wait_ge(self.s_hot, n + 1)
            for c in range(self.BATCH):
                mm = pe.matmul(self.k.bank[4][:, 0:TILES], self.lo_hot[s][:, c, :], self.hi_hot[s][:, c, :],
                               start=isinstance(n, int) and n == 0 and c == 0, stop=last and c == self.BATCH - 1)
            mm.then_inc(self.s_mm, 1)
        self.over(pe, EC // self.BATCH, batch)

    def root(self, act):
        act.wait_ge(self.s_deg, 1)
        act.activation(self.k.small[:, 1, :], self.k.small[:, 0, :], ACT.Sqrt).then_inc(self.s_deg, 1)

    def finish(self, dve):
        k, n = self.k, [0]

        def link(ins):
            n[0] += 1
            ins.then_inc(self.s_fin, 1)
            dve.wait_ge(self.s_fin, n[0])
        dve.wait_ge(self.s_mm, EC // self.BATCH)
        dve.tensor_scalar(k.small[:, 0, :], k.bank[4][:, 0:TILES], 1.0, None, ALU.add).then_inc(self.s_deg, 1)
        dve.wait_ge(self.s_deg, 2)
        link(dve.reciprocal(k.dinv[:, :], k.small[:, 1, :]))
        slot, low = k.slot_dst[:, :].bitcast(I32), k.keys[:, 0:SLOTS].bitcast(I32)
        value = k.keys[:, SLOTS:2 * SLOTS]
        dve.wait_ge(self.s_slots, BY_PRODUCT // self.BATCH)
        for h in range(2):
            link(dve.tensor_scalar(value[:, h * HALF:(h + 1) * HALF], k.bank[h][:, 0:HALF], 1024.0, None, ALU.mult))
            link(dve.tensor_tensor(value[:, h * HALF:(h + 1) * HALF], value[:, h * HALF:(h + 1) * HALF],
                                   k.bank[2 + h][:, 0:HALF], ALU.add))
        dve.wait_ge(self.s_loaded, 16)
        link(dve.tensor_copy(low.bitcast(F32), slot))
        link(dve.tensor_tensor(value, value, low.bitcast(F32), ALU.add))
        link(dve.tensor_copy(slot, value))
        link(dve.tensor_scalar(low, slot, 255, None, ALU.bitwise_and))
        link(dve.tensor_copy(k.slot_row[:, :], low))
        link(dve.tensor_scalar(k.slot_row[:, :], k.slot_row[:, :], -1.0, None, ALU.add))
        link(dve.tensor_scalar(slot, slot, 8, None, ALU.logical_shift_right))


def scale_input(k, a):
    nc, sem = k.nc, k.sem
    s_scaled, s_written, s_loaded = sem("scaled"), sem("scaled_written"), sem("gnn_weights_loaded")
    with nc.Block() as block:
        @block.vector
        def _(dve):
            with dve.Fori(0, TILES // 7) as q:
                for i in range(7):
                    t = bass.ds(q * 7 + i, 1)
                    dve.tensor_scalar(k.acc[:, t, 0:D], k.acc[:, t, 0:D], k.dinv[:, t], None, ALU.mult
                                      ).then_inc(s_scaled, 1)

        @block.sync
        def _(sp):
            for to, name in ((k.W1, "L0_gnn_W1"), (k.Wfc, "L0_gnn_Wfc"), (k.W2, "L0_gnn_W2"), (k.W3, "L0_gnn_W3")):
                sp.dma_start(to, a[name].rearrange("(k p) n -> p k n", p=P)).then_inc(s_loaded, 16)
            sp.wait_ge(s_scaled, TILES)
            sp.dma_start(k.feats[0].rearrange("(t p) d -> p t d", p=P), k.acc[:, :, 0:D]).then_inc(s_written, 16)
            sp.wait_ge(s_written, 16)
            sp.wait_ge(s_loaded, 64)


class Update:

    def __init__(self, k, layer, depth, place, banks):
        self.k, self.layer, self.depth = k, layer, depth

        def parts(at, width):
            return [place[:, at + i * width:at + (i + 1) * width] for i in range(depth)]
        self.v, self.vT = parts(0, D), parts(depth * D, D)
        self.z, self.zT = parts(2 * depth * D, H), parts(depth * (2 * D + H), H)
        self.res = self.v
        self.A, self.B, self.C, self.E = (banks[i * depth:(i + 1) * depth] for i in range(4))
        self.W, self.width = (k.W2, k.W3, k.Wfc)[layer], (H, H, D)[layer]
        sems = k.upd[layer]
        (self.s_v, self.s_t1, self.s_k1, self.s_m1, self.s_z, self.s_r, self.s_t, self.s_k, self.s_m, self.s_done,
         self.s_stored) = sems[0:11]
        self.s_res = sems[11:13]

    def reuse(self, eng, sem, t):
        reuse(eng, sem, t, self.depth)

    def scale(self, dve, t, s):
        self.reuse(dve, self.s_t1, t)
        dve.tensor_scalar(self.v[s], self.k.acc[:, bass.ds(t, 1), 0:D].rearrange("p a n -> p (a n)"),
                          self.k.dinv[:, bass.ds(t, 1)], None, ALU.mult).then_inc(self.s_v, 1)

    def bias(self, dve, t, s):
        self.reuse(dve, self.s_t, t)
        if self.layer == 0:
            dve.wait_ge(self.s_m1, t + 1)
            dve.tensor_tensor(self.z[s], self.B[s][:, :], self.k.bias[0][:, :], ALU.add).then_inc(self.s_z, 1)
        else:
            dve.scalar_tensor_tensor(out=self.z[s], in0=self.k.acc[:, bass.ds(t, 1), :].rearrange("p a n -> p (a n)"),
                                     scalar=self.k.dinv[:, bass.ds(t, 1)], in1=self.k.bias[self.layer][:, :],
                                     op0=ALU.mult, op1=ALU.add).then_inc(self.s_z, 1)

    def finish(self, dve, t, s):
        one = self.k.acc[:, bass.ds(t, 1), 0:self.width].rearrange("p a n -> p (a n)")
        if self.layer < 2:
            dve.wait_ge(self.s_m, t + 1)
            dve.tensor_scalar(one, self.E[s][:, :], self.k.dinv[:, bass.ds(t, 1)], None, ALU.mult
                              ).then_inc(self.s_done, 1)
        else:
            dve.wait_ge(self.s_res[s], self.loads(t, s))
            dve.wait_ge(self.s_m, t + 1)
            dve.tensor_tensor(one, self.E[s][:, 0:D], self.res[s], ALU.add).then_inc(self.s_done, 1)

    def keep1(self, act, t, s):
        self.reuse(act, self.s_m1, t)
        act.wait_ge(self.s_t1, t + 1)
        act.activation(self.vT[s], self.A[s][:, 0:D], ACT.Copy).then_inc(self.s_k1, 1)

    def relu(self, act, t, s):
        act.wait_ge(self.s_z, t + 1)
        act.activation(self.z[s], self.z[s], ACT.Relu).then_inc(self.s_r, 1)

    def keep(self, act, t, s):
        self.reuse(act, self.s_m, t)
        act.wait_ge(self.s_t, t + 1)
        act.activation(self.zT[s], self.C[s][:, :], ACT.Copy).then_inc(self.s_k, 1)

    def turn1(self, pe, t, s):
        pe.wait_ge(self.s_v, t + 1)
        self.reuse(pe, self.s_k1, t)
        for c in range(KD):
            mm = pe.transpose(self.A[s][:, c * P:(c + 1) * P], self.v[s][:, c * P:(c + 1) * P], self.k.ident[:, :])
        mm.then_inc(self.s_t1, 1)

    def lift(self, pe, t, s):
        pe.wait_ge(self.s_k1, t + 1)
        self.reuse(pe, self.s_z, t)
        for c in range(KD):
            mm = pe.matmul(self.B[s][:, :], self.vT[s][:, c * P:(c + 1) * P], self.k.W1[:, c, :],
                           start=c == 0, stop=c == KD - 1)
        mm.then_inc(self.s_m1, 1)

    def turn(self, pe, t, s):
        pe.wait_ge(self.s_r, t + 1)
        self.reuse(pe, self.s_k, t)
        for c in range(KH):
            mm = pe.transpose(self.C[s][:, c * P:(c + 1) * P], self.z[s][:, c * P:(c + 1) * P], self.k.ident[:, :])
        mm.then_inc(self.s_t, 1)

    def product(self, pe, t, s):
        pe.wait_ge(self.s_k, t + 1)
        self.reuse(pe, self.s_done, t)
        for c in range(KH):
            mm = pe.matmul(self.E[s][:, 0:self.width], self.zT[s][:, c * P:(c + 1) * P], self.W[:, c, :],
                           start=c == 0, stop=c == KH - 1)
        mm.then_inc(self.s_m, 1)

    def store(self, sp, t):
        sp.wait_ge(self.s_done, t + 1)
        sp.dma_start(self.k.feats[self.layer + 1][bass.ds(t * P, P), :],
                     self.k.acc[:, bass.ds(t, 1), :].rearrange("p a n -> p (a n)")).then_inc(self.s_stored, 16)

    def fetch(self, sp, t, s):
        self.reuse(sp, self.s_done, t)
        sp.dma_start(self.res[s], self.k.resid[bass.ds(t * P, P), :]).then_inc(self.s_res[s], 16)

    def loads(self, t, s):
        if self.depth == 1:
            return 16 * (t + 1)
        return 16 * (t // 2 + 1) if isinstance(t, int) else 8 * (t - s) + 16


def more(t):
    return not isinstance(t, int) or t < TILES - 1


def evenly(k, eng):
    return eng.value_load(k.even[0:1, 0:1], min_val=0, max_val=1)


def update(k, layer):
    u = Update(k, layer, 2, k.work, k.bank)
    with k.nc.Block() as block:
        @block.vector
        def _(dve):
            with dve.If(evenly(k, dve) == 0):
                if layer == 0:
                    u.scale(dve, 0, 0)
                else:
                    u.bias(dve, 0, 0)

                def step(t, s):
                    if layer == 0:
                        if more(t):
                            u.scale(dve, t + 1, 1 - s)
                        u.bias(dve, t, s)
                    elif more(t):
                        u.bias(dve, t + 1, 1 - s)
                    u.finish(dve, t, s)
                over_tiles(dve, step)
                dve.wait_ge(u.s_done, TILES)
                dve.sem_inc(k.s_tick, 1)

        @block.scalar
        def _(act):
            with act.If(evenly(k, act) == 0):
                def step(t, s):
                    if layer == 0:
                        u.keep1(act, t, s)
                    u.relu(act, t, s)
                    u.keep(act, t, s)
                over_tiles(act, step)
                act.sem_inc(k.s_tick, 1)

        @block.tensor
        def _(pe):
            with pe.If(evenly(k, pe) == 0):
                if layer == 0:
                    u.turn1(pe, 0, 0)
                    u.lift(pe, 0, 0)
                else:
                    u.turn(pe, 0, 0)

                def step(t, s):
                    if layer == 0:
                        if more(t):
                            u.turn1(pe, t + 1, 1 - s)
                        u.turn(pe, t, s)
                        if more(t):
                            u.lift(pe, t + 1, 1 - s)
                    elif more(t):
                        u.turn(pe, t + 1, 1 - s)
                    u.product(pe, t, s)
                over_tiles(pe, step)
                pe.sem_inc(k.s_tick, 1)

        @block.sync
        def _(sp):
            with sp.If(evenly(k, sp) == 0):
                if layer < 2:
                    over_tiles(sp, lambda t, s: u.store(sp, t))
                    sp.wait_ge(u.s_stored, 16 * TILES)
                else:
                    over_tiles(sp, lambda t, s: u.fetch(sp, t, s))
                    for s in range(2):
                        sp.wait_ge(u.s_res[s], u.loads(TILES - 1 - s, s))
                sp.sem_inc(k.s_tick, 1)


def aggregate(k, layer, width):
    nc = k.nc
    feats = k.feats[layer]
    ring = k.work[:, 0:RING * H].rearrange("p (s n) -> p s n", s=RING)
    hot = k.work[:, RING * H:RING * (H + P)].rearrange("p (s n) -> p s n", s=RING)
    s_index, s_hot, s_sum, s_add = k.agg
    s_got = k.agg_got
    BANKS = 4
    LEAD = 3
    half = RING // 2
    u = Update(k, layer, 1, k.stage, k.bank[BANKS:])
    pe_does = {0: u.turn1, 2: u.lift, 4: u.turn, 6: u.product} if layer == 0 else {1: u.turn, 4: u.product}
    dve_does = {3: u.bias, 7: u.finish} if layer == 0 else {5: u.finish}

    class Course:

        def __init__(self, even):
            self.even, self.steps = even, STEPS_EVEN if even else STEPS
            self.groups = self.steps * UNROLL
            self.I0, self.G0 = layer * self.steps, layer * self.groups

        def over(self, eng, step):
            step(0, None)
            if self.even:
                with eng.Fori(1, LAG) as i:
                    step(i, None)
                step(LAG, 0)
                with eng.Fori(LAG + 1, self.steps - 1) as i:
                    step(i, i - LAG)
                step(self.steps - 1, self.steps - 1 - LAG)
            else:
                with eng.Fori(1, self.steps - 1) as i:
                    step(i, None)
                step(self.steps - 1, None)

    with nc.Block() as block:
        @block.gpsimd
        def _(pool):
            def gather_all(c):
                def index(i, p, h):
                    return k.index[:, p * RING + h * half:p * RING + (h + 1) * half]

                def copy(i, p, h):
                    pool.sem_inc(k.s_tick, 1)
                    pool.tensor_copy(index(i, p, h), k.slot_dst[:, bass.ds(i * RING + h * half, half)]
                                     ).then_inc(s_index, 1)

                def step(i, p):
                    for h in range(2):
                        if h == 0:
                            copy(i, p, 1)
                        elif not isinstance(i, int) or i < c.steps - 1:
                            copy(i + 1, 1 - p, 0)
                        if not isinstance(i, int) or i > 0:
                            pool.wait_ge(s_sum, c.G0 + (i - 1) * UNROLL + (h + 1) * (UNROLL // 2))
                        pool.wait_ge(s_index, 2 * c.I0 + 2 * i + h + 1)
                        pool.sem_inc(k.s_tick, 1)
                        for j in range(half):
                            s = h * half + j
                            pool.indirect_dma_start(
                                out=ring[:, s, 0:width], out_offset=None, in_=feats[:, :],
                                in_offset=bass.IndirectOffsetOnAxis(ap=index(i, p, h)[:, j:j + 1], axis=0),
                                bounds_check=TILES * P - 1, oob_is_err=False).then_inc(s_got[s], 16)
                copy(0, 0, 0)
                step(0, 0)
                step(1, 1)
                with pool.Fori(1, c.steps // 2 - 1) as i:
                    step(2 * i, 0)
                    step(2 * i + 1, 1)
                step(c.steps - 2, 0)
                step(c.steps - 1, 1)
                pool.sem_inc(k.s_tick, 1)
            with pool.If(evenly(k, pool) == 1):
                gather_all(Course(True))
            with pool.Else():
                gather_all(Course(False))

        @block.vector
        def _(dve):
            def sum_all(c):
                def one_hot(g, j):
                    if not isinstance(g, int) or g >= UNROLL:
                        dve.wait_ge(s_sum, c.G0 + g - UNROLL + 1)
                    for b in range(GRP):
                        s = j * GRP + b
                        ins = dve.tensor_scalar(hot[:, s, :], k.iota[:, :], k.slot_row[:, bass.ds(g * GRP + b, 1)],
                                                None, ALU.is_equal)
                    ins.then_inc(s_hot, 1)

                def tile_of(g):
                    return dve.value_load(k.table[0:1, bass.ds(g, 1)], min_val=0, max_val=TILES - 1)

                def add(g, j, t):
                    if not isinstance(g, int) or g > 0:
                        dve.wait_ge(s_add, c.G0 + g)
                    dve.wait_ge(s_sum, c.G0 + g + 1)
                    dve.tensor_tensor(k.acc[:, bass.ds(t, 1), 0:width], k.acc[:, bass.ds(t, 1), 0:width],
                                      k.bank[j % BANKS][:, 0:width].rearrange("p (a n) -> p a n", a=1),
                                      ALU.add).then_inc(s_add, 1)

                def step(i, tile):
                    if tile is not None:
                        dve.wait_ge(s_add, c.G0 + i * UNROLL)
                        (u.scale if layer == 0 else u.bias)(dve, tile, 0)
                    for j in range(UNROLL):
                        g = i * UNROLL + j
                        t = tile_of(g)
                        if not (isinstance(i, int) and g + LEAD >= c.groups):
                            one_hot(g + LEAD, (j + LEAD) % UNROLL)
                        if tile is not None and j in dve_does:
                            dve_does[j](dve, tile, 0)
                        add(g, j, t)

                for g in range(LEAD):
                    one_hot(g, g)
                c.over(dve, step)
                if c.even:
                    dve.wait_ge(s_add, c.G0 + c.groups)
                    if layer == 0:
                        u.scale(dve, TILES - 1, 0)
                    u.bias(dve, TILES - 1, 0)
                    u.finish(dve, TILES - 1, 0)
                    dve.wait_ge(u.s_done, TILES)
                dve.sem_inc(k.s_tick, 1)
            with dve.If(evenly(k, dve) == 1):
                sum_all(Course(True))
            with dve.Else():
                sum_all(Course(False))

        @block.tensor
        def _(pe):
            def multiply_all(c):
                def step(i, tile):
                    for j in range(UNROLL):
                        g = i * UNROLL + j
                        pe.wait_ge(s_hot, c.G0 + g + 1)
                        if not isinstance(i, int) or g >= BANKS:
                            pe.wait_ge(s_add, c.G0 + g - BANKS + 1)
                        for b in range(GRP):
                            s = j * GRP + b
                            pe.wait_ge(s_got[s], 16 * (c.I0 + i + 1))
                            mm = pe.matmul(k.bank[j % BANKS][:, 0:width], hot[:, s, :], ring[:, s, 0:width],
                                           start=b == 0, stop=b == GRP - 1)
                        mm.then_inc(s_sum, 1)
                        if tile is not None and j in pe_does:
                            pe_does[j](pe, tile, 0)
                c.over(pe, step)
                if c.even:
                    for j in sorted(pe_does):
                        pe_does[j](pe, TILES - 1, 0)
                pe.sem_inc(k.s_tick, 1)
            with pe.If(evenly(k, pe) == 1):
                multiply_all(Course(True))
            with pe.Else():
                multiply_all(Course(False))

        @block.scalar
        def _(act):
            with act.If(evenly(k, act) == 1):
                def step(t):
                    if layer == 0:
                        u.keep1(act, t, 0)
                    u.relu(act, t, 0)
                    u.keep(act, t, 0)
                step(0)
                with act.Fori(1, TILES) as t:
                    step(t)
                act.sem_inc(k.s_tick, 1)

        @block.sync
        def _(sp):
            with sp.If(evenly(k, sp) == 1):
                if layer < 2:
                    with sp.Fori(0, TILES) as t:
                        u.store(sp, t)
                    sp.wait_ge(u.s_stored, 16 * TILES)
                else:
                    u.fetch(sp, 0, 0)
                    with sp.Fori(1, TILES) as t:
                        u.fetch(sp, t, 0)
                    sp.wait_ge(u.s_res[0], 16 * TILES)
                sp.sem_inc(k.s_tick, 1)


def logits(k, a):
    nc, sem = k.nc, k.sem
    y = [k.wts[:, i * H:(i + 1) * H] for i in range(4)]
    yT = [k.wts[:, 2048 + i * H:2048 + (i + 1) * H] for i in range(4)]
    s_g, s_b, s_t, s_k, s_l, s_lb = (sem(f"logits_{x}") for x in ("scaled", "y", "turned", "kept", "product", "biased"))
    s_y = k.rows_moved
    PAIRS = TILES // 2

    def over_pairs(eng, body):
        for s in range(4):
            body(s, s, 2)
        with eng.Fori(1, PAIRS // 4) as j:
            for s in range(4):
                body(4 * j + s, s, 2)
        body(PAIRS, PAIRS % 4, 1)

    def rows(x, tiles):
        return x[:, :].rearrange("p (a n) -> p a n", a=1).to_broadcast([P, tiles, x.shape[1]])

    with nc.Block() as block:
        @block.vector
        def _(dve):
            def scale(i, tiles):
                part = k.acc[:, bass.ds(2 * i, tiles), D:2 * D]
                dve.tensor_tensor(part, part, rows(k.gamma, tiles), ALU.mult).then_inc(s_g, 1)

            def add(i, s, tiles):
                if not isinstance(i, int) or i < PAIRS - 1:
                    scale(i + 1, 2)
                reuse(dve, s_t, i, 4)
                if not isinstance(i, int) or i >= 4:
                    dve.wait_ge(s_y[s], 16 * (i // 4) if isinstance(i, int) else 4 * (i - s))
                dve.wait_ge(s_g, i + 1)
                dve.tensor_tensor(y[s][:, 0:tiles * D].rearrange("p (a n) -> p a n", n=D),
                                  k.acc[:, bass.ds(2 * i, tiles), D:2 * D], rows(k.beta, tiles),
                                  ALU.add).then_inc(s_b, 1)
                if not isinstance(i, int) or i >= 2:
                    bias(i - 2, (s + 2) % 4, 2)

            def bias(i, s, tiles):
                dve.wait_ge(s_l, i + 1)
                dve.tensor_tensor(k.logits[:, bass.ds(2 * i, tiles), :],
                                  k.bank[4 + s][:, 0:tiles * EXPERTS].rearrange("p (a e) -> p a e", e=EXPERTS),
                                  rows(k.br, tiles), ALU.add).then_inc(s_lb, 1)
            scale(0, 2)
            for s in range(4):
                add(s, s, 2)
            with dve.Fori(1, PAIRS // 4 - 1) as j:
                for s in range(4):
                    add(4 * j + s, s, 2)
            for i in range(PAIRS - 4, PAIRS):
                add(i, i % 4, 2)
            scale(PAIRS, 1)
            add(PAIRS, PAIRS % 4, 1)
            bias(PAIRS - 1, (PAIRS - 1) % 4, 2)
            bias(PAIRS, PAIRS % 4, 1)
            dve.wait_ge(s_lb, PAIRS + 1)

        @block.tensor
        def _(pe):
            def turn(i, s, tiles):
                pe.wait_ge(s_b, i + 1)
                reuse(pe, s_k, i, 4)
                for c in range(KD * tiles):
                    mm = pe.transpose(k.bank[s][:, c * P:(c + 1) * P], y[s][:, c * P:(c + 1) * P], k.ident[:, :])
                mm.then_inc(s_t, 1)

            def product(i, s, tiles):
                pe.wait_ge(s_k, i + 1)
                reuse(pe, s_lb, i, 4)
                for t in range(tiles):
                    for c in range(KD):
                        b = (KD * t + c) * P
                        mm = pe.matmul(k.bank[4 + s][:, t * EXPERTS:(t + 1) * EXPERTS], yT[s][:, b:b + P], k.Wr[:, c, :],
                                       start=c == 0, stop=c == KD - 1)
                mm.then_inc(s_l, 1)

            def step(i, s, tiles):
                if not isinstance(i, int) or i > 0:
                    turn(i, s, tiles)
                    product(i - 1, (s + 3) % 4, 2)
                else:
                    turn(i, s, tiles)
            over_pairs(pe, step)
            product(PAIRS, PAIRS % 4, 1)

        @block.scalar
        def _(act):
            def keep(i, s, tiles):
                reuse(act, s_l, i, 4)
                act.wait_ge(s_t, i + 1)
                act.activation(yT[s][:, 0:tiles * D], k.bank[s][:, 0:tiles * D], ACT.Copy).then_inc(s_k, 1)
            over_pairs(act, keep)

        @block.sync
        def _(sp):
            s_w2 = sem("expert_W2_loaded")
            sp.dma_start(k.eW2, a["L0_ffn_W2"].rearrange("e (c p) n -> p (e c) n", p=P)).then_inc(s_w2, 16)

            def store(i, s, tiles):
                sp.wait_ge(s_b, i + 1)
                sp.dma_start(k.y_rows[bass.ds(2 * i * P, tiles * P), :].rearrange("(a p) n -> p a n", p=P),
                             y[s][:, 0:tiles * D].rearrange("p (a n) -> p a n", n=D)).then_inc(s_y[s], 16)
            over_pairs(sp, store)
            for s in range(4):
                sp.wait_ge(s_y[s], 16 * (PAIRS // 4 + (1 if s == PAIRS % 4 else 0)))
            sp.wait_ge(s_w2, 16)


def choose(k, a):
    nc, sem = k.nc, k.sem
    NE = TILES * EXPERTS

    def spot(i):
        return k.work[:, EW + i * 400:EW + i * 400 + NE]
    best, whichf, one, two, rank = (spot(i).rearrange("p (t e) -> p t e", e=EXPERTS) for i in (1, 3, 4, 5, 6))
    which = spot(2).bitcast(U32).rearrange("p (t e) -> p t e", e=EXPERTS)
    pos = k.stats[:, :, :].rearrange("p t e -> p (t e)")[:, 0:2 * TILES].rearrange("p (c t) -> p c t", c=2)
    ints = k.stats[:, :, :].rearrange("p t e -> p (t e)")[:, 2 * TILES:4 * TILES].rearrange("p (c t) -> p c t", c=2).bitcast(I32)
    part, chunk, value = (k.slot_row[:, 200 + 100 * i:200 + 100 * i + 2 * TILES].rearrange("p (c t) -> p c t", c=2)
                          for i in range(3))
    cols = k.slot_row[:, 600:680].rearrange("p (i e) -> p i e", e=EXPERTS)
    total, counti, tiles_e, ends, start, zero = (cols[:, i, :] for i in range(6))
    tab, tmp, zrow = k.slot_row[:, 0:ETILES], k.slot_row[:, 720:720 + ETILES], k.rstd[:, :]
    w1, w2, dif = (k.small[:, i, :] for i in range(3))
    stat = [k.stage[:, i * 256:(i + 1) * 256].rearrange("p (c n) -> p c n", c=2) for i in range(2)]
    move = [k.stage[:, 512 + i * 256:512 + (i + 1) * 256].rearrange("p (c n) -> p c n", c=2) for i in range(2)]
    s_best, s_link, s_exp, s_val, s_tot, s_sums, s_hot, s_mm = (sem(f"choose_{x}") for x in (
        "best", "chain", "exp", "values", "totals", "sums", "one_hot", "placed"))
    s_w = sem("expert_weights_loaded")
    with nc.Block() as block:
        @block.sync
        def _(sp):
            first = a["L0_ffn_W1"].rearrange("e (c p) n -> p (e c) n", p=P)
            for q in range(4):
                for h in range(2):
                    sp.dma_start(k.acc[:, 8 * q + h:8 * q + 8:2, D:2 * D],
                                 first[:, 4 * q:4 * q + 4, h * D:(h + 1) * D]).then_inc(s_w, 16)
            sp.wait_ge(s_w, 16 * (8 + 2 * EXPERTS))

        @block.scalar
        def _(act):
            for e in range(EXPERTS):
                for to, name, n in ((k.eb1, "L0_ffn_b1", H), (k.eb2, "L0_ffn_b2", D)):
                    act.dma_start(to[:, e, :], a[name][e].rearrange("(a n) -> a n", a=1).to_broadcast([P, n])
                                  ).then_inc(s_w, 16)
            act.wait_ge(s_link, 1)
            act.activation(dif, dif, ACT.Exp).then_inc(s_exp, 1)

        @block.gpsimd
        def _(pool):
            for c in range(2):
                pool.iota(value[:, c, :], pattern=[[2 * P, TILES]], base=c + 1, channel_multiplier=2,
                          allow_small_or_imprecise_dtypes=True).then_inc(s_val, 1)

        @block.vector
        def _(dve):
            for t in range(TILES):
                dve.max(best[:, t, :], k.logits[:, t, :]).then_inc(s_best, 1)
            dve.wait_ge(s_best, TILES)
            n = [0]

            def link(ins):
                n[0] += 1
                ins.then_inc(s_link, 1)
                dve.wait_ge(s_link, n[0])
            link(dve.tensor_tensor(dif, best[:, :, 1], best[:, :, 0], ALU.subtract))
            for t in range(TILES):
                dve.max_index(which[:, t, :], best[:, t, :], k.logits[:, t, :]).then_inc(s_best, 1)
            dve.wait_ge(s_exp, 1)
            link(dve.tensor_scalar(w2, dif, 1.0, None, ALU.add))
            link(dve.reciprocal(w1, w2))
            link(dve.tensor_tensor(w2, dif, w1, ALU.mult))
            dve.wait_ge(s_best, 2 * TILES)
            link(dve.tensor_copy(whichf, which))
            numbers = k.iota[:, 0:EXPERTS].rearrange("p (a e) -> p a e", a=1).to_broadcast([P, TILES, EXPERTS])
            for i, to in enumerate((one, two)):
                dve.tensor_tensor(to, numbers, whichf[:, :, i:i + 1].to_broadcast([P, TILES, EXPERTS]),
                                  ALU.is_equal).then_inc(s_best, 1)
            dve.wait_ge(s_best, 2 * TILES + 2)
            both = whichf
            link(dve.tensor_tensor(both, one, two, ALU.add))
            link(dve.tensor_reduce(total, both.rearrange("p t e -> p e t"), AX.X, ALU.add))
            dve.memset(zero, 0.0)
            dve.memset(tab, 0.0)
            dve.memset(zrow, 0.0).then_inc(s_tot, 1)
            dve.wait_ge(s_sums, 1)
            link(dve.tensor_scalar(counti.bitcast(I32), k.bank[1][:, 0:EXPERTS], P - 1.0, None, ALU.add))
            link(dve.tensor_scalar(counti.bitcast(I32), counti.bitcast(I32), SHIFT, None, ALU.logical_shift_right))
            link(dve.tensor_copy(tiles_e, counti.bitcast(I32)))
            link(dve.tensor_tensor_scan(ends, tiles_e, zero, 0.0, ALU.add, ALU.add))
            link(dve.tensor_tensor(start, ends, tiles_e, ALU.subtract))
            link(dve.tensor_scalar(start, start, float(P), -1.0, ALU.mult, ALU.add))
            link(dve.tensor_tensor(start, start, k.bank[0][:, 0:EXPERTS], ALU.add))
            for e in range(EXPERTS):
                ins = dve.tensor_tensor_scan(rank[:, :, e], both[:, :, e], zrow, start[:, e:e + 1], ALU.add, ALU.add)
            link(ins)
            for c, hot in enumerate((one, two)):
                ins = dve.tensor_tensor(hot, hot, rank, ALU.mult)
            link(ins)
            for c, hot in enumerate((one, two)):
                ins = dve.tensor_reduce(pos[:, c, :], hot, AX.X, ALU.add)
            link(ins)
            link(dve.tensor_copy(ints, pos))
            link(dve.tensor_scalar(pos.bitcast(I32), ints, P - 1, None, ALU.bitwise_and))
            link(dve.tensor_copy(part, pos.bitcast(I32)))
            link(dve.tensor_scalar(pos.bitcast(I32), ints, SHIFT, None, ALU.logical_shift_right))
            link(dve.tensor_copy(chunk, pos.bitcast(I32)))
            dve.wait_ge(s_val, 2)

            def hots(t, s):
                reuse(dve, s_mm, t)
                for c in range(2):
                    dve.tensor_scalar(stat[s][:, c, :], k.iota[:, :], part[:, c, bass.ds(t, 1)],
                                      value[:, c, bass.ds(t, 1)], ALU.is_equal, ALU.mult)
                    ins = dve.tensor_scalar(move[s][:, c, 0:ETILES], k.iota[:, 0:ETILES], chunk[:, c, bass.ds(t, 1)],
                                            None, ALU.is_equal)
                ins.then_inc(s_hot, 1)
            over_tiles(dve, hots)
            for e in range(EXPERTS):
                link(dve.scalar_tensor_tensor(out=tab, in0=k.iota[:, 0:ETILES], scalar=ends[:, e:e + 1], in1=tab,
                                              op0=ALU.is_ge, op1=ALU.add))
            link(dve.tensor_scalar(tab, tab, EXPERTS - 1.0, None, ALU.min))
            link(dve.tensor_copy(k.tile_expert[:, :], tab[0:1, :]))
            dve.wait_ge(s_mm, TILES)
            link(dve.tensor_scalar(tmp, k.bank[2][:, 0:ETILES], -1.0, 0.0, ALU.add, ALU.max))
            link(dve.tensor_copy(k.slot_node, tmp))
            link(dve.tensor_scalar(k.slot_node, k.slot_node, 1, None, ALU.logical_shift_right))
            link(dve.tensor_scalar(tmp, k.bank[2][:, 0:ETILES], 0.0, 2.0 * NOWHERE, ALU.is_equal, ALU.mult))
            link(dve.tensor_tensor(tmp, tmp, k.bank[2][:, 0:ETILES], ALU.add))
            link(dve.tensor_scalar(tmp, tmp, -1.0, None, ALU.add))
            link(dve.tensor_copy(k.slot_result, tmp))

        @block.tensor
        def _(pe):
            pe.wait_ge(s_tot, 1)
            pe.matmul(k.bank[0][:, 0:EXPERTS], k.lower[:, :], total, start=True, stop=True)
            pe.matmul(k.bank[1][:, 0:EXPERTS], k.ones[:, :], total, start=True, stop=True).then_inc(s_sums, 1)

            def place(t, s):
                pe.wait_ge(s_hot, t + 1)
                for c in range(2):
                    mm = pe.matmul(k.bank[2][:, 0:ETILES], stat[s][:, c, :], move[s][:, c, 0:ETILES],
                                   start=isinstance(t, int) and t == 0 and c == 0,
                                   stop=isinstance(t, int) and t == TILES - 1 and c == 1)
                mm.then_inc(s_mm, 1)
            over_tiles(pe, place)


def experts(k):
    nc, sem = k.nc, k.sem
    R = 3
    y = [k.bias[i][:, 0:D] for i in range(R)]
    out = [k.bias[i][:, D:2 * D] for i in range(R)]
    yT = [k.stage[:, i * D:(i + 1) * D] for i in range(R)]
    h = [k.work[:, EW + i * H:EW + (i + 1) * H] for i in range(R)]
    hT = [k.work[:, EW + (R + i) * H:EW + (R + i + 1) * H] for i in range(R)]
    index = [[k.index[:, c * R + i:c * R + i + 1] for i in range(R)] for c in range(2)]
    B_y, B_yh, B_h, B_o = k.bank[6], k.bank[7], k.bank[0:3], k.bank[3:6]
    s_t1, s_k1, s_m1, s_h, s_g, s_t, s_k, s_m, s_o, s_ix = (sem(f"ffn_{x}") for x in (
        "turned1", "kept1", "product1", "hidden", "active", "turned", "kept", "product2", "result", "index"))
    s_got, s_put = ([sem(f"ffn_{x}{i}") for i in range(R)] for x in ("got", "put"))
    STEPS_E, L = ETILES // R, 5
    assert STEPS_E * R == ETILES

    def over_laps(eng, body):
        def lap(j):
            for s in range(R):
                body(R * j + s, s, j)
        for j in range(L):
            lap(j)
        with eng.Fori(1, (STEPS_E - 1) // L) as q:
            for j in range(L):
                lap(L * q + j)
        for j in range((STEPS_E - 1) // L * L, STEPS_E):
            lap(j)

    def ahead(i, n):
        return not isinstance(i, int) or i + n < ETILES

    with nc.Block() as block:
        @block.gpsimd
        def _(pool):
            def copy(c, i, s):
                of = (k.slot_node, k.slot_result)[c]
                pool.sem_inc(k.s_tick, 1)
                pool.tensor_copy(index[c][s], of[:, bass.ds(i, 1)]).then_inc(s_ix, 1)

            def gather(i, s):
                if not isinstance(i, int) or i >= R:
                    pool.wait_ge(s_t1, i - R + 1)
                copy(0, i, s)
                pool.wait_ge(s_ix, count(i, s))
                pool.sem_inc(k.s_tick, 1)
                pool.indirect_dma_start(
                    out=y[s], out_offset=None, in_=k.y_rows[:, :],
                    in_offset=bass.IndirectOffsetOnAxis(ap=index[0][s], axis=0),
                    bounds_check=TILES * P - 1, oob_is_err=False).then_inc(s_got[s], 16)

            def scatter(i, s, j):
                pool.wait_ge(s_o, i + 1)
                if not isinstance(j, int) or j > 0:
                    pool.wait_ge(s_put[s], 16 * j)
                copy(1, i, s)
                pool.wait_ge(s_ix, count(i, s, True))
                pool.sem_inc(k.s_tick, 1)
                pool.indirect_dma_start(
                    out=k.results[:, :], out_offset=bass.IndirectOffsetOnAxis(ap=index[1][s], axis=0),
                    in_=out[s], in_offset=None, bounds_check=2 * TILES * P - 1, oob_is_err=False
                    ).then_inc(s_put[s], 16)

            def count(i, s, put=False):
                if put:
                    return 2 * i + R + 2 if ahead(i, R) else ETILES + i + 1
                return 2 * i + 1 - R if not isinstance(i, int) or i >= R else i + 1

            for s in range(R):
                gather(s, s)

            def step(i, s, j):
                if ahead(i, R):
                    gather(i + R, s)
                scatter(i, s, j)
            over_laps(pool, step)
            for s in range(R):
                pool.wait_ge(s_put[s], 16 * STEPS_E)

        @block.vector
        def _(dve):
            def keep1(i, s):
                reuse(dve, s_m1, i, R)
                dve.wait_ge(s_t1, i + 1)
                dve.sem_inc(k.s_tick, 1)
                dve.tensor_copy(yT[s], B_y[:, 0:D]).then_inc(s_k1, 1)

            def hidden(i, s, e):
                reuse(dve, s_t, i, R)
                dve.wait_ge(s_m1, i + 1)
                dve.tensor_tensor(h[s].rearrange("p (a n) -> p a n", a=1),
                                  B_h[s][:, :].rearrange("p (a n) -> p a n", a=1), k.eb1[:, bass.ds(e, 1), :],
                                  ALU.add).then_inc(s_h, 1)

            def result(i, s, e, j):
                if not isinstance(j, int) or j > 0:
                    dve.wait_ge(s_put[s], 16 * j)
                dve.wait_ge(s_m, i + 1)
                dve.tensor_tensor(out[s].rearrange("p (a n) -> p a n", a=1),
                                  B_o[s][:, 0:D].rearrange("p (a n) -> p a n", a=1), k.eb2[:, bass.ds(e, 1), :],
                                  ALU.add).then_inc(s_o, 1)

            def expert(i):
                return dve.value_load(k.tile_expert[0:1, bass.ds(i, 1)], min_val=0, max_val=EXPERTS - 1)
            keep1(0, 0)
            keep1(1, 1)
            hidden(0, 0, expert(0))

            def step(i, s, j):
                if ahead(i, 1):
                    hidden(i + 1, (s + 1) % R, expert(i + 1))
                if ahead(i, 2):
                    keep1(i + 2, (s + 2) % R)
                result(i, s, expert(i), j)
            over_laps(dve, step)

        @block.scalar
        def _(act):
            def active(i, s):
                act.wait_ge(s_h, i + 1)
                act.activation(h[s], h[s], ACT.Gelu).then_inc(s_g, 1)

            def keep(i, s):
                reuse(act, s_m, i, R)
                act.wait_ge(s_t, i + 1)
                act.activation(hT[s], B_yh[:, :], ACT.Copy).then_inc(s_k, 1)
            active(0, 0)

            def step(i, s, j):
                keep(i, s)
                if ahead(i, 1):
                    active(i + 1, (s + 1) % R)
            over_laps(act, step)

        @block.tensor
        def _(pe):
            def turn1(i, s, lap):
                pe.wait_ge(s_got[s], lap)
                reuse(pe, s_k1, i, 1)
                for c in range(KD):
                    mm = pe.transpose(B_y[:, c * P:(c + 1) * P], y[s][:, c * P:(c + 1) * P], k.ident[:, :])
                mm.then_inc(s_t1, 1)

            def expert(i):
                return pe.value_load(k.tile_expert[0:1, bass.ds(i, 1)], min_val=0, max_val=EXPERTS - 1)

            def product1(i, s, e):
                pe.wait_ge(s_k1, i + 1)
                reuse(pe, s_h, i, R)
                pe.sem_inc(k.s_tick, 1)
                for c in range(KD):
                    mm = pe.matmul(B_h[s][:, :].rearrange("p (h n) -> p h n", h=2), yT[s][:, c * P:(c + 1) * P],
                                   k.acc[:, bass.ds(e * 4 + 2 * c, 2), D:2 * D], start=c == 0, stop=c == KD - 1)
                mm.then_inc(s_m1, 1)

            def turn(i, s):
                pe.wait_ge(s_g, i + 1)
                reuse(pe, s_k, i, 1)
                for c in range(KH):
                    mm = pe.transpose(B_yh[:, c * P:(c + 1) * P], h[s][:, c * P:(c + 1) * P], k.ident[:, :])
                mm.then_inc(s_t, 1)

            def product2(i, s, e):
                pe.wait_ge(s_k, i + 1)
                reuse(pe, s_o, i, R)
                pe.sem_inc(k.s_tick, 1)
                for c in range(KH):
                    mm = pe.matmul(B_o[s][:, 0:D].rearrange("p (a n) -> p a n", a=1), hT[s][:, c * P:(c + 1) * P],
                                   k.eW2[:, bass.ds(e * KH + c, 1), :], start=c == 0, stop=c == KH - 1)
                mm.then_inc(s_m, 1)
            turn1(0, 0, 16)
            turn1(1, 1, 16)
            product1(0, 0, expert(0))

            def step(i, s, j):
                e = expert(i)
                e_next = expert(i + 1) if ahead(i, 1) else None
                turn(i, s)
                if ahead(i, 1):
                    product1(i + 1, (s + 1) % R, e_next)
                if ahead(i, 2):
                    turn1(i + 2, (s + 2) % R, 16 * (j + (1 if s == 0 else 2)))
                product2(i, s, e)
            over_laps(pe, step)


def combine(k, a):
    nc, sem = k.nc, k.sem
    CT = 7
    N = TILES // CT
    assert N * CT == TILES
    room = [k.work[:, i * CT * 2 * D:(i + 1) * CT * 2 * D] for i in range(3)] + [k.wts[:, 0:CT * 2 * D]]
    room = [r.rearrange("p (t n) -> p t n", n=2 * D) for r in room]
    two = k.results.rearrange("(t p c) n -> p t (c n)", p=P, c=2)
    s_r = k.rows_moved
    stored = [16 * (TILES // 2 // 4 + (1 if s == TILES // 2 % 4 else 0)) for s in range(4)]
    s_first, s_second, s_y = sem("combine_first"), sem("combine_second"), sem("combine_stored")
    with nc.Block() as block:
        @block.sync
        def _(sp):
            for q in range(N):
                if q >= len(room):
                    sp.wait_ge(s_second, (q - len(room) + 1) * CT)
                sp.dma_start(room[q % 4], two[:, q * CT:(q + 1) * CT, :]).then_inc(s_r[q % 4], 16)

        @block.vector
        def _(dve):
            for q in range(N):
                dve.wait_ge(s_r[q % 4], stored[q % 4] + 16 * (q // 4 + 1))
                for c, sem_c in enumerate((s_first, s_second)):
                    if c == 1:
                        dve.wait_ge(s_first, (q + 1) * CT)
                    for t in range(q * CT, (q + 1) * CT):
                        dve.scalar_tensor_tensor(
                            out=k.acc[:, t, 0:D], in0=room[q % 4][:, t - q * CT, c * D:(c + 1) * D],
                            scalar=k.small[:, c, t:t + 1], in1=k.acc[:, t, 0:D], op0=ALU.mult, op1=ALU.add
                            ).then_inc(sem_c, 1)

        @block.scalar
        def _(act):
            for q in range(N):
                act.wait_ge(s_second, (q + 1) * CT)
                full = CT if q < N - 1 else CT - 1
                act.dma_start(a["out"][q * CT * P:(q * CT + full) * P, :].rearrange("(t p) d -> p t d", p=P),
                              k.acc[:, q * CT:q * CT + full, 0:D]).then_inc(s_y, 16)
            act.dma_start(a["out"][(TILES - 1) * P:NODES, :], k.acc[0:LAST, TILES - 1, 0:D]).then_inc(s_y, 16)
            act.wait_ge(s_y, 16 * (N + 1))


def build(nc, a):
    with ExitStack() as ctx:
        k = Core()
        allocate(nc, ctx, k)
        load(k, a)
        norm(k, "norm1", 0, 0)
        rank_edges(k)
        attention(k, a)
        scale_input(k, a)
        for layer, width in enumerate((D, H, H)):
            aggregate(k, layer, width)
            update(k, layer)
        norm(k, "norm2", 0, D)
        norm(k, "norm3", D, D)
        logits(k, a)
        choose(k, a)
        experts(k)
        combine(k, a)


INPUTS = ["x", "src", "dst", "L0_gnn_W1", "L0_gnn_b1", "L0_gnn_W2", "L0_gnn_b2", "L0_gnn_W3", "L0_gnn_b3",
          "L0_gnn_Wfc", "L0_gnn_bfc", "L0_mix_W_qkv", "L0_mix_W_out", "L0_mix_b_out", "L0_ffn_gamma",
          "L0_ffn_beta", "L0_ffn_Wr", "L0_ffn_br", "L0_ffn_W1", "L0_ffn_b1", "L0_ffn_W2", "L0_ffn_b2"]


def kernel(**inputs):
    import numpy as np
    import concourse.bacc as bacc
    from concourse.bass_utils import run_bass_kernel_spmd

    nc = bacc.Bacc("TRN2", target_bir_lowering=False, num_devices=1)
    arrays, a = {}, {}
    for name in INPUTS:
        array = np.ascontiguousarray(inputs[name])
        arrays[f"in_{name}"] = array
        a[name] = nc.dram_tensor(f"in_{name}", array.shape, mybir.dt.from_np(array.dtype), kind="ExternalInput").ap()
    a["out"] = nc.dram_tensor("out_0", (NODES, D), F32, kind="ExternalOutput").ap()
    build(nc, a)
    r = run_bass_kernel_spmd(nc, [arrays], core_ids=[0])
    return r.results[0]["out_0"]
```
